# Optimizing a Trainium2 kernel written in Bass

```python
import numpy as np
import jax
import jax.numpy as jnp

def _softmax(x, axis=-1):
    return jax.nn.softmax(x, axis=axis)

def _gelu(x):
    return jax.nn.gelu(x, approximate=True)

def _silu(x):
    return jax.nn.silu(x)

def _sigmoid(x):
    return jax.nn.sigmoid(x)

def _layernorm(x, axis=-1, eps=1e-05):
    m = jnp.mean(x, axis=axis, keepdims=True)
    v = jnp.var(x, axis=axis, keepdims=True)
    return (x - m) / jnp.sqrt(v + eps)

def _scatter_add(tgt, idx, src, axis=0):
    return tgt.at[idx].add(src)

def _segment_sum(src, seg, n):
    return jax.ops.segment_sum(src, seg, n)
kernel_name = 'mk_flamingo_gated_d1_seqx_r8_23385a'

def setup_inputs(seed: int=0):
    np.random.seed(seed)
    _w = jnp.asarray

    def _rec_inputs():
        import jax
        import jax.numpy as jnp
        _rk = jax.random.key(seed)
        x = -0.0002928 + 1 * jax.random.normal(jax.random.fold_in(_rk, 1), (8, 256, 128), jnp.float32)
        _lenS = 256 - jax.random.randint(jax.random.fold_in(_rk, 7), (8,), 0, max(1, 256 // 4) + 1, jnp.int32)
        _lenS2 = 512 - jax.random.randint(jax.random.fold_in(_rk, 8), (8,), 0, max(1, 512 // 4) + 1, jnp.int32)
        _ctx_1024P = jax.random.normal(jax.random.fold_in(_rk, 11), (8, 16, 128), jnp.float32)
        _ctx_1024c = jax.random.dirichlet(jax.random.fold_in(_rk, 511), 0.3 * jnp.ones((16,), jnp.float32), (8, 512))
        _ctx_1024t = jnp.einsum('bsk,bkd->bsd', _ctx_1024c, _ctx_1024P)
        _ctx_1024t = _ctx_1024t * jax.lax.rsqrt(jnp.mean(jnp.square(_ctx_1024t)) + 1e-12) * 0.953939
        ctx_1024 = -1.39393e-06 + 0.999914 * (_ctx_1024t + 0.3 * jax.random.normal(jax.random.fold_in(_rk, 611), (8, 512, 128), jnp.float32))
        _validS = jnp.arange(256)[None, :] < _lenS[:, None]
        _validS2 = jnp.arange(512)[None, :] < _lenS2[:, None]
        _causal = jnp.tril(jnp.ones((256, 256), dtype=bool))
        mask_Bx1xS2_ik0 = jnp.where(jnp.broadcast_to(_validS2[:, None, :], (8, 1, 512)), 0, 1).astype(jnp.int32)
        _g = jax.random.normal(jax.random.fold_in(_rk, 9001), (2, 1), jnp.float32)
        _g = jnp.sign(_g) * jnp.maximum(jnp.abs(_g), 1.0) + (_g == 0) * 1.0
        g_xattn = _g[0]
        g_ffn = _g[1]
        return (x, ctx_1024, mask_Bx1xS2_ik0, g_xattn, g_ffn)
    x, ctx_1024, mask_Bx1xS2_ik0, g_xattn, g_ffn = _rec_inputs()

    def _L0_xattn_setup():
        import jax, jax.numpy as jnp
        import numpy as np
        B, SQ, SK = (2, 256, 256)
        DQ = DK = DV = DM = DOUT = 128
        H = 16
        DHEAD = DM // H
        key = jax.random.key(seed)
        ks = jax.random.split(key, 12)
        s = 0.02
        return {'Q': jax.random.normal(ks[0], (B, SQ, DQ), jnp.float32), 'K': jax.random.normal(ks[1], (B, SK, DK), jnp.float32), 'V': jax.random.normal(ks[2], (B, SK, DV), jnp.float32), 'mask': jax.random.randint(ks[3], (B, 1, SK), 0, 2, jnp.int32), 'Wq': jax.random.normal(ks[4], (DQ, DM), jnp.float32) * s, 'bq': jnp.zeros((DM,), jnp.float32), 'Wk': jax.random.normal(ks[5], (DK, DM), jnp.float32) * s, 'bk': jnp.zeros((DM,), jnp.float32), 'Wv': jax.random.normal(ks[6], (DV, DM), jnp.float32) * s, 'bv': jnp.zeros((DM,), jnp.float32), 'Wo': jax.random.normal(ks[7], (DM, DOUT), jnp.float32) * s, 'bo': jnp.zeros((DOUT,), jnp.float32)}
    _L0_xattn_all = _L0_xattn_setup()
    _L0_xattn_in = {k: v for k, v in _L0_xattn_all.items() if k in ('Wq', 'bq', 'Wk', 'bk', 'Wv', 'bv', 'Wo', 'bo')}
    del _L0_xattn_all

    def _L0_ffn_setup():
        import jax, jax.numpy as jnp
        import numpy as np
        NUM_EXPERTS = 8
        TOP_K = 2
        B, T, D, F = (4, 256, 128, 352)
        key = jax.random.key(seed)
        ks = jax.random.split(key, 5)
        return {'x': jax.random.normal(ks[0], (B, T, D), dtype=jnp.float32), 'router_w': jax.random.normal(ks[1], (D, NUM_EXPERTS), dtype=jnp.float32) * 0.02, 'gate_proj': jax.random.normal(ks[2], (NUM_EXPERTS, D, F), dtype=jnp.float32) * 0.02, 'up_proj': jax.random.normal(ks[3], (NUM_EXPERTS, D, F), dtype=jnp.float32) * 0.02, 'down_proj': jax.random.normal(ks[4], (NUM_EXPERTS, F, D), dtype=jnp.float32) * 0.02}
    _L0_ffn_all = _L0_ffn_setup()
    _L0_ffn_in = {k: v for k, v in _L0_ffn_all.items() if k in ('router_w', 'gate_proj', 'up_proj', 'down_proj')}
    del _L0_ffn_all
    return {'x': x, 'ctx_1024': ctx_1024, 'mask_Bx1xS2_ik0': mask_Bx1xS2_ik0, 'g_xattn': g_xattn, 'g_ffn': g_ffn, 'L0_xattn_Wq': _L0_xattn_in['Wq'], 'L0_xattn_bq': _L0_xattn_in['bq'], 'L0_xattn_Wk': _L0_xattn_in['Wk'], 'L0_xattn_bk': _L0_xattn_in['bk'], 'L0_xattn_Wv': _L0_xattn_in['Wv'], 'L0_xattn_bv': _L0_xattn_in['bv'], 'L0_xattn_Wo': _L0_xattn_in['Wo'], 'L0_xattn_bo': _L0_xattn_in['bo'], 'L0_ffn_router_w': _L0_ffn_in['router_w'], 'L0_ffn_gate_proj': _L0_ffn_in['gate_proj'], 'L0_ffn_up_proj': _L0_ffn_in['up_proj'], 'L0_ffn_down_proj': _L0_ffn_in['down_proj']}

def reference(x, ctx_1024, mask_Bx1xS2_ik0, g_xattn, g_ffn, L0_xattn_Wq, L0_xattn_bq, L0_xattn_Wk, L0_xattn_bk, L0_xattn_Wv, L0_xattn_bv, L0_xattn_Wo, L0_xattn_bo, L0_ffn_router_w, L0_ffn_gate_proj, L0_ffn_up_proj, L0_ffn_down_proj):
    import jax
    import jax.numpy as jnp

    def _L0_xattn_ref(Q, K, V, mask, Wq, bq, Wk, bk, Wv, bv, Wo, bo):
        import jax, jax.numpy as jnp
        import numpy as np
        B, SQ, SK = (2, 256, 256)
        DQ = DK = DV = DM = DOUT = 128
        H = 16
        DHEAD = DM // H
        b, sq, _ = Q.shape
        q = (Q @ Wq + bq).reshape(b, sq, H, DHEAD).transpose(0, 2, 1, 3)
        k = (K @ Wk + bk).reshape(b, -1, H, DHEAD).transpose(0, 2, 1, 3)
        v = (V @ Wv + bv).reshape(b, -1, H, DHEAD).transpose(0, 2, 1, 3)
        scores = jnp.einsum('bhqd,bhkd->bhqk', q, k) / np.sqrt(DHEAD).astype(np.float32)
        m = mask[:, None]
        scores = jnp.where(m == 0, -jnp.inf, scores)
        attn = jax.nn.softmax(scores, axis=-1)
        out = jnp.einsum('bhqk,bhkd->bhqd', attn, v)
        out = out.transpose(0, 2, 1, 3).reshape(b, sq, DM)
        return out @ Wo + bo

    def _L0_ffn_ref(x, router_w, gate_proj, up_proj, down_proj):
        import jax, jax.numpy as jnp
        import numpy as np
        NUM_EXPERTS = 8
        TOP_K = 2
        B, T, D, F = (4, 256, 128, 352)
        scores = jnp.einsum('btd,de->bte', x, router_w).astype(jnp.float32)
        probs = jax.nn.softmax(scores, axis=-1)
        routing_weights, routing_idx = jax.lax.top_k(probs, TOP_K)
        routing_weights = (routing_weights / jnp.sum(routing_weights, axis=-1, keepdims=True)).astype(x.dtype)
        one_hot = jax.nn.one_hot(routing_idx, NUM_EXPERTS, dtype=x.dtype)
        expert_w = jnp.einsum('btke,btk->bte', one_hot, routing_weights)
        dispatched = jnp.einsum('btd,btke->bted', x, one_hot)
        gate = jnp.einsum('bted,edf->btef', dispatched, gate_proj)
        up = jnp.einsum('bted,edf->btef', dispatched, up_proj)
        acts = jax.nn.silu(gate) * up
        expert_out = jnp.einsum('btef,efd->bted', acts, down_proj)
        return jnp.einsum('bted,bte->btd', expert_out, expert_w)
    x = x + jnp.tanh(g_xattn[0]) * _L0_xattn_ref(_layernorm(x, axis=-1), ctx_1024, ctx_1024, mask_Bx1xS2_ik0, L0_xattn_Wq, L0_xattn_bq, L0_xattn_Wk, L0_xattn_bk, L0_xattn_Wv, L0_xattn_bv, L0_xattn_Wo, L0_xattn_bo)
    x = x + jnp.tanh(g_ffn[0]) * _L0_ffn_ref(_layernorm(x, axis=-1), L0_ffn_router_w, L0_ffn_gate_proj, L0_ffn_up_proj, L0_ffn_down_proj)
    return x

_drawn_inputs = setup_inputs


def setup_inputs(seed=0):
    import zlib

    import numpy as np

    out = dict(_drawn_inputs(seed))
    spreads = {'L0_xattn_bq': (0.0, 0.8),
     'L0_xattn_bk': (0.0, 0.8),
     'L0_xattn_bv': (0.0, 0.507),
     'L0_xattn_bo': (0.0, 0.1)}
    factors = {'ctx_1024': 2.815,
     'L0_xattn_Wq': 8.0,
     'L0_xattn_Wk': 8.0,
     'L0_xattn_Wv': 2.838,
     'L0_ffn_router_w': 8.0,
     'L0_ffn_gate_proj': 8.0,
     'L0_ffn_up_proj': 8.0,
     'L0_ffn_down_proj': 8.0}
    for name, (base, spread) in spreads.items():
        noise = np.random.default_rng([zlib.crc32(name.encode()), seed]).standard_normal(out[name].shape)
        drawn = base * np.exp(spread * noise) if base else spread * noise
        out[name] = jnp.asarray(drawn.astype(out[name].dtype))
    for name, factor in factors.items():
        out[name] = (out[name] * factor).astype(out[name].dtype)
    return out
```

```python
from contextlib import ExitStack

import concourse.bass as bass
from concourse import mybir

F32 = mybir.dt.float32
F32R = mybir.dt.float32r
BF16 = mybir.dt.bfloat16
I32 = mybir.dt.int32
U32 = mybir.dt.uint32
ALU = mybir.AluOpType
ACT = mybir.ActivationFunctionType
AX = mybir.AxisListType

P = 128
D = 128
B, SQ, SK = 8, 256, 512
H, DH = 16, 8
G = 4
BL = H // G
GR = P // G
QT = SQ // P
KT = SK // P
NTOK = B * SQ
TT = NTOK // P
MASK_ROW = 3 * DH
VSTEP = G * GR + DH
DSTEP = GR + DH
MASKED = -1.0e30
SCALE = float(DH) ** -0.5
EPS = 1e-5

NE, TOPK, F = 8, 2, 352
FC = -(-F // P)
FP = FC * P
REC = D + 1
CAP = NTOK + P
NTILES = TOPK * NTOK // P + NE
BLANK = NE * CAP
NOWHERE = 2 * TOPK * NTOK
BIG = 3.0e38


def wait(eng, sem, value):
    if isinstance(value, int) and value <= 0:
        return
    eng.wait_ge(sem, value)


def build(nc, x, ctxT, mask, wq, bq, wk, bk, wv, bv, wo, bo, g, wr, wgate, wup, wdown, out):
    ctx = ExitStack()
    with ctx:
        def sb(name, shape, dt=F32):
            return ctx.enter_context(nc.sbuf_tensor(name, shape, dt))

        def pb(name, shape):
            return ctx.enter_context(nc.psum_tensor(name, shape, F32))

        def sem(name):
            return ctx.enter_context(nc.semaphore(name))

        def sems(prefix, names):
            return {k: sem(prefix + k) for k in names.split()}

        lists = nc.dram_tensor("lists", (BLANK + P, REC), F32).ap()
        places = nc.dram_tensor("places", (TOPK * NTOK, D), F32).ap()

        x_sb = sb("x_sb", [P, TT, D])
        xn = sb("xn", [P, TT, D])
        xnT = sb("xnT", [P, NTOK])
        ident = sb("ident", [P, P])
        before = sb("before", [P, P], BF16)
        ones = sb("ones", [P, P], BF16)
        wq_sb = sb("wq_sb", [P, BL, P])
        wk_sb = sb("wk_sb", [P, BL, P])
        wv_sb = sb("wv_sb", [P, D])
        wo_sb = sb("wo_sb", [P, D])
        bq_sb = sb("bq_sb", [P, BL])
        bk_sb = sb("bk_sb", [P, BL])
        bv_sb = sb("bv_sb", [P, 1])
        bo_sb = sb("bo_sb", [P, D])
        wr_sb = sb("wr_sb", [P, NE])
        tg_in = sb("tg_in", [P, 2])
        tg = sb("tg", [P, 2])
        w_hi = sb("w_hi", [P, NE, 2 * F], F32R)
        w_lo = sb("w_lo", [P, NE, 2 * F], F32R)
        wd_sb = sb("wd_sb", [P, NE, FC, D])
        lows = sb("lows", [P, 2])
        split_q = sb("split_q", [P, 1])
        split_k = sb("split_k", [P, 1])
        sel = sb("sel", [P, H, P], F32R)
        selw = sb("selw", [P, H])
        halves = sb("halves", [P, TT])
        stats = sb("stats", [P, TT, 6])
        mv = sb("mv", [P, TT, 2])
        rstd = sb("rstd", [P, TT])
        varp = sb("varp", [P, TT])
        mask_in = sb("mask_in", [P, B, KT], I32)
        keep = sb("keep", [P, B, KT])
        early = sb("early", [P, 1])
        early_row = sb("early_row", [1, P])
        early_n = sb("early_n", [1, 1], I32)
        iota_e = sb("iota_e", [P, NE])
        base_e = sb("base_e", [P, NE])
        dest = sb("dest", [P, QT, TOPK])
        blank = sb("blank", [P, REC])

        attention_memory = ctx.enter_context(ExitStack())

        def att(name, shape, dt=F32):
            return attention_memory.enter_context(nc.sbuf_tensor(name, shape, dt))

        cnt = sb("cnt", [P, NE])
        gap = sb("gap", [P, TT])
        w_raw = att("w_raw", [P, 2, 2, F])
        arena_r = att("arena_r", [P, 15360], F32R)
        arena = att("arena", [P, 3400])
        mrows = att("mrows", [P, KT, P])
        q_t = att("q_t", [P, BL, SQ])
        q_hi = att("q_hi", [P, BL, SQ], F32R)
        k_t = att("k_t", [P, BL, P])
        k_hi = att("k_hi", [P, BL, P], F32R)
        mraw = att("mraw", [P, KT, QT, H])
        mall = att("mall", [P, QT, H])
        mhi = att("mhi", [P, QT, H], F32R)
        mm = att("mm", [P, QT, P])
        mT = att("mT", [P, SQ], F32R)
        pt = att("pt", [P, 2, G * SQ])
        rden = att("rden", [P, SQ])
        ot0 = att("ot0", [P, SQ])
        oT = att("oT", [P, SQ])
        stats2 = att("stats2", [P, QT, 6])
        mv2 = att("mv2", [P, QT, 2])
        var2 = att("var2", [P, QT])
        rstd2 = att("rstd2", [P, QT])
        hrec = att("hrec", [P, QT, TOPK, REC])
        hT = att("hT", [P, SQ])
        logit = att("logit", [P, QT, NE])
        top = att("top", [P, QT, NE])
        topi = att("topi", [P, QT, NE], U32)
        topf = att("topf", [P, QT, TOPK])
        hot = att("hot", [P, QT, TOPK, NE])
        selb = att("selb", [P, QT, NE], BF16)
        pos = att("pos", [P, QT, NE])
        prod = att("prod", [P, QT, TOPK, NE])
        rowf = att("rowf", [P, QT, TOPK])
        rowi = att("rowi", [P, QT, TOPK], U32)

        s_ps = pb("s_ps", [P, 4, 512])
        pv_ps = pb("pv_ps", [P, 512])
        k_ps = pb("k_ps", [P, 512])
        q_ps = pb("q_ps", [P, 512])
        m_ps = pb("m_ps", [P, 512])

        S = sems("a_", "x mask w g wd wr halves rows ident ident_d tri ones blank st mv var rs ln "
                 "xT_ps xT tg xb keep early early_ps early_n lows split selw sel hi lo base cnt dest wdz")
        gu_in = [sem(f"a_gu{u}") for u in range(2)]
        with nc.Block() as block:
            @block.sync
            def _(sp):
                sp.dma_start(mask_in[:, :, :], mask.rearrange("p (b t) -> p b t", b=B)).then_inc(S["mask"], 16)
                sp.dma_start(x_sb[:, :, :], x.rearrange("(t p) d -> p t d", p=P)).then_inc(S["x"], 16)
                sp.dma_start(wq_sb[:, :, :], wq).then_inc(S["w"], 16)
                sp.dma_start(wk_sb[:, :, :], wk).then_inc(S["w"], 16)
                sp.dma_start(wv_sb[:, :], wv).then_inc(S["w"], 16)
                sp.dma_start(wo_sb[:, :], wo).then_inc(S["w"], 16)
                sp.dma_start(bq_sb[:, :], bq).then_inc(S["w"], 16)
                sp.dma_start(bk_sb[:, :], bk).then_inc(S["w"], 16)
                sp.dma_start(bv_sb[:, :], bv).then_inc(S["w"], 16)
                sp.dma_start(wr_sb[:, :], wr).then_inc(S["w"], 16)
                sp.dma_start(bo_sb[:, :], bo.partition_broadcast(P)).then_inc(S["g"], 16)
                sp.dma_start(tg_in[:, :], g.partition_broadcast(P)).then_inc(S["g"], 16)
                for e in range(NE):
                    if e >= 2:
                        sp.wait_ge(S["lo"], e - 1)
                    sp.dma_start(w_raw[:, e % 2, 0, :], wgate[e, :, :]).then_inc(gu_in[e % 2], 16)
                    sp.dma_start(w_raw[:, e % 2, 1, :], wup[e, :, :]).then_inc(gu_in[e % 2], 16)
                sp.wait_ge(S["wdz"], 1)
                for c in range(FC):
                    n = min(P, F - c * P)
                    sp.dma_start(wd_sb[0:n, :, c, :],
                                 wdown[:, c * P:c * P + n, :].rearrange("e p d -> p e d")).then_inc(S["wd"], 16)
                sp.wait_ge(S["wd"], FC * 16)

            @block.gpsimd
            def _(pool):
                pool.memset(halves[:, :], -0.5).then_inc(S["halves"], 1)
                pool.memset(ident[:, :], 0.0).then_inc(S["ident"], 1)
                pool.memset(before[:, :], 1.0).then_inc(S["ones"], 1)
                pool.memset(ones[:, :], 1.0).then_inc(S["ones"], 1)
                pool.memset(blank[:, 0:D], 0.0).then_inc(S["blank"], 1)
                pool.memset(blank[:, D:REC], float(NOWHERE)).then_inc(S["blank"], 1)
                pool.wait_ge(S["ident"], 1)
                pool.affine_select(out=ident[:, :], in_=ident[:, :], compare_op=ALU.not_equal, fill=1.0, base=0,
                                   pattern=[[-1, P]], channel_multiplier=1).then_inc(S["ident_d"], 1)
                pool.wait_ge(S["ones"], 2)
                pool.affine_select(out=before[:, :], in_=before[:, :], compare_op=ALU.is_ge, fill=0.0, base=-1,
                                   pattern=[[1, P]], channel_multiplier=-1).then_inc(S["tri"], 1)
                pool.iota(iota_e[:, :], pattern=[[1, NE]], base=0, channel_multiplier=0,
                          allow_small_or_imprecise_dtypes=True).then_inc(S["base"], 1)
                pool.iota(base_e[:, :], pattern=[[CAP, NE]], base=0, channel_multiplier=0,
                          allow_small_or_imprecise_dtypes=True).then_inc(S["base"], 1)
                pool.iota(cnt[:, :], pattern=[[CAP, NE]], base=0, channel_multiplier=0,
                          allow_small_or_imprecise_dtypes=True).then_inc(S["base"], 1)
                pool.iota(dest[:, :, :], pattern=[[P, QT], [NTOK, TOPK]], base=0, channel_multiplier=1,
                          allow_small_or_imprecise_dtypes=True).then_inc(S["base"], 1)
                pool.wait_ge(S["halves"], 1)
                pool.wait_ge(S["var"], 1)
                pool.tensor_tensor(rstd[:, :], varp[:, :], halves[:, :], ALU.pow).then_inc(S["rs"], 1)
                pool.wait_ge(S["blank"], 2)
                pool.dma_start(lists[BLANK:BLANK + P, :], blank[:, :]).then_inc(S["wr"], 16)
                pool.wait_ge(S["wr"], 16)

            @block.scalar
            def _(act):
                act.wait_ge(S["g"], 32)
                act.activation(tg[:, :], tg_in[:, :], ACT.Tanh).then_inc(S["tg"], 1)
                for c in range(NTOK // 512):
                    act.wait_ge(S["xT_ps"], c + 1)
                    act.activation(xnT[:, c * 512:(c + 1) * 512], s_ps[:, c, :], ACT.Copy).then_inc(S["xT"], 1)
                for e in range(NE):
                    act.wait_ge(gu_in[e % 2], 32 * (e // 2 + 1))
                    act.activation(w_hi[:, e, :], w_raw[:, e % 2, :, :].rearrange("p a f -> p (a f)"),
                                   ACT.Copy).then_inc(S["hi"], 1)

            @block.vector
            def _(dve):
                dve.memset(wd_sb[F - (FC - 1) * P:P, :, FC - 1, :], 0.0).then_inc(S["wdz"], 1)
                dve.memset(mm[:, :, :], 0.0)
                dve.wait_ge(S["mask"], 16)
                dve.tensor_scalar(keep[:, :, :], mask_in[:, :, :], 0.0, None, ALU.not_equal).then_inc(S["keep"], 1)
                dve.wait_ge(S["keep"], 1)
                dve.tensor_reduce(early[:, :], keep[:, :, 0:KT - 1], AX.XY, ALU.max).then_inc(S["early"], 1)
                dve.wait_ge(S["x"], 16)
                for t in range(TT):
                    dve.bn_stats(stats[:, t, :], x_sb[:, t, :]).then_inc(S["st"], 1)
                for t in range(TT):
                    dve.wait_ge(S["st"], t + 1)
                    dve.bn_aggr(mv[:, t, :], stats[:, t, :]).then_inc(S["mv"], 1)
                dve.wait_ge(S["mv"], TT)
                dve.tensor_scalar(varp[:, :], mv[:, :, 1], EPS, None, ALU.add).then_inc(S["var"], 1)
                dve.wait_ge(S["ident_d"], 1)
                iv = ident[:, :].rearrange("p (g r) -> p g r", g=G)
                dve.tensor_reduce(lows[:, 0:1], iv[:, :, 2 * DH:3 * DH], AX.XY, ALU.add).then_inc(S["lows"], 1)
                dve.tensor_reduce(lows[:, 1:2], iv[:, :, DH:2 * DH], AX.XY, ALU.add).then_inc(S["lows"], 1)
                dve.tensor_tensor(selw[:, :], ident[:, 0:H], ident[:, H:2 * H], ALU.add).then_inc(S["selw"], 1)
                dve.wait_ge(S["lows"], 2)
                dve.tensor_scalar(split_q[:, :], lows[:, 0:1], -1.0, None, ALU.mult).then_inc(S["split"], 1)
                dve.tensor_scalar(split_k[:, :], lows[:, 1:2], -1.0, None, ALU.mult).then_inc(S["split"], 1)
                dve.wait_ge(S["selw"], 1)
                dve.tensor_copy(sel[:, :, :], selw[:, :].unsqueeze(2).broadcast_to([P, H, P])).then_inc(S["sel"], 1)
                dve.wait_ge(S["early_ps"], 1)
                dve.tensor_reduce(early_n[:, :], m_ps[0:1, 0:P], AX.X, ALU.max).then_inc(S["early_n"], 1)
                dve.wait_ge(S["rs"], 1)
                for t in range(TT):
                    dve.tensor_scalar(xn[:, t, :], x_sb[:, t, :], mv[:, t, 0:1], rstd[:, t:t + 1],
                                      ALU.subtract, ALU.mult).then_inc(S["ln"], 1)
                dve.wait_ge(S["ln"], TT)
                dve.wait_ge(S["tg"], 1)
                dve.scalar_tensor_tensor(out=x_sb[:, :, :], in0=bo_sb[:, :].unsqueeze(1).broadcast_to([P, TT, D]),
                                         scalar=tg[:, 0:1], in1=x_sb[:, :, :], op0=ALU.mult,
                                         op1=ALU.add).then_inc(S["xb"], 1)
                for e in range(NE):
                    dve.wait_ge(S["hi"], e + 1)
                    dve.tensor_tensor(w_lo[:, e, :], w_raw[:, e % 2, :, :].rearrange("p a f -> p (a f)"),
                                      w_hi[:, e, :], ALU.subtract).then_inc(S["lo"], 1)

            @block.tensor
            def _(pe):
                pe.wait_ge(S["ident_d"], 1)
                pe.wait_ge(S["early"], 1)
                pe.transpose(m_ps[0:1, 0:P], early[:, :], ident[:, :]).then_inc(S["early_ps"], 1)
                for t in range(TT):
                    pe.wait_ge(S["ln"], t + 1)
                    tr = pe.transpose(s_ps[:, t // 4, (t % 4) * P:(t % 4 + 1) * P], xn[:, t, :], ident[:, :])
                    if t % 4 == 3:
                        tr.then_inc(S["xT_ps"], 1)

        settled = sem("settled")

        def settle(eng):
            eng.sem_inc(settled, 1)

        T = sems("b_", "zero q_ps q_ev q_hi q_spl k_ps k_ev k_hi k_spl mrow v_ps v_ev dn s1 mx mall mhi mlo mm "
                 "mT_ps mT s2 ex pv rd ot oT y x2 r_st r_mv r_var r_rs r_h r_hd r_dest r_hT_ps r_hT r_lg_ps "
                 "r_lg r_top r_ti r_tf r_hot r_sel r_gap r_rk_ps r_pos r_prod r_row r_cnt r_rowi r_sent")
        ctx_s = [sem(f"b_ctx{u}") for u in range(2)]
        q_bd = [sem(f"b_qbd{u}") for u in range(2)]
        k_bd = [sem(f"b_kbd{u}") for u in range(2)]

        def attention(name, nt, depth):
            def part(tensor, at, shape):
                size = 1
                for s in shape:
                    size *= s
                v = tensor[:, at[0]:at[0] + size]
                at[0] += size
                letters = "abcde"[:len(shape)]
                if len(shape) > 1:
                    v = v.rearrange(f"p ({' '.join(letters)}) -> p {' '.join(letters)}",
                                    **{k: s for k, s in zip(letters[:-1], shape[:-1])})
                return v

            at = [0]
            qbd = part(arena_r, at, (depth, BL, G, SQ))
            qd = part(arena_r, at, (depth, BL, SQ))
            kd = part(arena_r, at, (depth, nt, BL, P))
            kbd = part(arena_r, at, (2, BL, G, P))
            assert at[0] <= arena_r.shape[1]
            used_r = at[0]
            at = [0]
            ctx_in = part(arena, at, (depth, nt * P))
            vn = part(arena, at, (depth, nt, BL * VSTEP))
            dn = part(arena, at, (depth, nt, BL * DSTEP))
            mrow = mrows[:, 0:depth * nt, :].rearrange("p (u n) k -> p u n k", u=depth)
            assert at[0] <= arena.shape[1], at
            used = at[0]

            U = BL * nt
            def drive(eng, front, back, route):
                if depth == 1:
                    front(0, 0, 0)
                    back(0, 0, 0, None)
                    route(0)
                    with eng.Fori(1, B) as n:
                        front(n, n, 0)
                        back(n, n, 0, None)
                        route(n)
                    return
                front(0, 0, 0)
                front(1, 0, 1)
                back(0, 0, 0, None)
                front(2, 1, 0)
                back(1, 0, 1, 0)
                with eng.Fori(1, B // 2 - 1) as i:
                    front(i * 2 + 1, i, 1)
                    back(i * 2, i, 0, i * 2 - 1)
                    front(i * 2 + 2, i + 1, 0)
                    back(i * 2 + 1, i, 1, i * 2)
                i = B // 2 - 1
                front(B - 1, i, 1)
                back(B - 2, i, 0, B - 3)
                back(B - 1, i, 1, B - 2)
                route(B - 1)

            def kbuf(u, kt):
                return u if nt == 1 else kt % 2

            def sync_(sp):
                def load(n, u):
                    wait(sp, T["v_ps"], nt * (n - depth + 1))
                    sp.dma_start(ctx_in[:, u, :],
                                 ctxT[bass.ds(n * P, P), (KT - nt) * P:KT * P]).then_inc(ctx_s[u], 16)

                def front(n, i, u):
                    if depth == 1:
                        load(n, u)
                    elif not (isinstance(n, int) and n == B - 1):
                        load(n + 1, 1 - u)
                    for kt in range(nt):
                        m = n * nt + kt
                        kb = kbuf(u, kt)
                        wait(sp, T["k_spl"], m + 1)
                        settle(sp)
                        wait(sp, T["s1"], BL * (m - 1))
                        for gr in range(G):
                            r = slice(gr * GR, (gr + 1) * GR)
                            sp.dma_start(kbd[r, kb, :, gr, :].bitcast(F32),
                                         kd[r, u, kt, :, :].bitcast(F32)).then_inc(k_bd[kb], 16)
                        if kt == 0:
                            wait(sp, T["q_spl"], n + 1)
                            settle(sp)
                            wait(sp, T["s2"], U * (n - depth + 1))
                            for gr in range(G):
                                r = slice(gr * GR, (gr + 1) * GR)
                                sp.dma_start(qbd[r, u, :, gr, :].bitcast(F32),
                                             qd[r, u, :, :].bitcast(F32)).then_inc(q_bd[u], 16)

                sp.wait_ge(T["zero"], 3)
                if depth == 2:
                    load(0, 0)
                drive(sp, front, lambda *a: None, lambda n: None)

            def gpsimd_(pool):
                def route(n):
                    pool.wait_ge(T["r_var"], n + 1)
                    pool.tensor_tensor(rstd2[:, :], var2[:, :], halves[:, 0:QT], ALU.pow).then_inc(T["r_rs"], 1)
                    pool.wait_ge(T["r_rowi"], n + 1)
                    pool.wait_ge(T["r_hd"], n + 1)
                    settle(pool)
                    for t in range(QT):
                        for k in range(TOPK):
                            pool.indirect_dma_start(
                                lists, bass.IndirectOffsetOnAxis(ap=rowi[:, t, k:k + 1], axis=0),
                                hrec[:, t, k, :], None, bounds_check=BLANK - 1,
                                oob_is_err=False).then_inc(T["r_sent"], 16)

                def back(n, i, u, rt):
                    if rt is not None:
                        route(rt)
                drive(pool, lambda *a: None, back, route)
                pool.wait_ge(T["r_sent"], B * QT * TOPK * 16)

            def scalar_(act):
                def front(n, i, u):
                    for r in range(2):
                        act.wait_ge(T["q_ps"], n * 2 + (r + 1))
                        if r == 0:
                            wait(act, T["q_spl"], n)
                        for j in (2 * r, 2 * r + 1):
                            act.activation(q_t[:, j, :], q_ps[:, (j % 2) * SQ:(j % 2 + 1) * SQ], ACT.Identity,
                                           bias=bq_sb[:, j:j + 1]).then_inc(T["q_ev"], 1)
                    for kt in range(nt):
                        m = n * nt + kt
                        act.wait_ge(T["k_ps"], m + 1)
                        wait(act, T["k_spl"], m)
                        for j in range(BL):
                            act.activation(k_t[:, j, :], k_ps[:, j * P:(j + 1) * P], ACT.Identity,
                                           bias=bk_sb[:, j:j + 1]).then_inc(T["k_ev"], 1)

                def hT_out(n):
                    act.wait_ge(T["r_hT_ps"], n + 1)
                    wait(act, T["r_lg_ps"], n)
                    act.activation(hT[:, :], m_ps[:, 0:SQ], ACT.Copy).then_inc(T["r_hT"], 1)

                def back(n, i, u, rt):
                    act.wait_ge(T["mT_ps"], n + 1)
                    wait(act, T["s2"], U * n)
                    act.activation(mT[:, :], m_ps[:, 0:SQ], ACT.Copy).then_inc(T["mT"], 1)
                    for m in range(U):
                        act.wait_ge(T["s2"], n * U + (m + 1))
                        wait(act, T["pv"], n * U + (m - 1))
                        act.activation(pt[:, m % 2, :],
                                       s_ps[:, 2 * (m % 2):2 * (m % 2) + 2, :].rearrange("p a b -> p (a b)"),
                                       ACT.Exp, scale=SCALE).then_inc(T["ex"], 1)
                        if m == 0 and rt is not None:
                            hT_out(rt)

                drive(act, front, back, hT_out)

            def vector_(dve):
                def front(n, i, u):
                    kp = keep[:, bass.ds(n, 1), KT - nt:KT].rearrange("p a t -> p (a t)")
                    wait(dve, T["k_ps"], nt * (n - depth + 1))
                    dve.tensor_scalar(mrow[:, u, :, :].rearrange("p n (g r) -> p n g r", g=G)[:, :, :, MASK_ROW],
                                      kp.unsqueeze(2).broadcast_to([P, nt, G]), 1.0, -MASKED, ALU.subtract,
                                      ALU.mult).then_inc(T["mrow"], 1)
                    wait(dve, T["pv"], U * (n - depth + 1))
                    settle(dve)
                    dve.tensor_copy(dn[:, u, :, :].rearrange("p n (j c) -> p n j c", j=BL)[:, :, :, 0:DH],
                                    kp.unsqueeze(2).unsqueeze(3).broadcast_to([P, nt, BL, DH])
                                    ).then_inc(T["dn"], 1)
                    dve.wait_ge(T["q_ev"], (n + 1) * BL)
                    wait(dve, T["q_spl"], n)
                    dve.tensor_copy(q_hi[:, :, :], q_t[:, :, :]).then_inc(T["q_hi"], 1)
                    dve.wait_ge(T["q_hi"], n + 1)
                    wait(dve, T["s1"], U * (n - depth + 1))
                    if not (isinstance(n, int) and n < depth):
                        dve.wait_ge(q_bd[u], i * 64)
                    dve.scalar_tensor_tensor(out=qd[:, u, :, :], in0=q_hi[:, :, :], scalar=split_q[:, :],
                                             in1=q_t[:, :, :], op0=ALU.mult, op1=ALU.add).then_inc(T["q_spl"], 1)
                    wait(dve, T["s2"], U * (n - depth + 1))
                    for kt in range(nt):
                        m = n * nt + kt
                        kb = kbuf(u, kt)
                        dve.wait_ge(T["k_ev"], (m + 1) * BL)
                        wait(dve, T["k_spl"], m)
                        dve.tensor_copy(k_hi[:, :, :], k_t[:, :, :]).then_inc(T["k_hi"], 1)
                        dve.wait_ge(T["k_hi"], m + 1)
                        if nt == 1:
                            if not (isinstance(n, int) and n < depth):
                                dve.wait_ge(k_bd[u], i * 64)
                        elif not (isinstance(n, int) and n < 1) and kt < 2:
                            dve.wait_ge(k_bd[kb], n * (nt // 2) * 64)
                        dve.scalar_tensor_tensor(out=kd[:, u, kt, :, :], in0=k_hi[:, :, :], scalar=split_k[:, :],
                                                 in1=k_t[:, :, :], op0=ALU.mult,
                                                 op1=ALU.add).then_inc(T["k_spl"], 1)
                        dve.wait_ge(T["v_ps"], m + 1)
                        vv = vn[:, u, kt, :].rearrange("p (j c) -> p j c", j=BL)[:, :, 0:G * GR]
                        vv = vv.rearrange("p j (g c) -> p j g c", g=G)[:, :, :, 0:DH]
                        dve.tensor_scalar(vv, q_ps[:, 0:P].rearrange("p (j g d) -> p j g d", j=BL, g=G),
                                          kp[:, kt:kt + 1], None, ALU.mult).then_inc(T["v_ev"], 1)
                        if kt == 0:
                            wait(dve, T["mall"], n)
                        for j in range(BL):
                            v = kt * BL + j
                            dve.wait_ge(T["s1"], n * U + (v + 1))
                            b0 = 2 * (v % 2)
                            dve.tensor_reduce(mraw[:, kt, :, j * G:(j + 1) * G],
                                              s_ps[:, b0:b0 + 2, :].rearrange("p a (g k) -> p a g k", g=G),
                                              AX.X, ALU.max).then_inc(T["mx"], 1)
                    dve.wait_ge(T["mx"], (n + 1) * U)
                    wait(dve, T["mlo"], n)
                    dve.tensor_reduce(mall[:, :, :], mraw[:, 0:nt, :, :].rearrange("p n a h -> p a h n"), AX.X,
                                      ALU.max).then_inc(T["mall"], 1)
                    dve.wait_ge(T["mall"], n + 1)
                    wait(dve, T["mm"], n)
                    dve.tensor_scalar(mhi[:, :, :], mall[:, :, :], -1.0, None, ALU.mult).then_inc(T["mhi"], 1)
                    dve.wait_ge(T["mhi"], n + 1)
                    wait(dve, T["mT_ps"], n)
                    dve.scalar_tensor_tensor(out=mm[:, :, H:2 * H], in0=mall[:, :, :], scalar=-1.0,
                                             in1=mhi[:, :, :], op0=ALU.mult,
                                             op1=ALU.subtract).then_inc(T["mlo"], 1)
                    dve.tensor_copy(mm[:, :, 0:H], mhi[:, :, :]).then_inc(T["mm"], 1)

                def route(n):
                    dve.wait_ge(T["x2"], (n + 1) * QT)
                    for t in range(QT):
                        wait(dve, T["r_mv"], n * QT)
                        settle(dve)
                        dve.bn_stats(stats2[:, t, :],
                                     xn[:, bass.ds(n * QT + t, 1), :].rearrange("p a d -> p (a d)")
                                     ).then_inc(T["r_st"], 1)
                    for t in range(QT):
                        dve.wait_ge(T["r_st"], n * QT + (t + 1))
                        wait(dve, T["r_h"], n * QT)
                        settle(dve)
                        dve.bn_aggr(mv2[:, t, :], stats2[:, t, :]).then_inc(T["r_mv"], 1)
                    dve.wait_ge(T["r_mv"], (n + 1) * QT)
                    wait(dve, T["r_rs"], n)
                    dve.tensor_scalar(var2[:, :], mv2[:, :, 1], EPS, None, ALU.add).then_inc(T["r_var"], 1)
                    dve.wait_ge(T["r_rs"], n + 1)
                    wait(dve, T["r_sent"], n * QT * TOPK * 16)
                    for t in range(QT):
                        dve.tensor_scalar(hrec[:, t, :, 0:D],
                                          xn[:, bass.ds(n * QT + t, 1), :].broadcast_to([P, TOPK, D]),
                                          mv2[:, t, 0:1], rstd2[:, t:t + 1], ALU.subtract,
                                          ALU.mult).then_inc(T["r_h"], 1)
                    wait(dve, T["r_dest"], n)
                    dve.tensor_copy(hrec[:, :, :, D:REC], dest[:, :, :].unsqueeze(3)).then_inc(T["r_hd"], 1)
                    dve.wait_ge(T["r_hd"], n + 1)
                    dve.tensor_scalar(dest[:, :, :], dest[:, :, :], float(SQ), None,
                                      ALU.add).then_inc(T["r_dest"], 1)
                    dve.wait_ge(T["r_lg_ps"], n + 1)
                    wait(dve, T["r_ti"], n * QT)
                    dve.tensor_scalar(logit[:, :, :], m_ps[:, SQ:SQ + QT * NE].rearrange("p (t e) -> p t e", t=QT),
                                      -BIG, BIG, ALU.max, ALU.min).then_inc(T["r_lg"], 1)
                    dve.wait_ge(T["r_lg"], n + 1)
                    wait(dve, T["r_gap"], n)
                    settle(dve)
                    for t in range(QT):
                        dve.max(top[:, t, :], logit[:, t, :]).then_inc(T["r_top"], 1)
                    for t in range(QT):
                        if t == 0:
                            wait(dve, T["r_tf"], n)
                        dve.wait_ge(T["r_top"], n * QT + (t + 1))
                        settle(dve)
                        dve.max_index(topi[:, t, :], top[:, t, :], logit[:, t, :]).then_inc(T["r_ti"], 1)
                    dve.tensor_tensor(gap[:, bass.ds(n * QT, QT)], top[:, :, 1], top[:, :, 0],
                                      ALU.subtract).then_inc(T["r_gap"], 1)
                    dve.wait_ge(T["r_ti"], (n + 1) * QT)
                    wait(dve, T["r_hot"], n)
                    dve.tensor_copy(topf[:, :, :], topi[:, :, 0:TOPK]).then_inc(T["r_tf"], 1)
                    dve.wait_ge(T["r_tf"], n + 1)
                    wait(dve, T["r_prod"], n)
                    wait(dve, T["r_sel"], n)
                    dve.tensor_tensor(hot[:, :, :, :],
                                      iota_e[:, :].unsqueeze(1).unsqueeze(1).broadcast_to([P, QT, TOPK, NE]),
                                      topf[:, :, :].unsqueeze(3).broadcast_to([P, QT, TOPK, NE]),
                                      ALU.is_equal).then_inc(T["r_hot"], 1)
                    dve.wait_ge(T["r_hot"], n + 1)
                    wait(dve, T["r_rk_ps"], n)
                    dve.tensor_tensor(selb[:, :, :], hot[:, :, 0, :], hot[:, :, 1, :],
                                      ALU.add).then_inc(T["r_sel"], 1)
                    dve.wait_ge(T["r_rk_ps"], n + 1)
                    wait(dve, T["r_cnt"], n)
                    r0 = SQ + QT * NE
                    dve.tensor_tensor(pos[:, :, :], m_ps[:, r0:r0 + QT * NE].rearrange("p (t e) -> p t e", t=QT),
                                      cnt[:, :].unsqueeze(1).broadcast_to([P, QT, NE]),
                                      ALU.add).then_inc(T["r_pos"], 1)
                    dve.wait_ge(T["r_pos"], n + 1)
                    dve.tensor_tensor(cnt[:, :], cnt[:, :], m_ps[:, r0 + QT * NE:r0 + (QT + 1) * NE],
                                      ALU.add).then_inc(T["r_cnt"], 1)
                    wait(dve, T["r_row"], n)
                    dve.tensor_tensor(prod[:, :, :, :], hot[:, :, :, :],
                                      pos[:, :, :].unsqueeze(2).broadcast_to([P, QT, TOPK, NE]),
                                      ALU.mult).then_inc(T["r_prod"], 1)
                    dve.wait_ge(T["r_prod"], n + 1)
                    wait(dve, T["r_rowi"], n)
                    dve.tensor_reduce(rowf[:, :, :], prod[:, :, :, :], AX.X, ALU.add).then_inc(T["r_row"], 1)
                    dve.wait_ge(T["r_row"], n + 1)
                    dve.tensor_copy(rowi[:, :, :], rowf[:, :, :]).then_inc(T["r_rowi"], 1)

                def back(n, i, u, rt):
                    if rt is not None:
                        route(rt)
                    dve.wait_ge(T["pv"], (n + 1) * U)
                    wait(dve, T["oT"], n)
                    dve.reciprocal(rden[:, :], pv_ps[:, SQ:2 * SQ]).then_inc(T["rd"], 1)
                    dve.tensor_scalar(ot0[:, :], pv_ps[:, SQ:2 * SQ], bv_sb[:, :], None,
                                      ALU.mult).then_inc(T["ot"], 1)
                    dve.wait_ge(T["ot"], n * 2 + 1)
                    dve.tensor_tensor(ot0[:, :], ot0[:, :], pv_ps[:, 0:SQ], ALU.add).then_inc(T["ot"], 1)
                    dve.wait_ge(T["ot"], n * 2 + 2)
                    dve.wait_ge(T["rd"], n + 1)
                    wait(dve, T["y"], n)
                    dve.tensor_tensor(oT[:, :], ot0[:, :], rden[:, :], ALU.mult).then_inc(T["oT"], 1)
                    dve.wait_ge(T["y"], n + 1)
                    for t in range(QT):
                        k = n * QT + t
                        dve.scalar_tensor_tensor(out=xn[:, bass.ds(k, 1), :],
                                                 in0=pv_ps[:, t * P:(t + 1) * P].unsqueeze(1),
                                                 scalar=tg[:, 0:1], in1=x_sb[:, bass.ds(k, 1), :], op0=ALU.mult,
                                                 op1=ALU.add).then_inc(T["x2"], 1)

                dve.memset(arena_r[:, 0:used_r].bitcast(F32), 0.0).then_inc(T["zero"], 1)
                dve.memset(arena[:, 0:used], 0.0).then_inc(T["zero"], 1)
                dve.memset(mrow[:, :, :, :], 0.0).then_inc(T["zero"], 1)
                dve.wait_ge(T["zero"], 3)
                drive(dve, front, back, route)

            def tensor_(pe):
                def front(n, i, u):
                    wait(pe, T["v_ev"], n * nt)
                    for r in range(2):
                        wait(pe, T["q_ev"], n * BL + 2 * r)
                        for j in (2 * r, 2 * r + 1):
                            mmi = pe.matmul(q_ps[:, (j % 2) * SQ:(j % 2 + 1) * SQ], wq_sb[:, j, :],
                                            xnT[:, bass.ds(n * SQ, SQ)], start=True, stop=True)
                        mmi.then_inc(T["q_ps"], 1)
                    pe.wait_ge(ctx_s[u], (i + 1) * 16)
                    pe.wait_ge(T["mrow"], n + 1)
                    for kt in range(nt):
                        m = n * nt + kt
                        kb = kbuf(u, kt)
                        c = ctx_in[:, u, kt * P:(kt + 1) * P]
                        wait(pe, T["k_ev"], m * BL)
                        for j in range(BL):
                            o = k_ps[:, j * P:(j + 1) * P]
                            pe.matmul(o, wk_sb[:, j, :], c, start=True, stop=False)
                            mmi = pe.matmul(o, mrow[:, u, kt, :], ident[:, :], start=False, stop=True)
                        mmi.then_inc(T["k_ps"], 1)
                        if kt == 0:
                            pe.wait_ge(T["q_ev"], (n + 1) * BL)
                        wait(pe, T["v_ev"], m)
                        pe.matmul(q_ps[:, 0:P], c, wv_sb[:, :], start=True, stop=True).then_inc(T["v_ps"], 1)
                        if kt == 0:
                            pe.wait_ge(T["q_spl"], n + 1)
                        if nt == 1:
                            pe.wait_ge(k_bd[kb], (i + 1) * 64)
                        else:
                            pe.wait_ge(k_bd[kb], (n * (nt // 2) + (kt // 2 + 1)) * 64)
                        for j in range(BL):
                            v = kt * BL + j
                            if v < 2:
                                wait(pe, T["ex"], U * (n - depth + 1) - 1 + v)
                            else:
                                pe.wait_ge(T["mx"], n * U + (v - 1))
                            for t in range(QT):
                                mmi = pe.matmul(s_ps[:, 2 * (v % 2) + t, :], qd[:, u, j, t * P:(t + 1) * P],
                                                kbd[:, kb, j, :, :].rearrange("p g k -> p (g k)"), start=True,
                                                stop=True)
                            mmi.then_inc(T["s1"], 1)

                def route1(n):
                    pe.wait_ge(T["r_h"], (n + 1) * QT)
                    for t in range(QT):
                        mmi = pe.transpose(m_ps[:, t * P:(t + 1) * P], hrec[:, t, 0, 0:D], ident[:, :])
                    mmi.then_inc(T["r_hT_ps"], 1)

                def route2(n):
                    pe.wait_ge(T["r_hT"], n + 1)
                    for t in range(QT):
                        mmi = pe.matmul(m_ps[:, SQ + t * NE:SQ + (t + 1) * NE], hT[:, t * P:(t + 1) * P],
                                        wr_sb[:, :], start=True, stop=True)
                    mmi.then_inc(T["r_lg_ps"], 1)

                def route3(n):
                    pe.wait_ge(T["r_sel"], n + 1)
                    pe.wait_ge(T["r_lg"], n + 1)
                    r0 = SQ + QT * NE
                    pe.matmul(m_ps[:, r0:r0 + QT * NE], before[:, :], selb[:, :, :].rearrange("p t e -> p (t e)"),
                              start=True, stop=False, skip_group_check=True)
                    for t in range(1, QT):
                        for s in range(t):
                            pe.matmul(m_ps[:, r0 + t * NE:r0 + (t + 1) * NE], ones[:, :], selb[:, s, :],
                                      start=False, stop=False, skip_group_check=True)
                    for t in range(QT):
                        mmi = pe.matmul(m_ps[:, r0 + QT * NE:r0 + (QT + 1) * NE], ones[:, :], selb[:, t, :],
                                        start=False, stop=(t == QT - 1), skip_group_check=True)
                    mmi.then_inc(T["r_rk_ps"], 1)

                def route(n):
                    route1(n)
                    route2(n)
                    route3(n)

                def back(n, i, u, rt):
                    pe.wait_ge(T["mm"], n + 1)
                    pe.wait_ge(T["mlo"], n + 1)
                    wait(pe, T["r_cnt"], n - 1 if depth == 2 else n)
                    for t in range(QT):
                        mmi = pe.transpose(m_ps[:, t * P:(t + 1) * P], mm[:, t, :], ident[:, :])
                    mmi.then_inc(T["mT_ps"], 1)
                    pe.wait_ge(q_bd[u], (i + 1) * 64)
                    pe.wait_ge(T["mT"], n + 1)
                    pe.wait_ge(T["dn"], n + 1)
                    pe.wait_ge(T["v_ev"], (n + 1) * nt)

                    def values(m):
                        kt, j = m // BL, m % BL
                        pe.wait_ge(T["ex"], n * U + (m + 1))
                        if m == 0:
                            wait(pe, T["x2"], n * QT)
                        for gr in range(G):
                            o = slice(gr * GR, (gr + 1) * GR)
                            r = pt[:, m % 2, gr * SQ:(gr + 1) * SQ]
                            c = (j * G + gr) * GR
                            pe.matmul(pv_ps[o, 0:SQ], vn[:, u, kt, c:c + GR], r, start=(m == 0),
                                      stop=(m == U - 1), skip_group_check=True)
                            mmi = pe.matmul(pv_ps[o, SQ:2 * SQ], dn[:, u, kt, j * GR:(j + 1) * GR], r,
                                            start=False, stop=(m == U - 1), skip_group_check=True)
                        mmi.then_inc(T["pv"], 1)

                    for m in range(U):
                        kt, j = m // BL, m % BL
                        if m < 2:
                            last = (n + 2) * U if depth == 2 and not (isinstance(n, int) and n == B - 1) \
                                else (n + 1) * U
                            pe.wait_ge(T["mx"], last + (m - 1))
                            if m == 0 and isinstance(n, int) and n == B - 1 and depth == 2:
                                pe.wait_ge(T["ex"], n * U)
                        else:
                            pe.wait_ge(T["ex"], n * U + (m - 1))
                        for a in range(2):
                            o = s_ps[:, 2 * (m % 2) + a, :]
                            pe.matmul(o, kd[:, u, kt, j, :],
                                      qbd[:, u, j, 2 * a:2 * a + 2, :].rearrange("p g q -> p (g q)"),
                                      start=True, stop=False, skip_group_check=True)
                            for gr in (2 * a, 2 * a + 1):
                                mmi = pe.matmul(o[:, (gr % 2) * SQ:(gr % 2 + 1) * SQ], sel[:, j * G + gr, :],
                                                mT[:, :], start=False, stop=(gr % 2 == 1),
                                                skip_group_check=True)
                        mmi.then_inc(T["s2"], 1)
                        if m:
                            values(m - 1)
                        if rt is not None and m == 0:
                            route1(rt)
                        if rt is not None and m == 2:
                            route2(rt)
                    values(U - 1)
                    if rt is not None:
                        route3(rt)
                    pe.wait_ge(T["oT"], n + 1)
                    for t in range(QT):
                        mmi = pe.matmul(pv_ps[:, t * P:(t + 1) * P], oT[:, t * P:(t + 1) * P], wo_sb[:, :],
                                        start=True, stop=True)
                    mmi.then_inc(T["y"], 1)

                pe.wait_ge(T["zero"], 3)
                drive(pe, front, back, route)

            return sync_, gpsimd_, scalar_, vector_, tensor_

        general = attention("g_", KT, 1)
        short = attention("s_", 1, 2)

        def choose(eng, k):
            n = eng.value_load(early_n[0:1, 0:1], min_val=0, max_val=1)
            with eng.If(n == 0):
                short[k](eng)
            with eng.Else():
                general[k](eng)

        with nc.Block() as block:
            @block.sync
            def _(sp):
                choose(sp, 0)

            @block.gpsimd
            def _(pool):
                choose(pool, 1)

            @block.scalar
            def _(act):
                choose(act, 2)

            @block.vector
            def _(dve):
                choose(dve, 3)

            @block.tensor
            def _(pe):
                choose(pe, 4)

        attention_memory.close()
        NT = NTILES
        NB = 8
        tile_i = sb("tile_i", [P, NT])
        part_i = sb("part_i", [P, 1])
        lane_e = sb("lane_e", [P, NE])
        lane_i = sb("lane_i", [P, NE], U32)
        used = sb("used", [P, NE])
        usedi = sb("usedi", [P, NE], I32)
        tilesi = sb("tilesi", [P, NE], I32)
        tiles = sb("tiles", [P, NE])
        ends = sb("ends", [P, NE])
        past = sb("past", [P, NT, NE])
        skip = sb("skip", [P, NT, NE])
        te = sb("te", [P, NT])
        ts_ = sb("ts_", [P, NT])
        tb = sb("tb", [P, NT])
        ti = sb("ti", [P, NT], I32)
        tw = sb("tw", [P, NT], I32)
        t0 = sb("t0", [P, NT])
        td = sb("td", [P, NT], I32)
        rec = sb("rec", [P, NB, REC])
        x_hi = sb("x_hi", [P, 2, P], F32R)
        x_lo = sb("x_lo", [P, 2, P], F32R)
        silu = sb("silu", [P, 2, F])
        acts = sb("acts", [P, 2, FP])
        actsT = sb("actsT", [P, 2, FP])
        yrow = sb("yrow", [P, NB, D])
        desti = sb("desti", [P, NB], U32)

        E = sems("e_", "iota lane lanei fill used usedi tilesi tiles ends past skip te ts tb t0 tab "
                 "az xT_ps x_hi x_lo gu silu acts aT_ps aT y_ps y di")
        rec_s = [sem(f"e_rec{u}") for u in range(NB)]
        sent = [sem(f"e_sent{u}") for u in range(NB)]

        def steps(eng, step, last):
            for s in range(NB):
                step(s, 0, s)
            with eng.Fori(1, NT // NB) as i:
                for u in range(NB):
                    step(i * NB + u, i, u)
            for s in range(NT, NT + last):
                step(s, s // NB, s % NB)

        def tile_at(s, i, u, lag):
            if isinstance(s, int) and not 0 <= s - lag < NT:
                return None
            return s - lag, (i if u >= lag else i - 1), (u - lag) % NB

        xT_ps = q_ps
        aT_ps = m_ps
        y_ps = k_ps
        with nc.Block() as block:
            @block.sync
            def _(sp):
                sp.wait_ge(E["tab"], 2)
                sp.wait_ge(E["fill"], NE * 16)

                def step(s, i, u):
                    row = sp.value_load(ti[0:1, bass.ds(s, 1)], min_val=0, max_val=BLANK)
                    wait(sp, E["y"], s - NB + 1)
                    wait(sp, E["di"], s - NB + 1)
                    sp.dma_start(rec[:, u, :], lists[bass.ds(row, P), :]).then_inc(rec_s[u], 16)
                steps(sp, step, 0)

            @block.gpsimd
            def _(pool):
                pool.iota(tile_i[:, :], pattern=[[1, NT]], base=0, channel_multiplier=0,
                          allow_small_or_imprecise_dtypes=True).then_inc(E["iota"], 1)
                pool.iota(part_i[:, :], pattern=[[0, 1]], base=0, channel_multiplier=1,
                          allow_small_or_imprecise_dtypes=True).then_inc(E["iota"], 1)
                pool.wait_ge(E["lanei"], 1)
                for e in range(NE):
                    pool.indirect_dma_start(lists, bass.IndirectOffsetOnAxis(ap=lane_i[:, e:e + 1], axis=0),
                                            blank[:, :], None, bounds_check=BLANK - 1,
                                            oob_is_err=False).then_inc(E["fill"], 16)

                def step(s, i, u):
                    pool.wait_ge(E["y"], s + 1)
                    pool.wait_ge(E["di"], s + 1)
                    settle(pool)
                    pool.indirect_dma_start(places, bass.IndirectOffsetOnAxis(ap=desti[:, u:u + 1], axis=0),
                                            yrow[:, u, :], None, bounds_check=TOPK * NTOK - 1,
                                            oob_is_err=False).then_inc(sent[u], 16)
                steps(pool, step, 0)
                for u in range(NB):
                    pool.wait_ge(sent[u], NT // NB * 16)

            @block.scalar
            def _(act):
                def step(s, i, u):
                    if at := tile_at(s, i, u, 0):
                        n = at[0]
                        act.wait_ge(E["xT_ps"], n + 1)
                        wait(act, E["gu"], n - 1)
                        act.activation(x_hi[:, u % 2, :], xT_ps[:, 0:P], ACT.Copy).then_inc(E["x_hi"], 1)
                    if at := tile_at(s, i, u, 1):
                        n, _, v = at
                        act.wait_ge(E["gu"], n + 1)
                        wait(act, E["acts"], n - 1)
                        act.activation(silu[:, v % 2, :], s_ps[:, 2 * (v % 2), 0:F],
                                       ACT.Silu).then_inc(E["silu"], 1)
                    if at := tile_at(s, i, u, 2):
                        n, _, v = at
                        act.wait_ge(E["aT_ps"], n + 1)
                        wait(act, E["y_ps"], n - 1)
                        act.activation(actsT[:, v % 2, :], aT_ps[:, 0:FP], ACT.Copy).then_inc(E["aT"], 1)
                steps(act, step, 2)

            @block.vector
            def _(dve):
                dve.memset(acts[:, :, F:FP], 0.0).then_inc(E["az"], 1)
                dve.wait_ge(E["iota"], 2)
                dve.tensor_scalar(lane_e[:, :], cnt[:, :], part_i[:, :], None, ALU.add).then_inc(E["lane"], 1)
                dve.wait_ge(E["lane"], 1)
                dve.tensor_copy(lane_i[:, :], lane_e[:, :]).then_inc(E["lanei"], 1)
                dve.scalar_tensor_tensor(out=used[:, :], in0=cnt[:, :], scalar=float(P - 1), in1=base_e[:, :],
                                         op0=ALU.add, op1=ALU.subtract).then_inc(E["used"], 1)
                dve.wait_ge(E["used"], 1)
                dve.tensor_copy(usedi[:, :], used[:, :]).then_inc(E["usedi"], 1)
                dve.wait_ge(E["usedi"], 1)
                dve.tensor_single_scalar(tilesi[:, :], usedi[:, :], 7, ALU.arith_shift_right).then_inc(E["tilesi"], 1)
                dve.wait_ge(E["tilesi"], 1)
                dve.tensor_copy(tiles[:, :], tilesi[:, :]).then_inc(E["tiles"], 1)
                dve.wait_ge(E["tiles"], 1)
                dve.tensor_tensor_scan(ends[:, :], tiles[:, :], tiles[:, :], 0.0, ALU.add,
                                       ALU.bypass).then_inc(E["ends"], 1)
                dve.wait_ge(E["ends"], 1)
                dve.tensor_tensor(past[:, :, :], tile_i[:, :].unsqueeze(2).broadcast_to([P, NT, NE]),
                                  ends[:, :].unsqueeze(1).broadcast_to([P, NT, NE]), ALU.is_ge).then_inc(E["past"], 1)
                dve.wait_ge(E["past"], 1)
                dve.tensor_tensor(skip[:, :, :], past[:, :, :],
                                  tiles[:, :].unsqueeze(1).broadcast_to([P, NT, NE]), ALU.mult).then_inc(E["skip"], 1)
                dve.tensor_reduce(te[:, :], past[:, :, :], AX.X, ALU.add).then_inc(E["te"], 1)
                dve.wait_ge(E["skip"], 1)
                dve.tensor_reduce(ts_[:, :], skip[:, :, :], AX.X, ALU.add).then_inc(E["ts"], 1)
                dve.wait_ge(E["ts"], 1)
                dve.wait_ge(E["te"], 1)
                dve.tensor_tensor(tb[:, :], tile_i[:, :], ts_[:, :], ALU.subtract).then_inc(E["tb"], 1)
                dve.tensor_scalar(t0[:, :], te[:, :], float(CAP), None, ALU.mult).then_inc(E["t0"], 1)
                dve.wait_ge(E["tb"], 1)
                dve.wait_ge(E["t0"], 1)
                dve.scalar_tensor_tensor(out=tb[:, :], in0=tb[:, :], scalar=float(P), in1=t0[:, :], op0=ALU.mult,
                                         op1=ALU.add).then_inc(E["tb"], 1)
                dve.wait_ge(E["tb"], 2)
                dve.tensor_scalar(ti[:, :], tb[:, :], float(BLANK), None, ALU.min).then_inc(E["tab"], 1)
                dve.tensor_scalar(tw[:, :], te[:, :], float(NE - 1), None, ALU.min).then_inc(E["tab"], 1)
                dve.wait_ge(E["az"], 1)

                def step(s, i, u):
                    if at := tile_at(s, i, u, 0):
                        n = at[0]
                        wait(dve, sent[u], i * 16)
                        dve.wait_ge(E["x_hi"], n + 1)
                        wait(dve, E["gu"], n - 1)
                        dve.tensor_tensor(x_lo[:, u % 2, :], xT_ps[:, 0:P], x_hi[:, u % 2, :],
                                          ALU.subtract).then_inc(E["x_lo"], 1)
                    if at := tile_at(s, i, u, 1):
                        n, _, v = at
                        dve.wait_ge(E["silu"], n + 1)
                        wait(dve, E["aT_ps"], n - 1)
                        dve.tensor_tensor(acts[:, v % 2, 0:F], silu[:, v % 2, :], s_ps[:, 2 * (v % 2) + 1, 0:F],
                                          ALU.mult).then_inc(E["acts"], 1)
                    if at := tile_at(s, i, u, 3):
                        n, _, v = at
                        dve.wait_ge(E["y_ps"], n + 1)
                        dve.tensor_copy(desti[:, v:v + 1], rec[:, v, D:REC]).then_inc(E["di"], 1)
                        dve.tensor_copy(yrow[:, v, :], y_ps[:, 0:D]).then_inc(E["y"], 1)
                steps(dve, step, 3)

            @block.tensor
            def _(pe):
                def step(s, i, u):
                    if at := tile_at(s, i, u, 0):
                        n, r, _ = at
                        pe.wait_ge(rec_s[u], (r + 1) * 16)
                        wait(pe, E["x_lo"], n)
                        pe.transpose(xT_ps[:, 0:P], rec[:, u, 0:D], ident[:, :]).then_inc(E["xT_ps"], 1)
                    if at := tile_at(s, i, u, 1):
                        n, _, v = at
                        e = pe.value_load(tw[0:1, bass.ds(n, 1)], min_val=0, max_val=NE - 1)
                        pe.wait_ge(E["x_lo"], n + 1)
                        wait(pe, E["acts"], n - 1)
                        for k, (xs, ws) in enumerate(((x_hi, w_hi), (x_hi, w_lo), (x_lo, w_hi))):
                            for a in range(2):
                                mmi = pe.matmul(s_ps[:, 2 * (v % 2) + a, 0:F], xs[:, v % 2, :],
                                                ws[:, bass.ds(e, 1), a * F:(a + 1) * F].rearrange("p a f -> p (a f)"),
                                                start=(k == 0), stop=(k == 2))
                        mmi.then_inc(E["gu"], 1)
                    if at := tile_at(s, i, u, 2):
                        n, _, v = at
                        pe.wait_ge(E["acts"], n + 1)
                        wait(pe, E["aT"], n)
                        for c in range(FC):
                            mmi = pe.transpose(aT_ps[:, c * P:(c + 1) * P], acts[:, v % 2, c * P:(c + 1) * P],
                                               ident[:, :])
                        mmi.then_inc(E["aT_ps"], 1)
                    if at := tile_at(s, i, u, 3):
                        n, _, v = at
                        e = pe.value_load(tw[0:1, bass.ds(n, 1)], min_val=0, max_val=NE - 1)
                        pe.wait_ge(E["aT"], n + 1)
                        wait(pe, E["y"], n)
                        for c in range(FC):
                            mmi = pe.matmul(y_ps[:, 0:D], actsT[:, v % 2, c * P:(c + 1) * P],
                                            wd_sb[:, bass.ds(e, 1), c, :].rearrange("p a d -> p (a d)"),
                                            start=(c == 0), stop=(c == FC - 1))
                        mmi.then_inc(E["y_ps"], 1)

                pe.wait_ge(E["tab"], 2)
                steps(pe, step, 3)

        C = sems("c_", "ed e1 w1 w2 wg1 wg2 s out")
        NCH = 4
        CT = TT // NCH
        got = [sem(f"c_got{c}") for c in range(NCH)]
        ed = sb("ed", [P, TT])
        e1 = sb("e1", [P, TT])
        w1 = sb("w1", [P, TT])
        w2 = sb("w2", [P, TT])
        wg = sb("wg", [P, TOPK, TT])
        y0 = x_sb
        y1 = xnT[:, :].rearrange("p (t d) -> p t d", t=TT)
        with nc.Block() as block:
            @block.sync
            def _(sp):
                for c in range(NCH):
                    for k, dst in enumerate((y0, y1)):
                        r = k * NTOK + c * CT * P
                        sp.dma_start(dst[:, c * CT:(c + 1) * CT, :],
                                     places[r:r + CT * P, :].rearrange("(t p) d -> p t d", p=P)).then_inc(got[c], 16)
                for c in range(NCH):
                    sp.wait_ge(C["s"], TOPK * CT * (c + 1))
                    sp.dma_start(out[c * CT * P:(c + 1) * CT * P, :].rearrange("(t p) d -> p t d", p=P),
                                 xn[:, c * CT:(c + 1) * CT, :]).then_inc(C["out"], 16)
                sp.wait_ge(C["out"], NCH * 16)

            @block.scalar
            def _(act):
                act.activation(ed[:, :], gap[:, :], ACT.Exp).then_inc(C["ed"], 1)

            @block.vector
            def _(dve):
                dve.wait_ge(C["ed"], 1)
                dve.tensor_scalar(e1[:, :], ed[:, :], 1.0, None, ALU.add).then_inc(C["e1"], 1)
                dve.wait_ge(C["e1"], 1)
                dve.reciprocal(w1[:, :], e1[:, :]).then_inc(C["w1"], 1)
                dve.wait_ge(C["w1"], 1)
                dve.tensor_tensor(w2[:, :], w1[:, :], ed[:, :], ALU.mult).then_inc(C["w2"], 1)
                dve.tensor_scalar(wg[:, 0, :], w1[:, :], tg[:, 1:2], None, ALU.mult).then_inc(C["wg1"], 1)
                dve.wait_ge(C["w2"], 1)
                dve.tensor_scalar(wg[:, 1, :], w2[:, :], tg[:, 1:2], None, ALU.mult).then_inc(C["wg2"], 1)
                dve.wait_ge(C["wg1"], 1)
                dve.wait_ge(C["wg2"], 1)
                n = 0
                for c in range(NCH):
                    dve.wait_ge(got[c], 32)
                    for k, y in enumerate((y0, y1)):
                        if k:
                            dve.wait_ge(C["s"], n)
                        for t in range(c * CT, (c + 1) * CT):
                            dve.scalar_tensor_tensor(out=xn[:, t, :], in0=y[:, t, :], scalar=wg[:, k, t:t + 1],
                                                     in1=xn[:, t, :], op0=ALU.mult, op1=ALU.add).then_inc(C["s"], 1)
                            n += 1


def kernel(x, ctx_1024, mask_Bx1xS2_ik0, g_xattn, g_ffn, L0_xattn_Wq, L0_xattn_bq, L0_xattn_Wk, L0_xattn_bk,
           L0_xattn_Wv, L0_xattn_bv, L0_xattn_Wo, L0_xattn_bo, L0_ffn_router_w, L0_ffn_gate_proj,
           L0_ffn_up_proj, L0_ffn_down_proj):
    import numpy as np
    import concourse.bacc as bacc
    from concourse.bass_utils import run_bass_kernel_spmd

    def thrice(w):
        w = np.asarray(w).reshape(-1, BL, G, DH)
        o = np.zeros((w.shape[0], BL, G, GR), w.dtype)
        for c in range(3):
            o[..., c * DH:(c + 1) * DH] = w
        return o.reshape(w.shape[0], BL, P)

    def columns(b, one):
        o = thrice(b).reshape(BL, G, GR)
        o[..., MASK_ROW] = one
        return np.ascontiguousarray(o.reshape(BL, P).T)

    heads = (BL, G, DH)
    arrays = {
        "x": np.asarray(x).reshape(NTOK, D),
        "ctxT": np.ascontiguousarray(np.asarray(ctx_1024).transpose(0, 2, 1)).reshape(B * D, SK),
        "mask": np.ascontiguousarray(np.asarray(mask_Bx1xS2_ik0).reshape(B, KT, P).transpose(2, 0, 1)).reshape(P, B * KT),
        "wq": thrice(L0_xattn_Wq), "bq": columns(L0_xattn_bq, 1),
        "wk": thrice(L0_xattn_Wk), "bk": columns(L0_xattn_bk, 0),
        "wv": np.asarray(L0_xattn_Wv),
        "bv": np.ascontiguousarray(np.asarray(L0_xattn_bv).reshape(heads).transpose(1, 0, 2)).reshape(P, 1),
        "wo": np.ascontiguousarray(np.asarray(L0_xattn_Wo).reshape(*heads, D).transpose(1, 0, 2, 3)).reshape(P, D),
        "bo": np.asarray(L0_xattn_bo),
        "g": np.concatenate([np.asarray(g_xattn), np.asarray(g_ffn)]),
        "wr": np.asarray(L0_ffn_router_w),
        "wgate": np.asarray(L0_ffn_gate_proj), "wup": np.asarray(L0_ffn_up_proj),
        "wdown": np.asarray(L0_ffn_down_proj),
    }
    nc = bacc.Bacc("TRN2", target_bir_lowering=False, num_devices=1)
    aps = {k: nc.dram_tensor("in_" + k, a.shape, mybir.dt.from_np(a.dtype), kind="ExternalInput").ap()
           for k, a in arrays.items()}
    aps["out"] = nc.dram_tensor("out_x", (NTOK, D), F32, kind="ExternalOutput").ap()
    build(nc, **aps)
    r = run_bass_kernel_spmd(nc, [{"in_" + k: a for k, a in arrays.items()}], core_ids=[0])
    return r.results[0]["out_x"].reshape(B, SQ, D)
```

```python
from contextlib import ExitStack

import concourse.bass as bass
from concourse import mybir

F32 = mybir.dt.float32
F32R = mybir.dt.float32r
BF16 = mybir.dt.bfloat16
I32 = mybir.dt.int32
U32 = mybir.dt.uint32
ALU = mybir.AluOpType
ACT = mybir.ActivationFunctionType
AX = mybir.AxisListType

P = 128
D = 128
B, SQ, SK = 8, 256, 512
H, DH = 16, 8
G = 4
BL = H // G
GR = P // G
QT = SQ // P
KT = SK // P
NTOK = B * SQ
TT = NTOK // P
MASK_ROW = 3 * DH
VSTEP = G * GR + DH
DSTEP = GR + DH
BD = 2 * (BL * G * SQ + BL * G * P)
MASKED = -1.0e30
SCALE = float(DH) ** -0.5
EPS = 1e-5

NE, TOPK, F = 8, 2, 352
FC = -(-F // P)
FP = FC * P
REC = D + 1
CAP = NTOK + P
NTILES = TOPK * NTOK // P + NE
BLANK = NE * CAP
NOWHERE = 2 * TOPK * NTOK
BIG = 3.0e38


def wait(eng, sem, value):
    if isinstance(value, int) and value <= 0:
        return
    eng.wait_ge(sem, value)


def build(nc, x, ctxT, mask, wq, bq, wk, bk, wv, bv, wo, bo, g, wr, wgate, wup, wdown, out):
    ctx = ExitStack()
    with ctx:
        def sb(name, shape, dt=F32):
            return ctx.enter_context(nc.sbuf_tensor(name, shape, dt))

        def pb(name, shape):
            return ctx.enter_context(nc.psum_tensor(name, shape, F32))

        def sem(name):
            return ctx.enter_context(nc.semaphore(name))

        def sems(prefix, names):
            return {k: sem(prefix + k) for k in names.split()}

        lists = nc.dram_tensor("lists", (BLANK + P, REC), F32).ap()
        places = nc.dram_tensor("places", (TOPK * NTOK, D), F32).ap()

        x_sb = sb("x_sb", [P, TT, D])
        xn = sb("xn", [P, TT, D])
        xnT = sb("xnT", [P, NTOK])
        ident = sb("ident", [P, P])
        before = sb("before", [P, P], BF16)
        ones = sb("ones", [P, P], BF16)
        wq_sb = sb("wq_sb", [P, BL, P])
        wk_sb = sb("wk_sb", [P, BL, P])
        wv_sb = sb("wv_sb", [P, D])
        wo_sb = sb("wo_sb", [P, D])
        bq_sb = sb("bq_sb", [P, BL])
        bk_sb = sb("bk_sb", [P, BL])
        bv_sb = sb("bv_sb", [P, 1])
        bo_sb = sb("bo_sb", [P, D])
        wr_sb = sb("wr_sb", [P, NE])
        tg_in = sb("tg_in", [P, 2])
        tg = sb("tg", [P, 2])
        w_hi = sb("w_hi", [P, NE, 2 * F], F32R)
        w_lo = sb("w_lo", [P, NE, 2 * F], F32R)
        wd_sb = sb("wd_sb", [P, NE, FC, D])
        lows = sb("lows", [P, 2])
        split_q = sb("split_q", [P, 1])
        split_k = sb("split_k", [P, 1])
        sel = sb("sel", [P, H, P], F32R)
        selw = sb("selw", [P, H])
        halves = sb("halves", [P, TT])
        stats = sb("stats", [P, TT, 6])
        mv = sb("mv", [P, TT, 2])
        rstd = sb("rstd", [P, TT])
        varp = sb("varp", [P, TT])
        mask_in = sb("mask_in", [P, B, KT], I32)
        keep = sb("keep", [P, B, KT])
        early = sb("early", [P, 1])
        early_row = sb("early_row", [1, P])
        early_n = sb("early_n", [1, 1], I32)
        iota_e = sb("iota_e", [P, NE])
        base_e = sb("base_e", [P, NE])
        dest = sb("dest", [P, QT, TOPK])
        blank = sb("blank", [P, REC])

        attention_memory = ctx.enter_context(ExitStack())

        def att(name, shape, dt=F32):
            return attention_memory.enter_context(nc.sbuf_tensor(name, shape, dt))

        cnt = sb("cnt", [P, NE])
        gap = sb("gap", [P, TT])
        arena_r = att("arena_r", [P, 15360], F32R)
        arena = att("arena", [P, 3400])
        mrows = att("mrows", [P, KT, P])
        q_t = att("q_t", [P, BL, SQ])
        q_hi = att("q_hi", [P, BL, SQ], F32R)
        k_new = att("k_new", [P, BL, P], F32R)
        k_t = att("k_t", [P, BL, P])
        k_hi = att("k_hi", [P, BL, P], F32R)
        mraw = att("mraw", [P, KT, QT, H])
        mall = att("mall", [P, QT, H])
        mhi = att("mhi", [P, QT, H], F32R)
        mm = att("mm", [P, QT, P])
        mT = att("mT", [P, SQ], F32R)
        pt = att("pt", [P, 2, G * SQ])
        den = att("den", [P, SQ])
        ot0 = att("ot0", [P, SQ])
        oT = att("oT", [P, SQ])
        stats2 = att("stats2", [P, QT, 6])
        mv2 = att("mv2", [P, QT, 2])
        var2 = att("var2", [P, QT])
        rstd2 = att("rstd2", [P, QT])
        hrec = att("hrec", [P, QT, TOPK, REC])
        hT = att("hT", [P, SQ])
        logit = att("logit", [P, QT, NE])
        top = att("top", [P, QT, NE])
        topi = att("topi", [P, QT, NE], U32)
        topf = att("topf", [P, QT, TOPK])
        hot = att("hot", [P, QT, TOPK, NE])
        selb = att("selb", [P, QT, NE], BF16)
        pos = att("pos", [P, QT, NE])
        prod = att("prod", [P, QT, TOPK, NE])
        rowf = att("rowf", [P, QT, TOPK])
        rowi = att("rowi", [P, QT, TOPK], U32)

        s_ps = pb("s_ps", [P, 4, 512])
        pv_ps = pb("pv_ps", [P, 512])
        k_ps = pb("k_ps", [P, 512])
        q_ps = pb("q_ps", [P, 512])
        m_ps = pb("m_ps", [P, 512])
        s1_ps = s_ps[:, 0:2, :]
        s2_ps = s_ps[:, 2:4, :].rearrange("p a b -> p (a b)")

        S = sems("a_", "x mask w g wd wr halves rows ident ident_d tri ones blank st mv var rs ln "
                 "xT_ps xT tg xb keep early early_ps early_n lows split selw sel gu zero base wdz")
        with nc.Block() as block:
            @block.sync
            def _(sp):
                sp.dma_start(mask_in[:, :, :], mask.rearrange("p (b t) -> p b t", b=B)).then_inc(S["mask"], 16)
                sp.dma_start(x_sb[:, :, :], x.rearrange("(t p) d -> p t d", p=P)).then_inc(S["x"], 16)
                sp.dma_start(wq_sb[:, :, :], wq).then_inc(S["w"], 16)
                sp.dma_start(wk_sb[:, :, :], wk).then_inc(S["w"], 16)
                sp.dma_start(wv_sb[:, :], wv).then_inc(S["w"], 16)
                sp.dma_start(wo_sb[:, :], wo).then_inc(S["w"], 16)
                sp.dma_start(bq_sb[:, :], bq).then_inc(S["w"], 16)
                sp.dma_start(bk_sb[:, :], bk).then_inc(S["w"], 16)
                sp.dma_start(bv_sb[:, :], bv).then_inc(S["w"], 16)
                sp.dma_start(wr_sb[:, :], wr).then_inc(S["w"], 16)
                sp.dma_start(bo_sb[:, :], bo.partition_broadcast(P)).then_inc(S["g"], 16)
                sp.dma_start(tg_in[:, :], g.partition_broadcast(P)).then_inc(S["g"], 16)
                sp.wait_ge(S["wdz"], 1)
                for a, w in enumerate((wgate, wup)):
                    sp.dma_start(w_lo[:, :, a * F:(a + 1) * F].bitcast(F32),
                                 w.rearrange("e p f -> p e f")).then_inc(S["gu"], 16)
                for c in range(FC):
                    n = min(P, F - c * P)
                    sp.dma_start(wd_sb[0:n, :, c, :],
                                 wdown[:, c * P:c * P + n, :].rearrange("e p d -> p e d")).then_inc(S["wd"], 16)

            @block.gpsimd
            def _(pool):
                pool.memset(halves[:, :], -0.5).then_inc(S["halves"], 1)
                pool.memset(ident[:, :], 0.0).then_inc(S["ident"], 1)
                pool.memset(before[:, :], 1.0).then_inc(S["ones"], 1)
                pool.memset(ones[:, :], 1.0).then_inc(S["ones"], 1)
                pool.memset(blank[:, 0:D], 0.0).then_inc(S["blank"], 1)
                pool.memset(blank[:, D:REC], float(NOWHERE)).then_inc(S["blank"], 1)
                pool.wait_ge(S["ident"], 1)
                pool.affine_select(out=ident[:, :], in_=ident[:, :], compare_op=ALU.not_equal, fill=1.0, base=0,
                                   pattern=[[-1, P]], channel_multiplier=1).then_inc(S["ident_d"], 1)
                pool.wait_ge(S["ones"], 2)
                pool.affine_select(out=before[:, :], in_=before[:, :], compare_op=ALU.is_ge, fill=0.0, base=-1,
                                   pattern=[[1, P]], channel_multiplier=-1).then_inc(S["tri"], 1)
                pool.iota(iota_e[:, :], pattern=[[1, NE]], base=0, channel_multiplier=0,
                          allow_small_or_imprecise_dtypes=True).then_inc(S["base"], 1)
                pool.iota(base_e[:, :], pattern=[[CAP, NE]], base=0, channel_multiplier=0,
                          allow_small_or_imprecise_dtypes=True).then_inc(S["base"], 1)
                pool.iota(cnt[:, :], pattern=[[CAP, NE]], base=0, channel_multiplier=0,
                          allow_small_or_imprecise_dtypes=True).then_inc(S["base"], 1)
                pool.iota(dest[:, :, :], pattern=[[P, QT], [NTOK, TOPK]], base=0, channel_multiplier=1,
                          allow_small_or_imprecise_dtypes=True).then_inc(S["base"], 1)
                pool.wait_ge(S["halves"], 1)
                pool.wait_ge(S["var"], 1)
                pool.tensor_tensor(rstd[:, :], varp[:, :], halves[:, :], ALU.pow).then_inc(S["rs"], 1)
                pool.memset(arena[:, :], 0.0).then_inc(S["zero"], 1)
                pool.memset(arena_r[:, 0:BD].bitcast(F32), 0.0).then_inc(S["zero"], 1)
                pool.memset(mrows[:, :, :], 0.0).then_inc(S["zero"], 1)
                pool.wait_ge(S["blank"], 2)
                pool.dma_start(lists[BLANK:BLANK + P, :], blank[:, :]).then_inc(S["wr"], 16)
                pool.wait_ge(S["wr"], 16)

            @block.scalar
            def _(act):
                act.wait_ge(S["g"], 32)
                act.activation(tg[:, :], tg_in[:, :], ACT.Tanh).then_inc(S["tg"], 1)
                for c in range(NTOK // 512):
                    act.wait_ge(S["xT_ps"], c + 1)
                    act.activation(xnT[:, c * 512:(c + 1) * 512], s_ps[:, c, :], ACT.Copy).then_inc(S["xT"], 1)

            @block.vector
            def _(dve):
                dve.memset(wd_sb[F - (FC - 1) * P:P, :, FC - 1, :], 0.0).then_inc(S["wdz"], 1)
                dve.memset(mm[:, :, :], 0.0)
                dve.wait_ge(S["mask"], 16)
                dve.tensor_scalar(keep[:, :, :], mask_in[:, :, :], 0.0, None, ALU.not_equal).then_inc(S["keep"], 1)
                dve.wait_ge(S["keep"], 1)
                dve.tensor_reduce(early[:, :], keep[:, :, 0:KT - 1], AX.XY, ALU.max).then_inc(S["early"], 1)
                dve.wait_ge(S["x"], 16)
                for t in range(TT):
                    dve.bn_stats(stats[:, t, :], x_sb[:, t, :]).then_inc(S["st"], 1)
                for t in range(TT):
                    dve.wait_ge(S["st"], t + 1)
                    dve.bn_aggr(mv[:, t, :], stats[:, t, :]).then_inc(S["mv"], 1)
                dve.wait_ge(S["mv"], TT)
                dve.tensor_scalar(varp[:, :], mv[:, :, 1], EPS, None, ALU.add).then_inc(S["var"], 1)
                dve.wait_ge(S["ident_d"], 1)
                iv = ident[:, :].rearrange("p (g r) -> p g r", g=G)
                dve.tensor_reduce(lows[:, 0:1], iv[:, :, 2 * DH:3 * DH], AX.XY, ALU.add).then_inc(S["lows"], 1)
                dve.tensor_reduce(lows[:, 1:2], iv[:, :, DH:2 * DH], AX.XY, ALU.add).then_inc(S["lows"], 1)
                dve.tensor_tensor(selw[:, :], ident[:, 0:H], ident[:, H:2 * H], ALU.add).then_inc(S["selw"], 1)
                dve.wait_ge(S["lows"], 2)
                dve.tensor_scalar(split_q[:, :], lows[:, 0:1], -1.0, None, ALU.mult).then_inc(S["split"], 1)
                dve.tensor_scalar(split_k[:, :], lows[:, 1:2], -1.0, None, ALU.mult).then_inc(S["split"], 1)
                dve.wait_ge(S["selw"], 1)
                dve.tensor_copy(sel[:, :, :], selw[:, :].unsqueeze(2).broadcast_to([P, H, P])).then_inc(S["sel"], 1)
                dve.wait_ge(S["early_ps"], 1)
                dve.tensor_reduce(early_n[:, :], m_ps[0:1, 0:P], AX.X, ALU.max).then_inc(S["early_n"], 1)
                dve.wait_ge(S["rs"], 1)
                for t in range(TT):
                    dve.tensor_scalar(xn[:, t, :], x_sb[:, t, :], mv[:, t, 0:1], rstd[:, t:t + 1],
                                      ALU.subtract, ALU.mult).then_inc(S["ln"], 1)
                dve.wait_ge(S["ln"], TT)
                dve.wait_ge(S["tg"], 1)
                dve.scalar_tensor_tensor(out=x_sb[:, :, :], in0=bo_sb[:, :].unsqueeze(1).broadcast_to([P, TT, D]),
                                         scalar=tg[:, 0:1], in1=x_sb[:, :, :], op0=ALU.mult,
                                         op1=ALU.add).then_inc(S["xb"], 1)

            @block.tensor
            def _(pe):
                pe.wait_ge(S["ident_d"], 1)
                pe.wait_ge(S["early"], 1)
                pe.transpose(m_ps[0:1, 0:P], early[:, :], ident[:, :]).then_inc(S["early_ps"], 1)
                for t in range(TT):
                    pe.wait_ge(S["ln"], t + 1)
                    tr = pe.transpose(s_ps[:, t // 4, (t % 4) * P:(t % 4 + 1) * P], xn[:, t, :], ident[:, :])
                    if t % 4 == 3:
                        tr.then_inc(S["xT_ps"], 1)

        settled = sem("settled")

        def settle(eng):
            eng.sem_inc(settled, 1)

        T = sems("b_", "q_ps q_ev q_hi q_spl k_ps k_ev k_hi k_spl mrow v_ps v_ev dn s1 mx mall mhi mlo mm "
                 "mT_ps mT s2 ex pv den ot oT y x2 r_st r_mv r_var r_rs r_h r_hd r_dest r_hT_ps r_hT r_lg_ps "
                 "r_lg r_top r_ti r_tf r_hot r_sel r_gap r_rk_ps r_pos r_prod r_row r_cnt r_rowi r_sent")
        ctx_s = [sem(f"b_ctx{u}") for u in range(2)]
        q_bd = [sem(f"b_qbd{u}") for u in range(2)]
        k_bd = [sem(f"b_kbd{u}") for u in range(2)]
        k_cp = [sem(f"b_kcp{u}") for u in range(2)]

        def attention(nt, depth):
            def part(tensor, at, shape):
                size = 1
                for s in shape:
                    size *= s
                v = tensor[:, at[0]:at[0] + size]
                at[0] += size
                letters = "abcde"[:len(shape)]
                if len(shape) > 1:
                    v = v.rearrange(f"p ({' '.join(letters)}) -> p {' '.join(letters)}",
                                    **{k: s for k, s in zip(letters[:-1], shape[:-1])})
                return v

            at = [0]
            qbd = part(arena_r, at, (depth, BL, G, SQ))
            kbd = part(arena_r, at, (2, BL, G, P))
            assert at[0] <= BD
            qd = part(arena_r, at, (depth, BL, SQ))
            kd = part(arena_r, at, (depth, nt, BL, P))
            assert at[0] <= arena_r.shape[1]
            at = [0]
            ctx_in = part(arena, at, (depth, nt * P))
            vn = part(arena, at, (depth, nt, BL * VSTEP))
            dn = part(arena, at, (depth, nt, BL * DSTEP))
            mrow = mrows[:, 0:depth * nt, :].rearrange("p (u n) k -> p u n k", u=depth)
            assert at[0] <= arena.shape[1]

            U = BL * nt

            def drive(eng, general, iteration):
                if depth == 1:
                    general((0, 0, 0))
                    with eng.Fori(1, B) as n:
                        general((n, n, 0))
                    return

                def row(n, i, u, off):
                    if isinstance(n, int) and not 0 <= n + off < B:
                        return None
                    return n + off, i + (u + off) // 2, (u + off) % 2

                def run(n, i, u):
                    iteration(lambda off, work, *a: row(n, i, u, off) and work(row(n, i, u, off), *a))

                for n in range(-2, 2):
                    run(n, n // 2, n % 2)
                with eng.Fori(1, B // 2 - 1) as i:
                    run(i * 2, i, 0)
                    run(i * 2 + 1, i, 1)
                for n in range(B - 2, B + 1):
                    run(n, n // 2, n % 2)

            def kbuf(u, kt):
                return u if nt == 1 else kt % 2

            def k_uses(at, kt):
                n, i, u = at
                return i + 1 if nt == 1 else n * (nt // 2) + (kt // 2 + 1)

            def sync_(sp):
                def load(at):
                    n, i, u = at
                    wait(sp, T["v_ps"], nt * (n - depth + 1))
                    sp.dma_start(ctx_in[:, u, :],
                                 ctxT[bass.ds(n * P, P), (KT - nt) * P:KT * P]).then_inc(ctx_s[u], 16)

                def k_groups(at, kt):
                    n, i, u = at
                    m = n * nt + kt
                    kb = kbuf(u, kt)
                    wait(sp, T["k_spl"], m + 1)
                    settle(sp)
                    wait(sp, T["s1"], BL * (m - 1))
                    for gr in range(G):
                        r = slice(gr * GR, (gr + 1) * GR)
                        sp.dma_start(kbd[r, kb, :, gr, :].bitcast(F32),
                                     k_new[r, :, :].bitcast(F32)).then_inc(k_bd[kb], 16)

                def k_copy(at, kt):
                    n, i, u = at
                    wait(sp, T["s2"], U * (n - depth + 1))
                    settle(sp)
                    sp.dma_start(kd[:, u, kt, :, :].bitcast(F32), k_new[:, :, :].bitcast(F32)).then_inc(k_cp[u], 16)

                def q_groups(at):
                    n, i, u = at
                    wait(sp, T["q_spl"], n + 1)
                    settle(sp)
                    wait(sp, T["s2"], U * (n - depth + 1))
                    for gr in range(G):
                        r = slice(gr * GR, (gr + 1) * GR)
                        sp.dma_start(qbd[r, u, :, gr, :].bitcast(F32),
                                     qd[r, u, :, :].bitcast(F32)).then_inc(q_bd[u], 16)

                def general(at):
                    load(at)
                    for kt in range(nt):
                        k_groups(at, kt)
                        k_copy(at, kt)
                    q_groups(at)

                def iteration(on):
                    on(2, load)
                    on(2, k_groups, 0)
                    on(2, k_copy, 0)
                    on(2, q_groups)

                drive(sp, general, iteration)

            def gpsimd_(pool):
                def route(at):
                    n = at[0]
                    pool.wait_ge(T["r_var"], n + 1)
                    pool.tensor_tensor(rstd2[:, :], var2[:, :], halves[:, 0:QT], ALU.pow).then_inc(T["r_rs"], 1)
                    pool.wait_ge(T["r_rowi"], n + 1)
                    pool.wait_ge(T["r_hd"], n + 1)
                    settle(pool)
                    for t in range(QT):
                        for k in range(TOPK):
                            pool.indirect_dma_start(
                                lists, bass.IndirectOffsetOnAxis(ap=rowi[:, t, k:k + 1], axis=0),
                                hrec[:, t, k, :], None, bounds_check=BLANK - 1,
                                oob_is_err=False).then_inc(T["r_sent"], 16)

                drive(pool, route, lambda on: on(-1, route))
                pool.wait_ge(T["r_sent"], B * QT * TOPK * 16)

            def scalar_(act):
                def q_out(at, r):
                    n = at[0]
                    act.wait_ge(T["q_ps"], n * 2 + (r + 1))
                    if r == 0:
                        wait(act, T["q_spl"], n)
                    for j in (2 * r, 2 * r + 1):
                        act.activation(q_t[:, j, :], q_ps[:, (j % 2) * SQ:(j % 2 + 1) * SQ], ACT.Identity,
                                       bias=bq_sb[:, j:j + 1]).then_inc(T["q_ev"], 1)
                    if r == 1:
                        act.wait_ge(T["q_ev"], (n + 1) * BL)
                        act.activation(q_hi[:, :, :], q_t[:, :, :], ACT.Copy).then_inc(T["q_hi"], 1)

                def k_out(at, kt):
                    m = at[0] * nt + kt
                    act.wait_ge(T["k_ps"], m + 1)
                    wait(act, T["k_spl"], m)
                    for j in range(BL):
                        act.activation(k_t[:, j, :], k_ps[:, j * P:(j + 1) * P], ACT.Identity,
                                       bias=bk_sb[:, j:j + 1]).then_inc(T["k_ev"], 1)
                    act.wait_ge(T["k_ev"], (m + 1) * BL)
                    act.activation(k_hi[:, :, :], k_t[:, :, :], ACT.Copy).then_inc(T["k_hi"], 1)

                def mT_out(at):
                    n = at[0]
                    act.wait_ge(T["mT_ps"], n + 1)
                    wait(act, T["s2"], U * n)
                    act.activation(mT[:, :], m_ps[:, 0:SQ], ACT.Copy).then_inc(T["mT"], 1)

                def exps(at, m):
                    n = at[0]
                    act.wait_ge(T["s2"], n * U + (m + 1))
                    wait(act, T["pv"], n * U + (m - 1))
                    act.activation(pt[:, m % 2, :], s2_ps, ACT.Exp, scale=SCALE).then_inc(T["ex"], 1)

                def bias_v(at):
                    n = at[0]
                    act.wait_ge(T["ot"], n + 1)
                    wait(act, T["y"], n)
                    act.activation(oT[:, :], ot0[:, :], ACT.Identity, bias=bv_sb[:, :]).then_inc(T["oT"], 1)

                def hT_out(at):
                    n = at[0]
                    act.wait_ge(T["r_hT_ps"], n + 1)
                    wait(act, T["r_lg_ps"], n)
                    act.activation(hT[:, :], m_ps[:, 0:SQ], ACT.Copy).then_inc(T["r_hT"], 1)

                def general(at):
                    q_out(at, 0)
                    q_out(at, 1)
                    for kt in range(nt):
                        k_out(at, kt)
                    mT_out(at)
                    for m in range(U):
                        exps(at, m)
                    bias_v(at)
                    hT_out(at)

                def iteration(on):
                    on(0, mT_out)
                    on(-1, bias_v)
                    on(2, q_out, 0)
                    on(0, exps, 0)
                    on(2, q_out, 1)
                    on(0, exps, 1)
                    on(2, k_out, 0)
                    on(0, exps, 2)
                    on(-1, hT_out)
                    on(0, exps, 3)

                drive(act, general, iteration)

            def vector_(dve):
                def kept(at):
                    return keep[:, bass.ds(at[0], 1), KT - nt:KT].rearrange("p a t -> p (a t)")

                def mask_rows(at):
                    n, i, u = at
                    wait(dve, T["k_ps"], nt * (n - depth + 1))
                    dve.tensor_scalar(mrow[:, u, :, :].rearrange("p n (g r) -> p n g r", g=G)[:, :, :, MASK_ROW],
                                      kept(at).unsqueeze(2).broadcast_to([P, nt, G]), 1.0, -MASKED, ALU.subtract,
                                      ALU.mult).then_inc(T["mrow"], 1)

                def ones_in(at):
                    n, i, u = at
                    wait(dve, T["pv"], U * (n - depth + 1))
                    settle(dve)
                    dve.tensor_copy(dn[:, u, :, :].rearrange("p n (j c) -> p n j c", j=BL)[:, :, :, 0:DH],
                                    kept(at).unsqueeze(2).unsqueeze(3).broadcast_to([P, nt, BL, DH])
                                    ).then_inc(T["dn"], 1)

                def q_split(at):
                    n, i, u = at
                    dve.wait_ge(T["q_hi"], n + 1)
                    wait(dve, T["s1"], U * (n - depth + 1))
                    if not (isinstance(n, int) and n < depth):
                        dve.wait_ge(q_bd[u], i * 64)
                    dve.scalar_tensor_tensor(out=qd[:, u, :, :], in0=q_hi[:, :, :], scalar=split_q[:, :],
                                             in1=q_t[:, :, :], op0=ALU.mult, op1=ALU.add).then_inc(T["q_spl"], 1)

                def k_split(at, kt):
                    n, i, u = at
                    m = n * nt + kt
                    dve.wait_ge(T["k_hi"], m + 1)
                    if nt == 1 and not (isinstance(n, int) and n == 0):
                        before_i = i if u == 0 else i + 1
                        dve.wait_ge(k_bd[1 - u], before_i * 64)
                        dve.wait_ge(k_cp[1 - u], before_i * 16)
                    elif nt > 1 and kt:
                        dve.wait_ge(k_bd[(kt - 1) % 2], k_uses(at, kt - 1) * 64)
                        dve.wait_ge(k_cp[0], m * 16)
                    elif nt > 1 and not (isinstance(n, int) and n == 0):
                        dve.wait_ge(k_bd[1], n * (nt // 2) * 64)
                        dve.wait_ge(k_cp[0], m * 16)
                    dve.scalar_tensor_tensor(out=k_new[:, :, :], in0=k_hi[:, :, :], scalar=split_k[:, :],
                                             in1=k_t[:, :, :], op0=ALU.mult, op1=ALU.add).then_inc(T["k_spl"], 1)

                def v_out(at, kt):
                    n, i, u = at
                    dve.wait_ge(T["v_ps"], n * nt + (kt + 1))
                    wait(dve, T["pv"], U * (n - depth + 1))
                    vv = vn[:, u, kt, :].rearrange("p (j c) -> p j c", j=BL)[:, :, 0:G * GR]
                    vv = vv.rearrange("p j (g c) -> p j g c", g=G)[:, :, :, 0:DH]
                    dve.tensor_scalar(vv, q_ps[:, 0:P].rearrange("p (j g d) -> p j g d", j=BL, g=G),
                                      kept(at)[:, kt:kt + 1], None, ALU.mult).then_inc(T["v_ev"], 1)

                def most(at, v):
                    n = at[0]
                    kt, j = v // BL, v % BL
                    dve.wait_ge(T["s1"], n * U + (v + 1))
                    if v == 0:
                        wait(dve, T["mlo"] if nt == 1 else T["mall"], n)
                    dve.tensor_reduce(mraw[:, kt, :, j * G:(j + 1) * G],
                                      s1_ps[:, :, :].rearrange("p a (g k) -> p a g k", g=G),
                                      AX.X, ALU.max).then_inc(T["mx"], 1)

                def most_all(at):
                    n = at[0]
                    dve.wait_ge(T["mx"], (n + 1) * U)
                    wait(dve, T["mlo"], n)
                    if nt == 1:
                        greatest = mraw[:, 0, :, :]
                    else:
                        greatest = mall
                        dve.tensor_reduce(mall[:, :, :], mraw[:, 0:nt, :, :].rearrange("p n a h -> p a h n"), AX.X,
                                          ALU.max).then_inc(T["mall"], 1)
                        dve.wait_ge(T["mall"], n + 1)
                    wait(dve, T["mm"], n)
                    dve.tensor_scalar(mhi[:, :, :], greatest[:, :, :], -1.0, None, ALU.mult).then_inc(T["mhi"], 1)
                    dve.wait_ge(T["mhi"], n + 1)
                    wait(dve, T["mT_ps"], n)
                    low = dve.scalar_tensor_tensor(out=mm[:, :, H:2 * H], in0=greatest[:, :, :], scalar=-1.0,
                                                   in1=mhi[:, :, :], op0=ALU.mult, op1=ALU.subtract)
                    low.then_inc(T["mlo"], 1)
                    dve.tensor_copy(mm[:, :, 0:H], mhi[:, :, :]).then_inc(T["mm"], 1)

                def divide(at):
                    n = at[0]
                    dve.wait_ge(T["pv"], (n + 1) * U)
                    wait(dve, T["oT"], n)
                    wait(dve, T["ot"], n)
                    dve.reciprocal(den[:, :], pv_ps[:, SQ:2 * SQ]).then_inc(T["den"], 1)
                    dve.wait_ge(T["den"], n + 1)
                    dve.tensor_tensor(ot0[:, :], pv_ps[:, 0:SQ], den[:, :], ALU.mult).then_inc(T["ot"], 1)

                def residual(at):
                    n = at[0]
                    dve.wait_ge(T["y"], n + 1)
                    for t in range(QT):
                        k = n * QT + t
                        dve.scalar_tensor_tensor(out=xn[:, bass.ds(k, 1), :],
                                                 in0=pv_ps[:, t * P:(t + 1) * P].unsqueeze(1),
                                                 scalar=tg[:, 0:1], in1=x_sb[:, bass.ds(k, 1), :], op0=ALU.mult,
                                                 op1=ALU.add).then_inc(T["x2"], 1)

                def deviations(at):
                    n = at[0]
                    dve.wait_ge(T["x2"], (n + 1) * QT)
                    for t in range(QT):
                        wait(dve, T["r_mv"], n * QT)
                        settle(dve)
                        dve.bn_stats(stats2[:, t, :],
                                     xn[:, bass.ds(n * QT + t, 1), :].rearrange("p a d -> p (a d)")
                                     ).then_inc(T["r_st"], 1)
                    for t in range(QT):
                        dve.wait_ge(T["r_st"], n * QT + (t + 1))
                        wait(dve, T["r_h"], n * QT)
                        settle(dve)
                        dve.bn_aggr(mv2[:, t, :], stats2[:, t, :]).then_inc(T["r_mv"], 1)
                    dve.wait_ge(T["r_mv"], (n + 1) * QT)
                    wait(dve, T["r_rs"], n)
                    dve.tensor_scalar(var2[:, :], mv2[:, :, 1], EPS, None, ALU.add).then_inc(T["r_var"], 1)

                def records(at):
                    n = at[0]
                    dve.wait_ge(T["r_rs"], n + 1)
                    wait(dve, T["r_sent"], n * QT * TOPK * 16)
                    for t in range(QT):
                        dve.tensor_scalar(hrec[:, t, :, 0:D],
                                          xn[:, bass.ds(n * QT + t, 1), :].broadcast_to([P, TOPK, D]),
                                          mv2[:, t, 0:1], rstd2[:, t:t + 1], ALU.subtract,
                                          ALU.mult).then_inc(T["r_h"], 1)
                    wait(dve, T["r_dest"], n)
                    dve.tensor_copy(hrec[:, :, :, D:REC], dest[:, :, :].unsqueeze(3)).then_inc(T["r_hd"], 1)
                    dve.wait_ge(T["r_hd"], n + 1)
                    dve.tensor_scalar(dest[:, :, :], dest[:, :, :], float(SQ), None,
                                      ALU.add).then_inc(T["r_dest"], 1)

                def choices(at):
                    n = at[0]
                    dve.wait_ge(T["r_lg_ps"], n + 1)
                    wait(dve, T["r_ti"], n * QT)
                    dve.tensor_scalar(logit[:, :, :], m_ps[:, SQ:SQ + QT * NE].rearrange("p (t e) -> p t e", t=QT),
                                      -BIG, BIG, ALU.max, ALU.min).then_inc(T["r_lg"], 1)
                    dve.wait_ge(T["r_lg"], n + 1)
                    wait(dve, T["r_gap"], n)
                    settle(dve)
                    for t in range(QT):
                        dve.max(top[:, t, :], logit[:, t, :]).then_inc(T["r_top"], 1)
                    for t in range(QT):
                        if t == 0:
                            wait(dve, T["r_tf"], n)
                        dve.wait_ge(T["r_top"], n * QT + (t + 1))
                        settle(dve)
                        dve.max_index(topi[:, t, :], top[:, t, :], logit[:, t, :]).then_inc(T["r_ti"], 1)
                    dve.tensor_tensor(gap[:, bass.ds(n * QT, QT)], top[:, :, 1], top[:, :, 0],
                                      ALU.subtract).then_inc(T["r_gap"], 1)
                    dve.wait_ge(T["r_ti"], (n + 1) * QT)
                    wait(dve, T["r_hot"], n)
                    dve.tensor_copy(topf[:, :, :], topi[:, :, 0:TOPK]).then_inc(T["r_tf"], 1)
                    dve.wait_ge(T["r_tf"], n + 1)
                    wait(dve, T["r_prod"], n)
                    wait(dve, T["r_sel"], n)
                    dve.tensor_tensor(hot[:, :, :, :],
                                      iota_e[:, :].unsqueeze(1).unsqueeze(1).broadcast_to([P, QT, TOPK, NE]),
                                      topf[:, :, :].unsqueeze(3).broadcast_to([P, QT, TOPK, NE]),
                                      ALU.is_equal).then_inc(T["r_hot"], 1)
                    dve.wait_ge(T["r_hot"], n + 1)
                    wait(dve, T["r_rk_ps"], n)
                    dve.tensor_tensor(selb[:, :, :], hot[:, :, 0, :], hot[:, :, 1, :],
                                      ALU.add).then_inc(T["r_sel"], 1)

                def ranks(at):
                    n = at[0]
                    dve.wait_ge(T["r_rk_ps"], n + 1)
                    wait(dve, T["r_cnt"], n)
                    r0 = SQ + QT * NE
                    dve.tensor_tensor(pos[:, :, :], m_ps[:, r0:r0 + QT * NE].rearrange("p (t e) -> p t e", t=QT),
                                      cnt[:, :].unsqueeze(1).broadcast_to([P, QT, NE]),
                                      ALU.add).then_inc(T["r_pos"], 1)
                    dve.wait_ge(T["r_pos"], n + 1)
                    dve.tensor_tensor(cnt[:, :], cnt[:, :], m_ps[:, r0 + QT * NE:r0 + (QT + 1) * NE],
                                      ALU.add).then_inc(T["r_cnt"], 1)
                    wait(dve, T["r_row"], n)
                    dve.tensor_tensor(prod[:, :, :, :], hot[:, :, :, :],
                                      pos[:, :, :].unsqueeze(2).broadcast_to([P, QT, TOPK, NE]),
                                      ALU.mult).then_inc(T["r_prod"], 1)
                    dve.wait_ge(T["r_prod"], n + 1)
                    wait(dve, T["r_rowi"], n)
                    dve.tensor_reduce(rowf[:, :, :], prod[:, :, :, :], AX.X, ALU.add).then_inc(T["r_row"], 1)
                    dve.wait_ge(T["r_row"], n + 1)
                    dve.tensor_copy(rowi[:, :, :], rowf[:, :, :]).then_inc(T["r_rowi"], 1)

                def general(at):
                    mask_rows(at)
                    ones_in(at)
                    q_split(at)
                    for kt in range(nt):
                        k_split(at, kt)
                        v_out(at, kt)
                        for j in range(BL):
                            most(at, kt * BL + j)
                    most_all(at)
                    divide(at)
                    residual(at)
                    for part_ in (deviations, records, choices, ranks):
                        part_(at)

                def iteration(on):
                    on(2, mask_rows)
                    on(-1, divide)
                    on(1, ones_in)
                    on(-1, residual)
                    on(-1, deviations)
                    on(1, most, 0)
                    on(-1, records)
                    on(1, v_out, 0)
                    on(2, q_split)
                    on(1, most, 1)
                    on(1, most, 2)
                    on(2, k_split, 0)
                    on(1, most, 3)
                    on(1, most_all)
                    on(-1, choices)
                    on(-1, ranks)

                drive(dve, general, iteration)

            def tensor_(pe):
                def q_project(at, r):
                    n = at[0]
                    if r == 0:
                        wait(pe, T["v_ev"], n * nt if depth == 1 else n - 1)
                    wait(pe, T["q_ev"], n * BL + 2 * r)
                    for j in (2 * r, 2 * r + 1):
                        mmi = pe.matmul(q_ps[:, (j % 2) * SQ:(j % 2 + 1) * SQ], wq_sb[:, j, :],
                                        xnT[:, bass.ds(n * SQ, SQ)], start=True, stop=True)
                    mmi.then_inc(T["q_ps"], 1)

                def k_project(at, kt):
                    n, i, u = at
                    if kt == 0:
                        pe.wait_ge(ctx_s[u], (i + 1) * 16)
                        pe.wait_ge(T["mrow"], n + 1)
                    wait(pe, T["k_ev"], (n * nt + kt) * BL)
                    for j in range(BL):
                        o = k_ps[:, j * P:(j + 1) * P]
                        pe.matmul(o, wk_sb[:, j, :], ctx_in[:, u, kt * P:(kt + 1) * P], start=True, stop=False)
                        mmi = pe.matmul(o, mrow[:, u, kt, :], ident[:, :], start=False, stop=True)
                    mmi.then_inc(T["k_ps"], 1)

                def v_project(at, kt):
                    n, i, u = at
                    ahead = n + 1 if depth == 1 else min(n + 2, B) if isinstance(n, int) else n + 2
                    pe.wait_ge(T["q_ev"], ahead * BL)
                    wait(pe, T["v_ev"], n * nt + kt)
                    pe.matmul(q_ps[:, 0:P], ctx_in[:, u, kt * P:(kt + 1) * P], wv_sb[:, :], start=True,
                              stop=True).then_inc(T["v_ps"], 1)

                def by_query(at, v):
                    n, i, u = at
                    kt, j = v // BL, v % BL
                    if v == 0:
                        pe.wait_ge(T["q_spl"], n + 1)
                    if j == 0:
                        pe.wait_ge(k_bd[kbuf(u, kt)], k_uses(at, kt) * 64)
                    wait(pe, T["mx"], n * U + v)
                    for t in range(QT):
                        mmi = pe.matmul(s1_ps[:, t, :], qd[:, u, j, t * P:(t + 1) * P],
                                        kbd[:, kbuf(u, kt), j, :, :].rearrange("p g k -> p (g k)"), start=True,
                                        stop=True)
                    mmi.then_inc(T["s1"], 1)

                def turn_most(at):
                    n = at[0]
                    pe.wait_ge(T["mm"], n + 1)
                    pe.wait_ge(T["mlo"], n + 1)
                    wait(pe, T["r_cnt"], n - 1 if depth == 2 else n)
                    for t in range(QT):
                        mmi = pe.transpose(m_ps[:, t * P:(t + 1) * P], mm[:, t, :], ident[:, :])
                    mmi.then_inc(T["mT_ps"], 1)

                def by_key(at, m):
                    n, i, u = at
                    kt, j = m // BL, m % BL
                    if m == 0:
                        pe.wait_ge(q_bd[u], (i + 1) * 64)
                        pe.wait_ge(k_cp[u], (i + 1) * nt * 16)
                        pe.wait_ge(T["mT"], n + 1)
                    wait(pe, T["ex"], n * U + m)
                    for a in range(2):
                        o = s2_ps[:, a * 512:(a + 1) * 512]
                        pe.matmul(o, kd[:, u, kt, j, :], qbd[:, u, j, 2 * a:2 * a + 2, :].rearrange("p g q -> p (g q)"),
                                  start=True, stop=False, skip_group_check=True)
                        for gr in (2 * a, 2 * a + 1):
                            mmi = pe.matmul(o[:, (gr % 2) * SQ:(gr % 2 + 1) * SQ], sel[:, j * G + gr, :],
                                            mT[:, :], start=False, stop=(gr % 2 == 1), skip_group_check=True)
                    mmi.then_inc(T["s2"], 1)

                def values(at, m):
                    n, i, u = at
                    kt, j = m // BL, m % BL
                    if m == 0:
                        pe.wait_ge(T["dn"], n + 1)
                        pe.wait_ge(T["v_ev"], (n + 1) * nt)
                        wait(pe, T["x2"], n * QT)
                    pe.wait_ge(T["ex"], n * U + (m + 1))
                    for gr in range(G):
                        o = slice(gr * GR, (gr + 1) * GR)
                        r = pt[:, m % 2, gr * SQ:(gr + 1) * SQ]
                        c = (j * G + gr) * GR
                        pe.matmul(pv_ps[o, 0:SQ], vn[:, u, kt, c:c + GR], r, start=(m == 0),
                                  stop=(m == U - 1), skip_group_check=True)
                        mmi = pe.matmul(pv_ps[o, SQ:2 * SQ], dn[:, u, kt, j * GR:(j + 1) * GR], r,
                                        start=False, stop=(m == U - 1), skip_group_check=True)
                    mmi.then_inc(T["pv"], 1)

                def project_out(at):
                    pe.wait_ge(T["oT"], at[0] + 1)
                    for t in range(QT):
                        mmi = pe.matmul(pv_ps[:, t * P:(t + 1) * P], oT[:, t * P:(t + 1) * P], wo_sb[:, :],
                                        start=True, stop=True)
                    mmi.then_inc(T["y"], 1)

                def turn_rows(at):
                    pe.wait_ge(T["r_h"], (at[0] + 1) * QT)
                    for t in range(QT):
                        mmi = pe.transpose(m_ps[:, t * P:(t + 1) * P], hrec[:, t, 0, 0:D], ident[:, :])
                    mmi.then_inc(T["r_hT_ps"], 1)

                def logits(at):
                    pe.wait_ge(T["r_hT"], at[0] + 1)
                    for t in range(QT):
                        mmi = pe.matmul(m_ps[:, SQ + t * NE:SQ + (t + 1) * NE], hT[:, t * P:(t + 1) * P],
                                        wr_sb[:, :], start=True, stop=True)
                    mmi.then_inc(T["r_lg_ps"], 1)

                def rank(at):
                    pe.wait_ge(T["r_sel"], at[0] + 1)
                    pe.wait_ge(T["r_lg"], at[0] + 1)
                    r0 = SQ + QT * NE
                    pe.matmul(m_ps[:, r0:r0 + QT * NE], before[:, :], selb[:, :, :].rearrange("p t e -> p (t e)"),
                              start=True, stop=False, skip_group_check=True)
                    for t in range(1, QT):
                        for s in range(t):
                            pe.matmul(m_ps[:, r0 + t * NE:r0 + (t + 1) * NE], ones[:, :], selb[:, s, :],
                                      start=False, stop=False, skip_group_check=True)
                    for t in range(QT):
                        mmi = pe.matmul(m_ps[:, r0 + QT * NE:r0 + (QT + 1) * NE], ones[:, :], selb[:, t, :],
                                        start=False, stop=(t == QT - 1), skip_group_check=True)
                    mmi.then_inc(T["r_rk_ps"], 1)

                def general(at):
                    q_project(at, 0)
                    q_project(at, 1)
                    for kt in range(nt):
                        k_project(at, kt)
                        v_project(at, kt)
                        for j in range(BL):
                            by_query(at, kt * BL + j)
                    turn_most(at)
                    for m in range(U):
                        by_key(at, m)
                        if m:
                            values(at, m - 1)
                    values(at, U - 1)
                    project_out(at)
                    turn_rows(at)
                    logits(at)
                    rank(at)

                def iteration(on):
                    on(0, turn_most)
                    on(2, q_project, 0)
                    on(-1, project_out)
                    on(0, by_key, 0)
                    on(1, by_query, 0)
                    on(2, q_project, 1)
                    on(0, by_key, 1)
                    on(0, values, 0)
                    on(1, v_project, 0)
                    on(1, by_query, 1)
                    on(2, k_project, 0)
                    on(0, by_key, 2)
                    on(0, values, 1)
                    on(1, by_query, 2)
                    on(-1, turn_rows)
                    on(0, by_key, 3)
                    on(1, by_query, 3)
                    on(-1, logits)
                    on(0, values, 2)
                    on(0, values, 3)
                    on(-1, rank)

                drive(pe, general, iteration)

            return sync_, gpsimd_, scalar_, vector_, tensor_

        general = attention(KT, 1)
        short = attention(1, 2)

        def choose(eng, k):
            n = eng.value_load(early_n[0:1, 0:1], min_val=0, max_val=1)
            with eng.If(n == 0):
                short[k](eng)
            with eng.Else():
                general[k](eng)

        with nc.Block() as block:
            @block.sync
            def _(sp):
                choose(sp, 0)

            @block.gpsimd
            def _(pool):
                choose(pool, 1)

            @block.scalar
            def _(act):
                choose(act, 2)

            @block.vector
            def _(dve):
                choose(dve, 3)

            @block.tensor
            def _(pe):
                choose(pe, 4)

        attention_memory.close()
        NT = NTILES
        NB = 8
        tile_i = sb("tile_i", [P, NT])
        part_i = sb("part_i", [P, 1])
        lane_e = sb("lane_e", [P, NE])
        lane_i = sb("lane_i", [P, NE], U32)
        used = sb("used", [P, NE])
        usedi = sb("usedi", [P, NE], I32)
        tilesi = sb("tilesi", [P, NE], I32)
        tiles = sb("tiles", [P, NE])
        ends = sb("ends", [P, NE])
        past = sb("past", [P, NT, NE])
        skip = sb("skip", [P, NT, NE])
        te = sb("te", [P, NT])
        ts_ = sb("ts_", [P, NT])
        tb = sb("tb", [P, NT])
        ti = sb("ti", [P, NT], I32)
        tw = sb("tw", [P, NT], I32)
        t0 = sb("t0", [P, NT])
        td = sb("td", [P, NT], I32)
        rec = sb("rec", [P, NB, REC])
        x_hi = sb("x_hi", [P, 2, P], F32R)
        x_lo = sb("x_lo", [P, 2, P], F32R)
        silu = sb("silu", [P, 2, F])
        acts = sb("acts", [P, 2, FP])
        actsT = sb("actsT", [P, 2, FP])
        yrow = sb("yrow", [P, NB, D])
        desti = sb("desti", [P, NB], U32)

        E = sems("e_", "iota lane lanei fill used usedi tilesi tiles ends past skip te ts tb t0 tab "
                 "w_hi w_lo az xT_ps x_hi x_lo gu silu acts aT_ps aT y_ps y di")
        rec_s = [sem(f"e_rec{u}") for u in range(NB)]
        sent = [sem(f"e_sent{u}") for u in range(NB)]

        def steps(eng, step, last):
            for s in range(NB):
                step(s, 0, s)
            with eng.Fori(1, NT // NB) as i:
                for u in range(NB):
                    step(i * NB + u, i, u)
            for s in range(NT, NT + last):
                step(s, s // NB, s % NB)

        def tile_at(s, i, u, lag):
            if isinstance(s, int) and not 0 <= s - lag < NT:
                return None
            return s - lag, (i if u >= lag else i - 1), (u - lag) % NB

        xT_ps = q_ps
        aT_ps = m_ps
        y_ps = k_ps
        with nc.Block() as block:
            @block.sync
            def _(sp):
                sp.wait_ge(E["tab"], 2)
                sp.wait_ge(E["fill"], NE * 16)

                def step(s, i, u):
                    row = sp.value_load(ti[0:1, bass.ds(s, 1)], min_val=0, max_val=BLANK)
                    wait(sp, E["y"], s - NB + 1)
                    wait(sp, E["di"], s - NB + 1)
                    sp.dma_start(rec[:, u, :], lists[bass.ds(row, P), :]).then_inc(rec_s[u], 16)
                steps(sp, step, 0)

            @block.gpsimd
            def _(pool):
                pool.iota(tile_i[:, :], pattern=[[1, NT]], base=0, channel_multiplier=0,
                          allow_small_or_imprecise_dtypes=True).then_inc(E["iota"], 1)
                pool.iota(part_i[:, :], pattern=[[0, 1]], base=0, channel_multiplier=1,
                          allow_small_or_imprecise_dtypes=True).then_inc(E["iota"], 1)
                pool.wait_ge(E["lanei"], 1)
                for e in range(NE):
                    pool.indirect_dma_start(lists, bass.IndirectOffsetOnAxis(ap=lane_i[:, e:e + 1], axis=0),
                                            blank[:, :], None, bounds_check=BLANK - 1,
                                            oob_is_err=False).then_inc(E["fill"], 16)

                def step(s, i, u):
                    pool.wait_ge(E["y"], s + 1)
                    pool.wait_ge(E["di"], s + 1)
                    settle(pool)
                    pool.indirect_dma_start(places, bass.IndirectOffsetOnAxis(ap=desti[:, u:u + 1], axis=0),
                                            yrow[:, u, :], None, bounds_check=TOPK * NTOK - 1,
                                            oob_is_err=False).then_inc(sent[u], 16)
                steps(pool, step, 0)
                for u in range(NB):
                    pool.wait_ge(sent[u], NT // NB * 16)

            @block.scalar
            def _(act):
                act.wait_ge(S["gu"], 32)
                for e in range(NE):
                    act.activation(w_hi[:, e, :], w_lo[:, e, :].bitcast(F32), ACT.Copy).then_inc(E["w_hi"], 1)

                def step(s, i, u):
                    if at := tile_at(s, i, u, 0):
                        n = at[0]
                        act.wait_ge(E["xT_ps"], n + 1)
                        wait(act, E["gu"], n - 1)
                        act.activation(x_hi[:, u % 2, :], xT_ps[:, 0:P], ACT.Copy).then_inc(E["x_hi"], 1)
                    if at := tile_at(s, i, u, 1):
                        n, _, v = at
                        act.wait_ge(E["gu"], n + 1)
                        wait(act, E["acts"], n - 1)
                        act.activation(silu[:, v % 2, :], s_ps[:, 2 * (v % 2), 0:F],
                                       ACT.Silu).then_inc(E["silu"], 1)
                    if at := tile_at(s, i, u, 2):
                        n, _, v = at
                        act.wait_ge(E["aT_ps"], n + 1)
                        wait(act, E["y_ps"], n - 1)
                        act.activation(actsT[:, v % 2, :], aT_ps[:, 0:FP], ACT.Copy).then_inc(E["aT"], 1)
                steps(act, step, 2)

            @block.vector
            def _(dve):
                dve.memset(acts[:, :, F:FP], 0.0).then_inc(E["az"], 1)
                dve.wait_ge(E["iota"], 2)
                dve.tensor_scalar(lane_e[:, :], cnt[:, :], part_i[:, :], None, ALU.add).then_inc(E["lane"], 1)
                dve.wait_ge(E["lane"], 1)
                dve.tensor_copy(lane_i[:, :], lane_e[:, :]).then_inc(E["lanei"], 1)
                dve.scalar_tensor_tensor(out=used[:, :], in0=cnt[:, :], scalar=float(P - 1), in1=base_e[:, :],
                                         op0=ALU.add, op1=ALU.subtract).then_inc(E["used"], 1)
                dve.wait_ge(E["used"], 1)
                dve.tensor_copy(usedi[:, :], used[:, :]).then_inc(E["usedi"], 1)
                dve.wait_ge(E["usedi"], 1)
                dve.tensor_single_scalar(tilesi[:, :], usedi[:, :], 7, ALU.arith_shift_right).then_inc(E["tilesi"], 1)
                dve.wait_ge(E["tilesi"], 1)
                dve.tensor_copy(tiles[:, :], tilesi[:, :]).then_inc(E["tiles"], 1)
                dve.wait_ge(E["tiles"], 1)
                dve.tensor_tensor_scan(ends[:, :], tiles[:, :], tiles[:, :], 0.0, ALU.add,
                                       ALU.bypass).then_inc(E["ends"], 1)
                dve.wait_ge(E["ends"], 1)
                dve.tensor_tensor(past[:, :, :], tile_i[:, :].unsqueeze(2).broadcast_to([P, NT, NE]),
                                  ends[:, :].unsqueeze(1).broadcast_to([P, NT, NE]), ALU.is_ge).then_inc(E["past"], 1)
                dve.wait_ge(E["past"], 1)
                dve.tensor_tensor(skip[:, :, :], past[:, :, :],
                                  tiles[:, :].unsqueeze(1).broadcast_to([P, NT, NE]), ALU.mult).then_inc(E["skip"], 1)
                dve.tensor_reduce(te[:, :], past[:, :, :], AX.X, ALU.add).then_inc(E["te"], 1)
                dve.wait_ge(E["skip"], 1)
                dve.tensor_reduce(ts_[:, :], skip[:, :, :], AX.X, ALU.add).then_inc(E["ts"], 1)
                dve.wait_ge(E["ts"], 1)
                dve.wait_ge(E["te"], 1)
                dve.tensor_tensor(tb[:, :], tile_i[:, :], ts_[:, :], ALU.subtract).then_inc(E["tb"], 1)
                dve.tensor_scalar(t0[:, :], te[:, :], float(CAP), None, ALU.mult).then_inc(E["t0"], 1)
                dve.wait_ge(E["tb"], 1)
                dve.wait_ge(E["t0"], 1)
                dve.scalar_tensor_tensor(out=tb[:, :], in0=tb[:, :], scalar=float(P), in1=t0[:, :], op0=ALU.mult,
                                         op1=ALU.add).then_inc(E["tb"], 1)
                dve.wait_ge(E["tb"], 2)
                dve.tensor_scalar(ti[:, :], tb[:, :], float(BLANK), None, ALU.min).then_inc(E["tab"], 1)
                dve.tensor_scalar(tw[:, :], te[:, :], float(NE - 1), None, ALU.min).then_inc(E["tab"], 1)
                dve.wait_ge(S["gu"], 32)
                for e in range(NE):
                    dve.wait_ge(E["w_hi"], e + 1)
                    dve.tensor_tensor(w_lo[:, e, :], w_lo[:, e, :].bitcast(F32), w_hi[:, e, :],
                                      ALU.subtract).then_inc(E["w_lo"], 1)
                dve.wait_ge(E["az"], 1)

                def step(s, i, u):
                    if at := tile_at(s, i, u, 0):
                        n = at[0]
                        wait(dve, sent[u], i * 16)
                        dve.wait_ge(E["x_hi"], n + 1)
                        wait(dve, E["gu"], n - 1)
                        dve.tensor_tensor(x_lo[:, u % 2, :], xT_ps[:, 0:P], x_hi[:, u % 2, :],
                                          ALU.subtract).then_inc(E["x_lo"], 1)
                    if at := tile_at(s, i, u, 1):
                        n, _, v = at
                        dve.wait_ge(E["silu"], n + 1)
                        wait(dve, E["aT_ps"], n - 1)
                        dve.tensor_tensor(acts[:, v % 2, 0:F], silu[:, v % 2, :], s_ps[:, 2 * (v % 2) + 1, 0:F],
                                          ALU.mult).then_inc(E["acts"], 1)
                    if at := tile_at(s, i, u, 3):
                        n, _, v = at
                        dve.wait_ge(E["y_ps"], n + 1)
                        dve.tensor_copy(desti[:, v:v + 1], rec[:, v, D:REC]).then_inc(E["di"], 1)
                        dve.tensor_copy(yrow[:, v, :], y_ps[:, 0:D]).then_inc(E["y"], 1)
                steps(dve, step, 3)

            @block.tensor
            def _(pe):
                def step(s, i, u):
                    if at := tile_at(s, i, u, 0):
                        n, r, _ = at
                        pe.wait_ge(rec_s[u], (r + 1) * 16)
                        wait(pe, E["x_lo"], n)
                        pe.transpose(xT_ps[:, 0:P], rec[:, u, 0:D], ident[:, :]).then_inc(E["xT_ps"], 1)
                    if at := tile_at(s, i, u, 1):
                        n, _, v = at
                        e = pe.value_load(tw[0:1, bass.ds(n, 1)], min_val=0, max_val=NE - 1)
                        pe.wait_ge(E["x_lo"], n + 1)
                        wait(pe, E["acts"], n - 1)
                        for k, (xs, ws) in enumerate(((x_hi, w_hi), (x_hi, w_lo), (x_lo, w_hi))):
                            for a in range(2):
                                mmi = pe.matmul(s_ps[:, 2 * (v % 2) + a, 0:F], xs[:, v % 2, :],
                                                ws[:, bass.ds(e, 1), a * F:(a + 1) * F].rearrange("p a f -> p (a f)"),
                                                start=(k == 0), stop=(k == 2))
                        mmi.then_inc(E["gu"], 1)
                    if at := tile_at(s, i, u, 2):
                        n, _, v = at
                        pe.wait_ge(E["acts"], n + 1)
                        wait(pe, E["aT"], n)
                        for c in range(FC):
                            mmi = pe.transpose(aT_ps[:, c * P:(c + 1) * P], acts[:, v % 2, c * P:(c + 1) * P],
                                               ident[:, :])
                        mmi.then_inc(E["aT_ps"], 1)
                    if at := tile_at(s, i, u, 3):
                        n, _, v = at
                        e = pe.value_load(tw[0:1, bass.ds(n, 1)], min_val=0, max_val=NE - 1)
                        pe.wait_ge(E["aT"], n + 1)
                        wait(pe, E["y"], n)
                        for c in range(FC):
                            mmi = pe.matmul(y_ps[:, 0:D], actsT[:, v % 2, c * P:(c + 1) * P],
                                            wd_sb[:, bass.ds(e, 1), c, :].rearrange("p a d -> p (a d)"),
                                            start=(c == 0), stop=(c == FC - 1))
                        mmi.then_inc(E["y_ps"], 1)

                pe.wait_ge(E["tab"], 2)
                pe.wait_ge(E["w_lo"], NE)
                pe.wait_ge(S["wd"], FC * 16)
                steps(pe, step, 3)

        C = sems("c_", "ed e1 w1 w2 wg1 wg2 s out")
        NCH = 4
        CT = TT // NCH
        got = [sem(f"c_got{c}") for c in range(NCH)]
        ed = sb("ed", [P, TT])
        e1 = sb("e1", [P, TT])
        w1 = sb("w1", [P, TT])
        w2 = sb("w2", [P, TT])
        wg = sb("wg", [P, TOPK, TT])
        y0 = x_sb
        y1 = xnT[:, :].rearrange("p (t d) -> p t d", t=TT)
        with nc.Block() as block:
            @block.sync
            def _(sp):
                for c in range(NCH):
                    for k, dst in enumerate((y0, y1)):
                        r = k * NTOK + c * CT * P
                        sp.dma_start(dst[:, c * CT:(c + 1) * CT, :],
                                     places[r:r + CT * P, :].rearrange("(t p) d -> p t d", p=P)).then_inc(got[c], 16)
                for c in range(NCH):
                    sp.wait_ge(C["s"], TOPK * CT * (c + 1))
                    sp.dma_start(out[c * CT * P:(c + 1) * CT * P, :].rearrange("(t p) d -> p t d", p=P),
                                 xn[:, c * CT:(c + 1) * CT, :]).then_inc(C["out"], 16)
                sp.wait_ge(C["out"], NCH * 16)

            @block.scalar
            def _(act):
                act.activation(ed[:, :], gap[:, :], ACT.Exp).then_inc(C["ed"], 1)

            @block.vector
            def _(dve):
                dve.wait_ge(C["ed"], 1)
                dve.tensor_scalar(e1[:, :], ed[:, :], 1.0, None, ALU.add).then_inc(C["e1"], 1)
                dve.wait_ge(C["e1"], 1)
                dve.reciprocal(w1[:, :], e1[:, :]).then_inc(C["w1"], 1)
                dve.wait_ge(C["w1"], 1)
                dve.tensor_tensor(w2[:, :], w1[:, :], ed[:, :], ALU.mult).then_inc(C["w2"], 1)
                dve.tensor_scalar(wg[:, 0, :], w1[:, :], tg[:, 1:2], None, ALU.mult).then_inc(C["wg1"], 1)
                dve.wait_ge(C["w2"], 1)
                dve.tensor_scalar(wg[:, 1, :], w2[:, :], tg[:, 1:2], None, ALU.mult).then_inc(C["wg2"], 1)
                dve.wait_ge(C["wg1"], 1)
                dve.wait_ge(C["wg2"], 1)
                n = 0
                for c in range(NCH):
                    dve.wait_ge(got[c], 32)
                    for k, y in enumerate((y0, y1)):
                        if k:
                            dve.wait_ge(C["s"], n)
                        for t in range(c * CT, (c + 1) * CT):
                            dve.scalar_tensor_tensor(out=xn[:, t, :], in0=y[:, t, :], scalar=wg[:, k, t:t + 1],
                                                     in1=xn[:, t, :], op0=ALU.mult, op1=ALU.add).then_inc(C["s"], 1)
                            n += 1


def kernel(x, ctx_1024, mask_Bx1xS2_ik0, g_xattn, g_ffn, L0_xattn_Wq, L0_xattn_bq, L0_xattn_Wk, L0_xattn_bk,
           L0_xattn_Wv, L0_xattn_bv, L0_xattn_Wo, L0_xattn_bo, L0_ffn_router_w, L0_ffn_gate_proj,
           L0_ffn_up_proj, L0_ffn_down_proj):
    import numpy as np
    import concourse.bacc as bacc
    from concourse.bass_utils import run_bass_kernel_spmd

    def thrice(w):
        w = np.asarray(w).reshape(-1, BL, G, DH)
        o = np.zeros((w.shape[0], BL, G, GR), w.dtype)
        for c in range(3):
            o[..., c * DH:(c + 1) * DH] = w
        return o.reshape(w.shape[0], BL, P)

    def columns(b, one):
        o = thrice(b).reshape(BL, G, GR)
        o[..., MASK_ROW] = one
        return np.ascontiguousarray(o.reshape(BL, P).T)

    heads = (BL, G, DH)
    arrays = {
        "x": np.asarray(x).reshape(NTOK, D),
        "ctxT": np.ascontiguousarray(np.asarray(ctx_1024).transpose(0, 2, 1)).reshape(B * D, SK),
        "mask": np.ascontiguousarray(np.asarray(mask_Bx1xS2_ik0).reshape(B, KT, P).transpose(2, 0, 1)).reshape(P, B * KT),
        "wq": thrice(L0_xattn_Wq), "bq": columns(L0_xattn_bq, 1),
        "wk": thrice(L0_xattn_Wk), "bk": columns(L0_xattn_bk, 0),
        "wv": np.asarray(L0_xattn_Wv),
        "bv": np.ascontiguousarray(np.asarray(L0_xattn_bv).reshape(heads).transpose(1, 0, 2)).reshape(P, 1),
        "wo": np.ascontiguousarray(np.asarray(L0_xattn_Wo).reshape(*heads, D).transpose(1, 0, 2, 3)).reshape(P, D),
        "bo": np.asarray(L0_xattn_bo),
        "g": np.concatenate([np.asarray(g_xattn), np.asarray(g_ffn)]),
        "wr": np.asarray(L0_ffn_router_w),
        "wgate": np.asarray(L0_ffn_gate_proj), "wup": np.asarray(L0_ffn_up_proj),
        "wdown": np.asarray(L0_ffn_down_proj),
    }
    nc = bacc.Bacc("TRN2", target_bir_lowering=False, num_devices=1)
    aps = {k: nc.dram_tensor("in_" + k, a.shape, mybir.dt.from_np(a.dtype), kind="ExternalInput").ap()
           for k, a in arrays.items()}
    aps["out"] = nc.dram_tensor("out_x", (NTOK, D), F32, kind="ExternalOutput").ap()
    build(nc, **aps)
    r = run_bass_kernel_spmd(nc, [{"in_" + k: a for k, a in arrays.items()}], core_ids=[0])
    return r.results[0]["out_x"].reshape(B, SQ, D)
```

```python
from contextlib import ExitStack

import concourse.bass as bass
from concourse import mybir

F32 = mybir.dt.float32
F32R = mybir.dt.float32r
BF16 = mybir.dt.bfloat16
I32 = mybir.dt.int32
U32 = mybir.dt.uint32
ALU = mybir.AluOpType
ACT = mybir.ActivationFunctionType
AX = mybir.AxisListType

P = 128
D = 128
B, SQ, SK = 8, 256, 512
H, DH = 16, 8
G = 4
BL = H // G
GR = P // G
QT = SQ // P
KT = SK // P
NTOK = B * SQ
TT = NTOK // P
MASK_ROW = 3 * DH
VSTEP = G * GR + DH
DSTEP = GR + DH
BD = 2 * (BL * G * SQ + BL * G * P)
MASKED = -1.0e30
SCALE = float(DH) ** -0.5
EPS = 1e-5

NE, TOPK, F = 8, 2, 352
FC = -(-F // P)
FP = FC * P
REC = D + 1
CAP = NTOK + P
BLANK = NE * CAP
NOWHERE = 2 * TOPK * NTOK
BIG = 3.0e38


def wait(eng, sem, value):
    if isinstance(value, int) and value <= 0:
        return
    eng.wait_ge(sem, value)


def build(nc, x, ctxT, mask, wq, bq, wk, bk, wv, bv, wo, bo, g, wr, wgate, wup, wdown, out):
    ctx = ExitStack()
    with ctx:
        def sb(name, shape, dt=F32):
            return ctx.enter_context(nc.sbuf_tensor(name, shape, dt))

        def pb(name, shape):
            return ctx.enter_context(nc.psum_tensor(name, shape, F32))

        def sem(name):
            return ctx.enter_context(nc.semaphore(name))

        def sems(prefix, names):
            return {k: sem(prefix + k) for k in names.split()}

        lists = nc.dram_tensor("lists", (BLANK + P, REC), F32).ap()
        places = nc.dram_tensor("places", (TOPK * NTOK, D), F32).ap()

        x_sb = sb("x_sb", [P, TT, D])
        xn = sb("xn", [P, TT, D])
        xnT = sb("xnT", [P, NTOK])
        ident = sb("ident", [P, P])
        before = sb("before", [P, P], BF16)
        ones = sb("ones", [P, P], BF16)
        wq_sb = sb("wq_sb", [P, BL, P])
        wk_sb = sb("wk_sb", [P, BL, P])
        wv_sb = sb("wv_sb", [P, D])
        wo_sb = sb("wo_sb", [P, D])
        bq_sb = sb("bq_sb", [P, BL])
        bk_sb = sb("bk_sb", [P, BL])
        bv_sb = sb("bv_sb", [P, 1])
        bo_sb = sb("bo_sb", [P, D])
        wr_sb = sb("wr_sb", [P, NE])
        tg_in = sb("tg_in", [P, 2])
        tg = sb("tg", [P, 2])
        w_hi = sb("w_hi", [P, NE, 2 * F], F32R)
        w_lo = sb("w_lo", [P, NE, 2 * F], F32R)
        wd_sb = sb("wd_sb", [P, NE, FC, D])
        lows = sb("lows", [P, 2])
        split_q = sb("split_q", [P, 1])
        split_k = sb("split_k", [P, 1])
        sel = sb("sel", [P, H, P], F32R)
        selw = sb("selw", [P, H])
        halves = sb("halves", [P, TT])
        stats = sb("stats", [P, TT, 6])
        mv = sb("mv", [P, TT, 2])
        rstd = sb("rstd", [P, TT])
        varp = sb("varp", [P, TT])
        mask_in = sb("mask_in", [P, B, KT], I32)
        keep = sb("keep", [P, B, KT])
        early = sb("early", [P, 1])
        early_row = sb("early_row", [1, P])
        early_n = sb("early_n", [1, 1], I32)
        iota_e = sb("iota_e", [P, NE])
        base_e = sb("base_e", [P, NE])
        dest = sb("dest", [P, QT, TOPK])
        blank = sb("blank", [P, REC])

        FT = TOPK * NTOK // P
        NT = FT + NE
        NB = 8
        tile_i = sb("tile_i", [P, FT])
        part_i = sb("part_i", [P, 1])
        lane_e = sb("lane_e", [P, NE])
        lane_i = sb("lane_i", [P, NE], U32)
        used = sb("used", [P, NE])
        usedi = sb("usedi", [P, NE], I32)
        tilesi = sb("tilesi", [P, NE], I32)
        tiles = sb("tiles", [P, NE])
        ends = sb("ends", [P, NE])
        te = sb("te", [P, FT])
        ts_ = sb("ts_", [P, FT])
        tb = sb("tb", [P, FT])
        ti = sb("ti", [P, NT], I32)
        tw = sb("tw", [P, NT], I32)
        t0 = sb("t0", [P, FT])

        attention_memory = ctx.enter_context(ExitStack())

        def att(name, shape, dt=F32):
            return attention_memory.enter_context(nc.sbuf_tensor(name, shape, dt))

        cnt = sb("cnt", [P, NE])
        gap = sb("gap", [P, TT])
        arena_r = att("arena_r", [P, 15360], F32R)
        arena = att("arena", [P, 3400])
        mrows = att("mrows", [P, KT, P])
        q_t = att("q_t", [P, BL, SQ])
        q_hi = att("q_hi", [P, BL, SQ], F32R)
        k_new = att("k_new", [P, BL, P], F32R)
        k_t = att("k_t", [P, BL, P])
        k_hi = att("k_hi", [P, BL, P], F32R)
        mraw = att("mraw", [P, KT, QT, H])
        mall = att("mall", [P, QT, H])
        mhi = att("mhi", [P, QT, H], F32R)
        mm = att("mm", [P, QT, P])
        mT = att("mT", [P, SQ], F32R)
        pt = att("pt", [P, 2, G * SQ])
        rden = att("rden", [P, SQ])
        ot0 = att("ot0", [P, SQ])
        oT = att("oT", [P, SQ])
        q_flat = q_t[:, :, :].rearrange("p j q -> p (j q)")
        past = q_flat[:, 0:FT * NE].rearrange("p (t e) -> p t e", e=NE)
        skip = q_flat[:, FT * NE:2 * FT * NE].rearrange("p (t e) -> p t e", e=NE)
        stats2 = att("stats2", [P, QT, 6])
        mv2 = att("mv2", [P, QT, 2])
        var2 = att("var2", [P, QT])
        rstd2 = att("rstd2", [P, QT])
        hrec = att("hrec", [P, 2, QT, TOPK, REC])
        hT = att("hT", [P, SQ])
        logit = att("logit", [P, QT, NE])
        top = att("top", [P, QT, NE])
        topi = att("topi", [P, QT, NE], U32)
        topf = att("topf", [P, QT, TOPK])
        hot = att("hot", [P, QT, TOPK, NE])
        selb = att("selb", [P, QT, NE], BF16)
        pos = att("pos", [P, QT, NE])
        prod = att("prod", [P, QT, TOPK, NE])
        rowf = att("rowf", [P, QT, TOPK])
        rowi = att("rowi", [P, 2, QT, TOPK], U32)

        s_ps = pb("s_ps", [P, 4, 512])
        pv_ps = pb("pv_ps", [P, 512])
        k_ps = pb("k_ps", [P, 512])
        q_ps = pb("q_ps", [P, 512])
        m_ps = pb("m_ps", [P, 512])
        s1_ps = s_ps[:, 0:2, :]
        s2_ps = s_ps[:, 2:4, :].rearrange("p a b -> p (a b)")

        S = sems("a_", "x mask w g wd wr halves rows ident ident_d tri ones blank st mv var rs ln "
                 "xT_ps xT tg keep early early_ps early_n lows split selw sel gu zero iota base wdz")
        with nc.Block() as block:
            @block.sync
            def _(sp):
                sp.dma_start(mask_in[:, :, :], mask.rearrange("p (b t) -> p b t", b=B)).then_inc(S["mask"], 16)
                sp.dma_start(x_sb[:, :, :], x.rearrange("(t p) d -> p t d", p=P)).then_inc(S["x"], 16)
                sp.dma_start(wq_sb[:, :, :], wq).then_inc(S["w"], 16)
                sp.dma_start(wk_sb[:, :, :], wk).then_inc(S["w"], 16)
                sp.dma_start(wv_sb[:, :], wv).then_inc(S["w"], 16)
                sp.dma_start(wo_sb[:, :], wo).then_inc(S["w"], 16)
                sp.dma_start(bq_sb[:, :], bq).then_inc(S["w"], 16)
                sp.dma_start(bk_sb[:, :], bk).then_inc(S["w"], 16)
                sp.dma_start(bv_sb[:, :], bv).then_inc(S["w"], 16)
                sp.dma_start(wr_sb[:, :], wr).then_inc(S["w"], 16)
                sp.dma_start(bo_sb[:, :], bo.partition_broadcast(P)).then_inc(S["g"], 16)
                sp.dma_start(tg_in[:, :], g.partition_broadcast(P)).then_inc(S["g"], 16)
                sp.wait_ge(S["wdz"], 1)
                for a, w in enumerate((wgate, wup)):
                    sp.dma_start(w_lo[:, :, a * F:(a + 1) * F].bitcast(F32),
                                 w.rearrange("e p f -> p e f")).then_inc(S["gu"], 16)
                for c in range(FC):
                    n = min(P, F - c * P)
                    sp.dma_start(wd_sb[0:n, :, c, :],
                                 wdown[:, c * P:c * P + n, :].rearrange("e p d -> p e d")).then_inc(S["wd"], 16)

            @block.gpsimd
            def _(pool):
                pool.memset(halves[:, :], -0.5).then_inc(S["halves"], 1)
                pool.memset(ident[:, :], 0.0).then_inc(S["ident"], 1)
                pool.memset(before[:, :], 1.0).then_inc(S["ones"], 1)
                pool.memset(ones[:, :], 1.0).then_inc(S["ones"], 1)
                pool.memset(blank[:, 0:D], 0.0).then_inc(S["blank"], 1)
                pool.memset(blank[:, D:REC], float(NOWHERE)).then_inc(S["blank"], 1)
                pool.wait_ge(S["ident"], 1)
                pool.affine_select(out=ident[:, :], in_=ident[:, :], compare_op=ALU.not_equal, fill=1.0, base=0,
                                   pattern=[[-1, P]], channel_multiplier=1).then_inc(S["ident_d"], 1)
                pool.wait_ge(S["ones"], 2)
                pool.affine_select(out=before[:, :], in_=before[:, :], compare_op=ALU.is_ge, fill=0.0, base=-1,
                                   pattern=[[1, P]], channel_multiplier=-1).then_inc(S["tri"], 1)
                pool.iota(iota_e[:, :], pattern=[[1, NE]], base=0, channel_multiplier=0,
                          allow_small_or_imprecise_dtypes=True).then_inc(S["base"], 1)
                pool.iota(base_e[:, :], pattern=[[CAP, NE]], base=0, channel_multiplier=0,
                          allow_small_or_imprecise_dtypes=True).then_inc(S["base"], 1)
                pool.iota(cnt[:, :], pattern=[[CAP, NE]], base=0, channel_multiplier=0,
                          allow_small_or_imprecise_dtypes=True).then_inc(S["base"], 1)
                pool.iota(dest[:, :, :], pattern=[[P, QT], [NTOK, TOPK]], base=0, channel_multiplier=1,
                          allow_small_or_imprecise_dtypes=True).then_inc(S["base"], 1)
                pool.iota(tile_i[:, :], pattern=[[1, FT]], base=0, channel_multiplier=0,
                          allow_small_or_imprecise_dtypes=True).then_inc(S["iota"], 1)
                pool.iota(part_i[:, :], pattern=[[0, 1]], base=0, channel_multiplier=1,
                          allow_small_or_imprecise_dtypes=True).then_inc(S["iota"], 1)
                pool.memset(arena_r[:, 0:3 * BD // 4].bitcast(F32), 0.0).then_inc(S["zero"], 1)
                pool.wait_ge(S["halves"], 1)
                pool.wait_ge(S["var"], 1)
                pool.tensor_tensor(rstd[:, :], varp[:, :], halves[:, :], ALU.pow).then_inc(S["rs"], 1)
                pool.memset(arena_r[:, 3 * BD // 4:BD].bitcast(F32), 0.0).then_inc(S["zero"], 1)
                pool.memset(mrows[:, :, :], 0.0).then_inc(S["zero"], 1)
                pool.wait_ge(S["blank"], 2)
                pool.dma_start(lists[BLANK:BLANK + P, :], blank[:, :]).then_inc(S["wr"], 16)
                pool.wait_ge(S["wr"], 16)

            @block.scalar
            def _(act):
                act.wait_ge(S["g"], 32)
                act.activation(tg[:, :], tg_in[:, :], ACT.Tanh).then_inc(S["tg"], 1)
                for c in range(NTOK // 512):
                    act.wait_ge(S["xT_ps"], c + 1)
                    act.activation(xnT[:, c * 512:(c + 1) * 512], s_ps[:, c, :], ACT.Copy).then_inc(S["xT"], 1)

            @block.vector
            def _(dve):
                dve.memset(wd_sb[F - (FC - 1) * P:P, :, FC - 1, :], 0.0).then_inc(S["wdz"], 1)
                dve.memset(mm[:, :, :], 0.0)
                dve.memset(arena[:, :], 0.0).then_inc(S["zero"], 1)
                dve.wait_ge(S["mask"], 16)
                dve.tensor_scalar(keep[:, :, :], mask_in[:, :, :], 0.0, None, ALU.not_equal).then_inc(S["keep"], 1)
                dve.wait_ge(S["keep"], 1)
                dve.tensor_reduce(early[:, :], keep[:, :, 0:KT - 1], AX.XY, ALU.max).then_inc(S["early"], 1)
                dve.wait_ge(S["x"], 16)
                for t in range(TT):
                    dve.bn_stats(stats[:, t, :], x_sb[:, t, :]).then_inc(S["st"], 1)
                for t in range(TT):
                    dve.wait_ge(S["st"], t + 1)
                    dve.bn_aggr(mv[:, t, :], stats[:, t, :]).then_inc(S["mv"], 1)
                dve.wait_ge(S["mv"], TT)
                dve.tensor_scalar(varp[:, :], mv[:, :, 1], EPS, None, ALU.add).then_inc(S["var"], 1)
                dve.wait_ge(S["ident_d"], 1)
                iv = ident[:, :].rearrange("p (g r) -> p g r", g=G)
                dve.tensor_reduce(lows[:, 0:1], iv[:, :, 2 * DH:3 * DH], AX.XY, ALU.add).then_inc(S["lows"], 1)
                dve.tensor_reduce(lows[:, 1:2], iv[:, :, DH:2 * DH], AX.XY, ALU.add).then_inc(S["lows"], 1)
                dve.tensor_tensor(selw[:, :], ident[:, 0:H], ident[:, H:2 * H], ALU.add).then_inc(S["selw"], 1)
                dve.wait_ge(S["lows"], 2)
                dve.tensor_scalar(split_q[:, :], lows[:, 0:1], -1.0, None, ALU.mult).then_inc(S["split"], 1)
                dve.tensor_scalar(split_k[:, :], lows[:, 1:2], -1.0, None, ALU.mult).then_inc(S["split"], 1)
                dve.wait_ge(S["selw"], 1)
                dve.tensor_copy(sel[:, :, :], selw[:, :].unsqueeze(2).broadcast_to([P, H, P])).then_inc(S["sel"], 1)
                dve.wait_ge(S["early_ps"], 1)
                dve.tensor_reduce(early_n[:, :], m_ps[0:1, 0:P], AX.X, ALU.max).then_inc(S["early_n"], 1)
                dve.wait_ge(S["rs"], 1)
                for t in range(TT):
                    dve.tensor_scalar(xn[:, t, :], x_sb[:, t, :], mv[:, t, 0:1], rstd[:, t:t + 1],
                                      ALU.subtract, ALU.mult).then_inc(S["ln"], 1)

            @block.tensor
            def _(pe):
                pe.wait_ge(S["ident_d"], 1)
                pe.wait_ge(S["early"], 1)
                pe.transpose(m_ps[0:1, 0:P], early[:, :], ident[:, :]).then_inc(S["early_ps"], 1)
                for t in range(TT):
                    pe.wait_ge(S["ln"], t + 1)
                    tr = pe.transpose(s_ps[:, t // 4, (t % 4) * P:(t % 4 + 1) * P], xn[:, t, :], ident[:, :])
                    if t % 4 == 3:
                        tr.then_inc(S["xT_ps"], 1)

        settled = sem("settled")

        def settle(eng):
            eng.sem_inc(settled, 1)

        T = sems("b_", "xb q_ps q_ev q_hi q_spl k_ps k_ev k_hi k_spl mrow v_ps v_ev dn s1 mx mall mhi mlo mm "
                 "mT_ps mT s2 ex pv rden ot oT y x2 r_st r_mv r_var r_rs r_h r_hd r_dest r_hT_ps r_hT r_lg_ps "
                 "r_lg r_top r_ti r_tf r_hot r_sel r_gap r_rk_ps r_pos r_prod r_row r_cnt r_rowi w_hi w_lo")
        r_sent = [sem(f"b_sent{u}") for u in range(2)]
        ctx_s = [sem(f"b_ctx{u}") for u in range(2)]
        q_bd = [sem(f"b_qbd{u}") for u in range(2)]
        k_bd = [sem(f"b_kbd{u}") for u in range(2)]
        k_cp = [sem(f"b_kcp{u}") for u in range(2)]

        def attention(nt, depth):
            def part(tensor, at, shape):
                size = 1
                for s in shape:
                    size *= s
                v = tensor[:, at[0]:at[0] + size]
                at[0] += size
                letters = "abcde"[:len(shape)]
                if len(shape) > 1:
                    v = v.rearrange(f"p ({' '.join(letters)}) -> p {' '.join(letters)}",
                                    **{k: s for k, s in zip(letters[:-1], shape[:-1])})
                return v

            at = [0]
            qbd = part(arena_r, at, (depth, BL, G, SQ))
            kbd = part(arena_r, at, (2, BL, G, P))
            assert at[0] <= BD
            qd = part(arena_r, at, (depth, BL, SQ))
            kd = part(arena_r, at, (depth, nt, BL, P))
            assert at[0] <= arena_r.shape[1]
            at = [0]
            ctx_in = part(arena, at, (depth, nt * P))
            vn = part(arena, at, (depth, nt, BL * VSTEP))
            dn = part(arena, at, (depth, nt, BL * DSTEP))
            mrow = mrows[:, 0:depth * nt, :].rearrange("p (u n) k -> p u n k", u=depth)
            assert at[0] <= arena.shape[1]

            U = BL * nt

            def drive(eng, general, iteration):
                if depth == 1:
                    general((0, 0, 0))
                    with eng.Fori(1, B) as n:
                        general((n, n, 0))
                    return

                def row(n, i, u, off):
                    if isinstance(n, int) and not 0 <= n + off < B:
                        return None
                    return n + off, i + (u + off) // 2, (u + off) % 2

                def run(n, i, u):
                    iteration(lambda off, work, *a: row(n, i, u, off) and work(row(n, i, u, off), *a),
                              isinstance(n, int) and n == -2)

                for n in range(-2, 2):
                    run(n, n // 2, n % 2)
                with eng.Fori(1, B // 2 - 1) as i:
                    run(i * 2, i, 0)
                    run(i * 2 + 1, i, 1)
                for n in range(B - 2, B + 2):
                    run(n, n // 2, n % 2)

            def kbuf(u, kt):
                return u if nt == 1 else kt % 2

            def k_uses(at, kt):
                n, i, u = at
                return i + 1 if nt == 1 else n * (nt // 2) + (kt // 2 + 1)

            def sync_(sp):
                def load(at):
                    n, i, u = at
                    wait(sp, T["v_ps"], nt * (n - depth + 1))
                    sp.dma_start(ctx_in[:, u, :],
                                 ctxT[bass.ds(n * P, P), (KT - nt) * P:KT * P]).then_inc(ctx_s[u], 16)

                def k_groups(at, kt):
                    n, i, u = at
                    m = n * nt + kt
                    kb = kbuf(u, kt)
                    wait(sp, T["k_spl"], m + 1)
                    settle(sp)
                    wait(sp, T["s1"], BL * (m - 1))
                    for gr in range(G):
                        r = slice(gr * GR, (gr + 1) * GR)
                        sp.dma_start(kbd[r, kb, :, gr, :].bitcast(F32),
                                     k_new[r, :, :].bitcast(F32)).then_inc(k_bd[kb], 16)

                def k_copy(at, kt):
                    n, i, u = at
                    wait(sp, T["s2"], U * (n - depth + 1))
                    settle(sp)
                    sp.dma_start(kd[:, u, kt, :, :].bitcast(F32), k_new[:, :, :].bitcast(F32)).then_inc(k_cp[u], 16)

                def q_groups(at):
                    n, i, u = at
                    wait(sp, T["q_spl"], n + 1)
                    settle(sp)
                    wait(sp, T["s2"], U * (n - depth + 1))
                    for gr in range(G):
                        r = slice(gr * GR, (gr + 1) * GR)
                        sp.dma_start(qbd[r, u, :, gr, :].bitcast(F32),
                                     qd[r, u, :, :].bitcast(F32)).then_inc(q_bd[u], 16)

                def general(at):
                    load(at)
                    for kt in range(nt):
                        k_groups(at, kt)
                        k_copy(at, kt)
                    q_groups(at)

                def iteration(on, first):
                    on(2, load)
                    on(2, k_groups, 0)
                    on(2, k_copy, 0)
                    on(2, q_groups)

                drive(sp, general, iteration)
                for u in range(depth):
                    sp.wait_ge(r_sent[u], B // depth * QT * TOPK * 16)

            def gpsimd_(pool):
                def deviations(at):
                    pool.wait_ge(T["r_var"], at[0] + 1)
                    pool.tensor_tensor(rstd2[:, :], var2[:, :], halves[:, 0:QT], ALU.pow).then_inc(T["r_rs"], 1)

                def send(at):
                    n, i, u = at
                    pool.wait_ge(T["r_rowi"], n + 1)
                    pool.wait_ge(T["r_hd"], n + 1)
                    settle(pool)
                    for t in range(QT):
                        for k in range(TOPK):
                            pool.indirect_dma_start(
                                lists, bass.IndirectOffsetOnAxis(ap=rowi[:, u, t, k:k + 1], axis=0),
                                hrec[:, u, t, k, :], None, bounds_check=BLANK - 1,
                                oob_is_err=False).then_inc(r_sent[u], 16)

                def w_low(at):
                    n = at[0]
                    pool.wait_ge(T["w_hi"], n + 1)
                    pool.tensor_tensor(w_lo[:, bass.ds(n, 1), :], w_lo[:, bass.ds(n, 1), :].bitcast(F32),
                                       w_hi[:, bass.ds(n, 1), :].bitcast(F32), ALU.subtract).then_inc(T["w_lo"], 1)

                def general(at):
                    deviations(at)
                    w_low(at)
                    send(at)

                def iteration(on, first):
                    on(-1, deviations)
                    on(-2, send)
                    on(-1, w_low)

                drive(pool, general, iteration)

            def scalar_(act):
                def q_out(at, r):
                    n = at[0]
                    act.wait_ge(T["q_ps"], n * 2 + (r + 1))
                    if r == 0:
                        wait(act, T["q_spl"], n)
                    for j in (2 * r, 2 * r + 1):
                        act.activation(q_t[:, j, :], q_ps[:, (j % 2) * SQ:(j % 2 + 1) * SQ], ACT.Identity,
                                       bias=bq_sb[:, j:j + 1]).then_inc(T["q_ev"], 1)
                    if r == 1:
                        act.wait_ge(T["q_ev"], (n + 1) * BL)
                        act.activation(q_hi[:, :, :], q_t[:, :, :], ACT.Copy).then_inc(T["q_hi"], 1)

                def k_out(at, kt):
                    m = at[0] * nt + kt
                    act.wait_ge(T["k_ps"], m + 1)
                    wait(act, T["k_spl"], m)
                    for j in range(BL):
                        act.activation(k_t[:, j, :], k_ps[:, j * P:(j + 1) * P], ACT.Identity,
                                       bias=bk_sb[:, j:j + 1]).then_inc(T["k_ev"], 1)
                    act.wait_ge(T["k_ev"], (m + 1) * BL)
                    act.activation(k_hi[:, :, :], k_t[:, :, :], ACT.Copy).then_inc(T["k_hi"], 1)

                def mT_out(at):
                    n = at[0]
                    act.wait_ge(T["mT_ps"], n + 1)
                    wait(act, T["s2"], U * n)
                    act.activation(mT[:, :], m_ps[:, 0:SQ], ACT.Copy).then_inc(T["mT"], 1)

                def exps(at, m):
                    n = at[0]
                    act.wait_ge(T["s2"], n * U + (m + 1))
                    wait(act, T["pv"], n * U + (m - 1))
                    act.activation(pt[:, m % 2, :], s2_ps, ACT.Exp, scale=SCALE).then_inc(T["ex"], 1)

                def bias_v(at):
                    n = at[0]
                    act.wait_ge(T["ot"], n + 1)
                    wait(act, T["y"], n)
                    act.activation(oT[:, :], ot0[:, :], ACT.Identity, bias=bv_sb[:, :]).then_inc(T["oT"], 1)

                def hT_out(at):
                    n = at[0]
                    act.wait_ge(T["r_hT_ps"], n + 1)
                    wait(act, T["r_lg_ps"], n)
                    act.activation(hT[:, :], m_ps[:, 0:SQ], ACT.Copy).then_inc(T["r_hT"], 1)

                def w_high(at):
                    act.wait_ge(S["gu"], 32)
                    act.activation(w_hi[:, bass.ds(at[0], 1), :], w_lo[:, bass.ds(at[0], 1), :].bitcast(F32),
                                   ACT.Copy).then_inc(T["w_hi"], 1)

                def general(at):
                    q_out(at, 0)
                    q_out(at, 1)
                    for kt in range(nt):
                        k_out(at, kt)
                    mT_out(at)
                    for m in range(U):
                        exps(at, m)
                    bias_v(at)
                    w_high(at)
                    hT_out(at)

                def iteration(on, first):
                    if first:
                        on(2, k_out, 0)
                    on(2, q_out, 0)
                    on(-1, bias_v)
                    on(0, exps, 0)
                    on(2, q_out, 1)
                    on(0, exps, 1)
                    if not first:
                        on(2, k_out, 0)
                    on(0, exps, 2)
                    on(-1, hT_out)
                    on(0, exps, 3)
                    on(1, mT_out)
                    on(0, w_high)

                drive(act, general, iteration)

            def vector_(dve):
                def kept(at):
                    return keep[:, bass.ds(at[0], 1), KT - nt:KT].rearrange("p a t -> p (a t)")

                def mask_rows(at):
                    n, i, u = at
                    wait(dve, T["k_ps"], nt * (n - depth + 1))
                    dve.tensor_scalar(mrow[:, u, :, :].rearrange("p n (g r) -> p n g r", g=G)[:, :, :, MASK_ROW],
                                      kept(at).unsqueeze(2).broadcast_to([P, nt, G]), 1.0, -MASKED, ALU.subtract,
                                      ALU.mult).then_inc(T["mrow"], 1)

                def ones_in(at):
                    n, i, u = at
                    wait(dve, T["pv"], U * (n - depth + 1))
                    settle(dve)
                    dve.tensor_copy(dn[:, u, :, :].rearrange("p n (j c) -> p n j c", j=BL)[:, :, :, 0:DH],
                                    kept(at).unsqueeze(2).unsqueeze(3).broadcast_to([P, nt, BL, DH])
                                    ).then_inc(T["dn"], 1)

                def q_split(at):
                    n, i, u = at
                    dve.wait_ge(T["q_hi"], n + 1)
                    wait(dve, T["s1"], U * (n - depth + 1))
                    if not (isinstance(n, int) and n < depth):
                        dve.wait_ge(q_bd[u], i * 64)
                    dve.scalar_tensor_tensor(out=qd[:, u, :, :], in0=q_hi[:, :, :], scalar=split_q[:, :],
                                             in1=q_t[:, :, :], op0=ALU.mult, op1=ALU.add).then_inc(T["q_spl"], 1)

                def k_split(at, kt):
                    n, i, u = at
                    m = n * nt + kt
                    dve.wait_ge(T["k_hi"], m + 1)
                    if nt == 1 and not (isinstance(n, int) and n == 0):
                        before_i = i if u == 0 else i + 1
                        dve.wait_ge(k_bd[1 - u], before_i * 64)
                        dve.wait_ge(k_cp[1 - u], before_i * 16)
                    elif nt > 1 and kt:
                        dve.wait_ge(k_bd[(kt - 1) % 2], k_uses(at, kt - 1) * 64)
                        dve.wait_ge(k_cp[0], m * 16)
                    elif nt > 1 and not (isinstance(n, int) and n == 0):
                        dve.wait_ge(k_bd[1], n * (nt // 2) * 64)
                        dve.wait_ge(k_cp[0], m * 16)
                    dve.scalar_tensor_tensor(out=k_new[:, :, :], in0=k_hi[:, :, :], scalar=split_k[:, :],
                                             in1=k_t[:, :, :], op0=ALU.mult, op1=ALU.add).then_inc(T["k_spl"], 1)

                def v_out(at, kt):
                    n, i, u = at
                    dve.wait_ge(T["v_ps"], n * nt + (kt + 1))
                    wait(dve, T["pv"], U * (n - depth + 1))
                    vv = vn[:, u, kt, :].rearrange("p (j c) -> p j c", j=BL)[:, :, 0:G * GR]
                    vv = vv.rearrange("p j (g c) -> p j g c", g=G)[:, :, :, 0:DH]
                    dve.tensor_scalar(vv, q_ps[:, 0:P].rearrange("p (j g d) -> p j g d", j=BL, g=G),
                                      kept(at)[:, kt:kt + 1], None, ALU.mult).then_inc(T["v_ev"], 1)

                def most(at, v):
                    n = at[0]
                    kt, j = v // BL, v % BL
                    dve.wait_ge(T["s1"], n * U + (v + 1))
                    if v == 0:
                        wait(dve, T["mlo"] if nt == 1 else T["mall"], n)
                    dve.tensor_reduce(mraw[:, kt, :, j * G:(j + 1) * G],
                                      s1_ps[:, :, :].rearrange("p a (g k) -> p a g k", g=G),
                                      AX.X, ALU.max).then_inc(T["mx"], 1)

                def most_all(at):
                    n = at[0]
                    dve.wait_ge(T["mx"], (n + 1) * U)
                    wait(dve, T["mlo"], n)
                    if nt == 1:
                        greatest = mraw[:, 0, :, :]
                    else:
                        greatest = mall
                        dve.tensor_reduce(mall[:, :, :], mraw[:, 0:nt, :, :].rearrange("p n a h -> p a h n"), AX.X,
                                          ALU.max).then_inc(T["mall"], 1)
                        dve.wait_ge(T["mall"], n + 1)
                    wait(dve, T["mm"], n)
                    dve.tensor_scalar(mhi[:, :, :], greatest[:, :, :], -1.0, None, ALU.mult).then_inc(T["mhi"], 1)
                    dve.wait_ge(T["mhi"], n + 1)
                    wait(dve, T["mT_ps"], n)
                    low = dve.scalar_tensor_tensor(out=mm[:, :, H:2 * H], in0=greatest[:, :, :], scalar=-1.0,
                                                   in1=mhi[:, :, :], op0=ALU.mult, op1=ALU.subtract)
                    low.then_inc(T["mlo"], 1)
                    dve.tensor_copy(mm[:, :, 0:H], mhi[:, :, :]).then_inc(T["mm"], 1)

                def divide(at):
                    n = at[0]
                    dve.wait_ge(T["pv"], (n + 1) * U)
                    wait(dve, T["oT"], n)
                    wait(dve, T["ot"], n)
                    dve.reciprocal(rden[:, :], pv_ps[:, SQ:2 * SQ]).then_inc(T["rden"], 1)
                    dve.wait_ge(T["rden"], n + 1)
                    dve.tensor_tensor(ot0[:, :], pv_ps[:, 0:SQ], rden[:, :], ALU.mult).then_inc(T["ot"], 1)

                def residual(at):
                    n = at[0]
                    dve.wait_ge(T["xb"], 1)
                    dve.wait_ge(T["y"], n + 1)
                    for t in range(QT):
                        k = n * QT + t
                        dve.scalar_tensor_tensor(out=xn[:, bass.ds(k, 1), :],
                                                 in0=pv_ps[:, t * P:(t + 1) * P].unsqueeze(1),
                                                 scalar=tg[:, 0:1], in1=x_sb[:, bass.ds(k, 1), :], op0=ALU.mult,
                                                 op1=ALU.add).then_inc(T["x2"], 1)

                def sent_before(at):
                    n, i, u = at
                    if not (isinstance(n, int) and n < depth):
                        dve.wait_ge(r_sent[u], i * QT * TOPK * 16)
                        settle(dve)

                def deviations(at):
                    n, i, u = at
                    dve.wait_ge(T["x2"], (n + 1) * QT)
                    for t in range(QT):
                        wait(dve, T["r_mv"], n * QT)
                        settle(dve)
                        dve.bn_stats(stats2[:, t, :],
                                     xn[:, bass.ds(n * QT + t, 1), :].rearrange("p a d -> p (a d)")
                                     ).then_inc(T["r_st"], 1)
                    for t in range(QT):
                        dve.wait_ge(T["r_st"], n * QT + (t + 1))
                        wait(dve, T["r_h"], n * QT)
                        settle(dve)
                        dve.bn_aggr(mv2[:, t, :], stats2[:, t, :]).then_inc(T["r_mv"], 1)
                    dve.wait_ge(T["r_mv"], (n + 1) * QT)
                    wait(dve, T["r_rs"], n)
                    dve.tensor_scalar(var2[:, :], mv2[:, :, 1], EPS, None, ALU.add).then_inc(T["r_var"], 1)

                def records(at):
                    n, i, u = at
                    dve.wait_ge(T["r_rs"], n + 1)
                    for t in range(QT):
                        dve.tensor_scalar(hrec[:, u, t, :, 0:D],
                                          xn[:, bass.ds(n * QT + t, 1), :].broadcast_to([P, TOPK, D]),
                                          mv2[:, t, 0:1], rstd2[:, t:t + 1], ALU.subtract,
                                          ALU.mult).then_inc(T["r_h"], 1)
                    wait(dve, T["r_dest"], n)
                    dve.tensor_copy(hrec[:, u, :, :, D:REC], dest[:, :, :].unsqueeze(3)).then_inc(T["r_hd"], 1)
                    dve.wait_ge(T["r_hd"], n + 1)
                    dve.tensor_scalar(dest[:, :, :], dest[:, :, :], float(SQ), None,
                                      ALU.add).then_inc(T["r_dest"], 1)

                def logits_out(at):
                    n, i, u = at
                    dve.wait_ge(T["r_lg_ps"], n + 1)
                    wait(dve, T["r_ti"], n * QT)
                    dve.tensor_scalar(logit[:, :, :], m_ps[:, SQ:SQ + QT * NE].rearrange("p (t e) -> p t e", t=QT),
                                      -BIG, BIG, ALU.max, ALU.min).then_inc(T["r_lg"], 1)

                def choices(at):
                    n, i, u = at
                    dve.wait_ge(T["r_lg"], n + 1)
                    wait(dve, T["r_gap"], n)
                    settle(dve)
                    for t in range(QT):
                        dve.max(top[:, t, :], logit[:, t, :]).then_inc(T["r_top"], 1)
                    for t in range(QT):
                        if t == 0:
                            wait(dve, T["r_tf"], n)
                        dve.wait_ge(T["r_top"], n * QT + (t + 1))
                        settle(dve)
                        dve.max_index(topi[:, t, :], top[:, t, :], logit[:, t, :]).then_inc(T["r_ti"], 1)
                    dve.tensor_tensor(gap[:, bass.ds(n * QT, QT)], top[:, :, 1], top[:, :, 0],
                                      ALU.subtract).then_inc(T["r_gap"], 1)
                    dve.wait_ge(T["r_ti"], (n + 1) * QT)
                    wait(dve, T["r_hot"], n)
                    dve.tensor_copy(topf[:, :, :], topi[:, :, 0:TOPK]).then_inc(T["r_tf"], 1)
                    dve.wait_ge(T["r_tf"], n + 1)
                    wait(dve, T["r_prod"], n)
                    wait(dve, T["r_sel"], n)
                    dve.tensor_tensor(hot[:, :, :, :],
                                      iota_e[:, :].unsqueeze(1).unsqueeze(1).broadcast_to([P, QT, TOPK, NE]),
                                      topf[:, :, :].unsqueeze(3).broadcast_to([P, QT, TOPK, NE]),
                                      ALU.is_equal).then_inc(T["r_hot"], 1)
                    dve.wait_ge(T["r_hot"], n + 1)
                    wait(dve, T["r_rk_ps"], n)
                    dve.tensor_tensor(selb[:, :, :], hot[:, :, 0, :], hot[:, :, 1, :],
                                      ALU.add).then_inc(T["r_sel"], 1)

                def ranks(at):
                    n, i, u = at
                    dve.wait_ge(T["r_rk_ps"], n + 1)
                    wait(dve, T["r_cnt"], n)
                    r0 = SQ + QT * NE
                    dve.tensor_tensor(pos[:, :, :], m_ps[:, r0:r0 + QT * NE].rearrange("p (t e) -> p t e", t=QT),
                                      cnt[:, :].unsqueeze(1).broadcast_to([P, QT, NE]),
                                      ALU.add).then_inc(T["r_pos"], 1)
                    dve.wait_ge(T["r_pos"], n + 1)
                    dve.tensor_tensor(cnt[:, :], cnt[:, :], m_ps[:, r0 + QT * NE:r0 + (QT + 1) * NE],
                                      ALU.add).then_inc(T["r_cnt"], 1)
                    wait(dve, T["r_row"], n)
                    dve.tensor_tensor(prod[:, :, :, :], hot[:, :, :, :],
                                      pos[:, :, :].unsqueeze(2).broadcast_to([P, QT, TOPK, NE]),
                                      ALU.mult).then_inc(T["r_prod"], 1)
                    dve.wait_ge(T["r_prod"], n + 1)
                    wait(dve, T["r_rowi"], n)
                    dve.tensor_reduce(rowf[:, :, :], prod[:, :, :, :], AX.X, ALU.add).then_inc(T["r_row"], 1)
                    dve.wait_ge(T["r_row"], n + 1)
                    dve.tensor_copy(rowi[:, u, :, :], rowf[:, :, :]).then_inc(T["r_rowi"], 1)

                def general(at):
                    mask_rows(at)
                    ones_in(at)
                    q_split(at)
                    for kt in range(nt):
                        k_split(at, kt)
                        v_out(at, kt)
                        for j in range(BL):
                            most(at, kt * BL + j)
                    most_all(at)
                    divide(at)
                    residual(at)
                    sent_before(at)
                    for part_ in (deviations, records, logits_out, choices, ranks):
                        part_(at)

                def iteration(on, first):
                    on(2, mask_rows)
                    if first:
                        on(2, k_split, 0)
                    on(1, ones_in)
                    on(1, most, 0)
                    on(-1, residual)
                    on(-1, deviations)
                    on(-1, records)
                    on(1, v_out, 0)
                    on(1, most, 1)
                    on(2, q_split)
                    on(1, most, 2)
                    if not first:
                        on(2, k_split, 0)
                    on(-1, logits_out)
                    on(1, most, 3)
                    on(1, most_all)
                    on(-1, choices)
                    on(0, sent_before)
                    on(0, divide)
                    on(-1, ranks)

                drive(dve, general, iteration)

            def tensor_(pe):
                def q_project(at, r):
                    n = at[0]
                    if r == 0:
                        wait(pe, T["v_ev"], n * nt if depth == 1 else n - 1)
                    wait(pe, T["q_ev"], n * BL + 2 * r)
                    for j in (2 * r, 2 * r + 1):
                        mmi = pe.matmul(q_ps[:, (j % 2) * SQ:(j % 2 + 1) * SQ], wq_sb[:, j, :],
                                        xnT[:, bass.ds(n * SQ, SQ)], start=True, stop=True)
                    mmi.then_inc(T["q_ps"], 1)

                def k_project(at, kt):
                    n, i, u = at
                    if kt == 0:
                        pe.wait_ge(ctx_s[u], (i + 1) * 16)
                        pe.wait_ge(T["mrow"], n + 1)
                    wait(pe, T["k_ev"], (n * nt + kt) * BL)
                    for j in range(BL):
                        o = k_ps[:, j * P:(j + 1) * P]
                        pe.matmul(o, wk_sb[:, j, :], ctx_in[:, u, kt * P:(kt + 1) * P], start=True, stop=False)
                        mmi = pe.matmul(o, mrow[:, u, kt, :], ident[:, :], start=False, stop=True)
                    mmi.then_inc(T["k_ps"], 1)

                def v_project(at, kt):
                    n, i, u = at
                    ahead = n + 1 if depth == 1 else min(n + 2, B) if isinstance(n, int) else n + 2
                    pe.wait_ge(T["q_ev"], ahead * BL)
                    wait(pe, T["v_ev"], n * nt + kt)
                    pe.matmul(q_ps[:, 0:P], ctx_in[:, u, kt * P:(kt + 1) * P], wv_sb[:, :], start=True,
                              stop=True).then_inc(T["v_ps"], 1)

                def by_query(at, v):
                    n, i, u = at
                    kt, j = v // BL, v % BL
                    if v == 0:
                        pe.wait_ge(T["q_spl"], n + 1)
                    if j == 0:
                        pe.wait_ge(k_bd[kbuf(u, kt)], k_uses(at, kt) * 64)
                    wait(pe, T["mx"], n * U + v)
                    for t in range(QT):
                        mmi = pe.matmul(s1_ps[:, t, :], qd[:, u, j, t * P:(t + 1) * P],
                                        kbd[:, kbuf(u, kt), j, :, :].rearrange("p g k -> p (g k)"), start=True,
                                        stop=True)
                    mmi.then_inc(T["s1"], 1)

                def turn_most(at):
                    n = at[0]
                    pe.wait_ge(T["mm"], n + 1)
                    pe.wait_ge(T["mlo"], n + 1)
                    wait(pe, T["r_lg"], n - 1 if depth == 2 else n)
                    if depth == 1:
                        wait(pe, T["r_cnt"], n)
                    for t in range(QT):
                        mmi = pe.transpose(m_ps[:, t * P:(t + 1) * P], mm[:, t, :], ident[:, :])
                    mmi.then_inc(T["mT_ps"], 1)

                def by_key(at, m):
                    n, i, u = at
                    kt, j = m // BL, m % BL
                    if m == 0:
                        pe.wait_ge(q_bd[u], (i + 1) * 64)
                        pe.wait_ge(k_cp[u], (i + 1) * nt * 16)
                        pe.wait_ge(T["mT"], n + 1)
                    wait(pe, T["ex"], n * U + m)
                    for a in range(2):
                        o = s2_ps[:, a * 512:(a + 1) * 512]
                        pe.matmul(o, kd[:, u, kt, j, :], qbd[:, u, j, 2 * a:2 * a + 2, :].rearrange("p g q -> p (g q)"),
                                  start=True, stop=False, skip_group_check=True)
                        for gr in (2 * a, 2 * a + 1):
                            mmi = pe.matmul(o[:, (gr % 2) * SQ:(gr % 2 + 1) * SQ], sel[:, j * G + gr, :],
                                            mT[:, :], start=False, stop=(gr % 2 == 1), skip_group_check=True)
                    mmi.then_inc(T["s2"], 1)

                def values(at, m):
                    n, i, u = at
                    kt, j = m // BL, m % BL
                    if m == 0:
                        pe.wait_ge(T["dn"], n + 1)
                        pe.wait_ge(T["v_ev"], (n + 1) * nt)
                        wait(pe, T["x2"], n * QT)
                    pe.wait_ge(T["ex"], n * U + (m + 1))
                    for gr in range(G):
                        o = slice(gr * GR, (gr + 1) * GR)
                        r = pt[:, m % 2, gr * SQ:(gr + 1) * SQ]
                        c = (j * G + gr) * GR
                        pe.matmul(pv_ps[o, 0:SQ], vn[:, u, kt, c:c + GR], r, start=(m == 0),
                                  stop=(m == U - 1), skip_group_check=True)
                        mmi = pe.matmul(pv_ps[o, SQ:2 * SQ], dn[:, u, kt, j * GR:(j + 1) * GR], r,
                                        start=False, stop=(m == U - 1), skip_group_check=True)
                    mmi.then_inc(T["pv"], 1)

                def project_out(at):
                    pe.wait_ge(T["oT"], at[0] + 1)
                    for t in range(QT):
                        mmi = pe.matmul(pv_ps[:, t * P:(t + 1) * P], oT[:, t * P:(t + 1) * P], wo_sb[:, :],
                                        start=True, stop=True)
                    mmi.then_inc(T["y"], 1)

                def turn_rows(at):
                    pe.wait_ge(T["r_h"], (at[0] + 1) * QT)
                    wait(pe, T["r_cnt"], at[0])
                    for t in range(QT):
                        mmi = pe.transpose(m_ps[:, t * P:(t + 1) * P], hrec[:, at[2], t, 0, 0:D], ident[:, :])
                    mmi.then_inc(T["r_hT_ps"], 1)

                def logits(at):
                    pe.wait_ge(T["r_hT"], at[0] + 1)
                    for t in range(QT):
                        mmi = pe.matmul(m_ps[:, SQ + t * NE:SQ + (t + 1) * NE], hT[:, t * P:(t + 1) * P],
                                        wr_sb[:, :], start=True, stop=True)
                    mmi.then_inc(T["r_lg_ps"], 1)

                def rank(at):
                    n = at[0]
                    pe.wait_ge(T["r_sel"], n + 1)
                    pe.wait_ge(T["r_lg"], n + 1)
                    if depth == 2:
                        pe.wait_ge(T["mT"], min(n + 3, B) if isinstance(n, int) else n + 3)
                    r0 = SQ + QT * NE
                    pe.matmul(m_ps[:, r0:r0 + QT * NE], before[:, :], selb[:, :, :].rearrange("p t e -> p (t e)"),
                              start=True, stop=False, skip_group_check=True)
                    for t in range(1, QT):
                        for s in range(t):
                            pe.matmul(m_ps[:, r0 + t * NE:r0 + (t + 1) * NE], ones[:, :], selb[:, s, :],
                                      start=False, stop=False, skip_group_check=True)
                    for t in range(QT):
                        mmi = pe.matmul(m_ps[:, r0 + QT * NE:r0 + (QT + 1) * NE], ones[:, :], selb[:, t, :],
                                        start=False, stop=(t == QT - 1), skip_group_check=True)
                    mmi.then_inc(T["r_rk_ps"], 1)

                def general(at):
                    q_project(at, 0)
                    q_project(at, 1)
                    for kt in range(nt):
                        k_project(at, kt)
                        v_project(at, kt)
                        for j in range(BL):
                            by_query(at, kt * BL + j)
                    turn_most(at)
                    for m in range(U):
                        by_key(at, m)
                        if m:
                            values(at, m - 1)
                    values(at, U - 1)
                    project_out(at)
                    turn_rows(at)
                    logits(at)
                    rank(at)

                def iteration(on, first):
                    if first:
                        on(2, k_project, 0)
                    on(2, q_project, 0)
                    on(-2, rank)
                    on(0, by_key, 0)
                    on(1, by_query, 0)
                    on(2, q_project, 1)
                    on(-1, project_out)
                    on(0, by_key, 1)
                    on(0, values, 0)
                    on(1, v_project, 0)
                    on(1, by_query, 1)
                    if not first:
                        on(2, k_project, 0)
                    on(0, by_key, 2)
                    on(0, values, 1)
                    on(1, by_query, 2)
                    on(-1, turn_rows)
                    on(0, by_key, 3)
                    on(-1, logits)
                    on(1, by_query, 3)
                    on(0, values, 2)
                    on(0, values, 3)
                    on(1, turn_most)

                drive(pe, general, iteration)

            return sync_, gpsimd_, scalar_, vector_, tensor_

        general = attention(KT, 1)
        short = attention(1, 2)

        def choose(eng, k):
            n = eng.value_load(early_n[0:1, 0:1], min_val=0, max_val=1)
            with eng.If(n == 0):
                short[k](eng)
            with eng.Else():
                general[k](eng)

        E = sems("e_", "warm lane lanei fill used usedi tilesi tiles ends past skip te ts tb t0 tab "
                 "az xT_ps x_hi x_lo gu silu acts aT_ps aT y_ps y di")
        with nc.Block() as block:
            @block.sync
            def _(sp):
                choose(sp, 0)

            @block.gpsimd
            def _(pool):
                choose(pool, 1)

            @block.scalar
            def _(act):
                choose(act, 2)

            @block.vector
            def _(dve):
                dve.scalar_tensor_tensor(out=x_sb[:, :, :], in0=bo_sb[:, :].unsqueeze(1).broadcast_to([P, TT, D]),
                                         scalar=tg[:, 0:1], in1=x_sb[:, :, :], op0=ALU.mult,
                                         op1=ALU.add).then_inc(T["xb"], 1)
                choose(dve, 3)
                dve.wait_ge(T["r_cnt"], B)
                dve.wait_ge(S["iota"], 2)
                dve.tensor_scalar(lane_e[:, :], cnt[:, :], part_i[:, :], None, ALU.add).then_inc(E["lane"], 1)
                dve.wait_ge(E["lane"], 1)
                dve.tensor_copy(lane_i[:, :], lane_e[:, :]).then_inc(E["lanei"], 1)
                dve.tensor_tensor(used[:, :], cnt[:, :], base_e[:, :], ALU.subtract).then_inc(E["used"], 1)
                dve.wait_ge(E["used"], 1)
                dve.tensor_copy(usedi[:, :], used[:, :]).then_inc(E["usedi"], 1)
                dve.wait_ge(E["usedi"], 1)
                dve.tensor_single_scalar(tilesi[:, :], usedi[:, :], 7, ALU.arith_shift_right).then_inc(E["tilesi"], 1)
                dve.wait_ge(E["tilesi"], 1)
                dve.tensor_copy(tiles[:, :], tilesi[:, :]).then_inc(E["tiles"], 1)
                dve.wait_ge(E["tiles"], 1)
                dve.scalar_tensor_tensor(out=ti[:, FT:NT], in0=tiles[:, :], scalar=float(P), in1=base_e[:, :],
                                         op0=ALU.mult, op1=ALU.add).then_inc(E["tab"], 1)
                dve.tensor_copy(tw[:, FT:NT], iota_e[:, :]).then_inc(E["tab"], 1)
                dve.tensor_tensor_scan(ends[:, :], tiles[:, :], tiles[:, :], 0.0, ALU.add,
                                       ALU.bypass).then_inc(E["ends"], 1)
                dve.wait_ge(E["ends"], 1)
                dve.tensor_tensor(past[:, :, :], tile_i[:, :].unsqueeze(2).broadcast_to([P, FT, NE]),
                                  ends[:, :].unsqueeze(1).broadcast_to([P, FT, NE]), ALU.is_ge).then_inc(E["past"], 1)
                dve.wait_ge(E["past"], 1)
                dve.tensor_tensor(skip[:, :, :], past[:, :, :],
                                  tiles[:, :].unsqueeze(1).broadcast_to([P, FT, NE]), ALU.mult).then_inc(E["skip"], 1)
                dve.tensor_reduce(te[:, :], past[:, :, :], AX.X, ALU.add).then_inc(E["te"], 1)
                dve.wait_ge(E["skip"], 1)
                dve.tensor_reduce(ts_[:, :], skip[:, :, :], AX.X, ALU.add).then_inc(E["ts"], 1)
                dve.wait_ge(E["ts"], 1)
                dve.wait_ge(E["te"], 1)
                dve.tensor_tensor(tb[:, :], tile_i[:, :], ts_[:, :], ALU.subtract).then_inc(E["tb"], 1)
                dve.tensor_scalar(t0[:, :], te[:, :], float(CAP), None, ALU.mult).then_inc(E["t0"], 1)
                dve.wait_ge(E["tb"], 1)
                dve.wait_ge(E["t0"], 1)
                dve.scalar_tensor_tensor(out=tb[:, :], in0=tb[:, :], scalar=float(P), in1=t0[:, :], op0=ALU.mult,
                                         op1=ALU.add).then_inc(E["tb"], 1)
                dve.wait_ge(E["tb"], 2)
                dve.tensor_scalar(ti[:, 0:FT], tb[:, :], float(BLANK), None, ALU.min).then_inc(E["tab"], 1)
                dve.tensor_scalar(tw[:, 0:FT], te[:, :], float(NE - 1), None, ALU.min).then_inc(E["tab"], 1)

            @block.tensor
            def _(pe):
                choose(pe, 4)

        attention_memory.close()
        warm = sb("warm", [P, 1])
        rec = sb("rec", [P, NB, REC])
        x_hi = sb("x_hi", [P, 2, P], F32R)
        x_lo = sb("x_lo", [P, 2, P], F32R)
        silu = sb("silu", [P, 2, F])
        acts = sb("acts", [P, 2, FP])
        actsT = sb("actsT", [P, 2, FP])
        yrow = sb("yrow", [P, NB, D])
        desti = sb("desti", [P, NB], U32)

        rec_s = [sem(f"e_rec{u}") for u in range(NB)]
        sent = [sem(f"e_sent{u}") for u in range(NB)]

        def steps(eng, step, last, rounds=NT // NB):
            for s in range(NB):
                step(s, 0, s)
            with eng.Fori(1, rounds) as i:
                for u in range(NB):
                    step(i * NB + u, i, u)
            for s in range(NT, NT + last):
                step(s, s // NB, s % NB)

        def tile_at(s, i, u, lag):
            if isinstance(s, int) and not 0 <= s - lag < NT:
                return None
            return s - lag, (i if u >= lag else i - 1), (u - lag) % NB

        xT_ps = q_ps
        aT_ps = m_ps
        y_ps = k_ps
        with nc.Block() as block:
            @block.sync
            def _(sp):
                sp.wait_ge(E["tab"], 4)

                def step(s, i, u):
                    if isinstance(s, int) and s == FT:
                        sp.wait_ge(E["fill"], NE * 16)
                    row = sp.value_load(ti[0:1, bass.ds(s, 1)], min_val=0, max_val=BLANK)
                    wait(sp, E["y"], s - NB + 1)
                    wait(sp, E["di"], s - NB + 1)
                    sp.dma_start(rec[:, u, :], lists[bass.ds(row, P), :]).then_inc(rec_s[u], 16)
                steps(sp, step, 0, NT // NB - 1)
                for u in range(NB):
                    step(FT + u, FT // NB, u)

            @block.gpsimd
            def _(pool):
                pool.wait_ge(E["lanei"], 1)
                for e in range(NE):
                    pool.indirect_dma_start(lists, bass.IndirectOffsetOnAxis(ap=lane_i[:, e:e + 1], axis=0),
                                            blank[:, :], None, bounds_check=BLANK - 1,
                                            oob_is_err=False).then_inc(E["fill"], 16)

                def step(s, i, u):
                    pool.wait_ge(E["y"], s + 1)
                    pool.wait_ge(E["di"], s + 1)
                    settle(pool)
                    pool.indirect_dma_start(places, bass.IndirectOffsetOnAxis(ap=desti[:, u:u + 1], axis=0),
                                            yrow[:, u, :], None, bounds_check=TOPK * NTOK - 1,
                                            oob_is_err=False).then_inc(sent[u], 16)
                steps(pool, step, 0)
                for u in range(NB):
                    pool.wait_ge(sent[u], NT // NB * 16)

            @block.scalar
            def _(act):
                act.activation(warm[:, :], halves[:, 0:1], ACT.Silu).then_inc(E["warm"], 1)

                def step(s, i, u):
                    if at := tile_at(s, i, u, 0):
                        n = at[0]
                        act.wait_ge(E["xT_ps"], n + 1)
                        wait(act, E["gu"], n - 1)
                        act.activation(x_hi[:, u % 2, :], xT_ps[:, 0:P], ACT.Copy).then_inc(E["x_hi"], 1)
                    if at := tile_at(s, i, u, 1):
                        n, _, v = at
                        act.wait_ge(E["gu"], n + 1)
                        wait(act, E["acts"], n - 1)
                        act.activation(silu[:, v % 2, :], s_ps[:, 2 * (v % 2), 0:F],
                                       ACT.Silu).then_inc(E["silu"], 1)
                    if at := tile_at(s, i, u, 2):
                        n, _, v = at
                        act.wait_ge(E["aT_ps"], n + 1)
                        wait(act, E["y_ps"], n - 1)
                        act.activation(actsT[:, v % 2, :], aT_ps[:, 0:FP], ACT.Copy).then_inc(E["aT"], 1)
                steps(act, step, 2)

            @block.vector
            def _(dve):
                dve.memset(acts[:, :, F:FP], 0.0).then_inc(E["az"], 1)
                dve.wait_ge(E["az"], 1)

                def step(s, i, u):
                    if at := tile_at(s, i, u, 0):
                        n = at[0]
                        wait(dve, sent[u], i * 16)
                        dve.wait_ge(E["x_hi"], n + 1)
                        wait(dve, E["gu"], n - 1)
                        dve.tensor_tensor(x_lo[:, u % 2, :], xT_ps[:, 0:P], x_hi[:, u % 2, :],
                                          ALU.subtract).then_inc(E["x_lo"], 1)
                    if at := tile_at(s, i, u, 1):
                        n, _, v = at
                        dve.wait_ge(E["silu"], n + 1)
                        wait(dve, E["aT_ps"], n - 1)
                        dve.tensor_tensor(acts[:, v % 2, 0:F], silu[:, v % 2, :], s_ps[:, 2 * (v % 2) + 1, 0:F],
                                          ALU.mult).then_inc(E["acts"], 1)
                    if at := tile_at(s, i, u, 3):
                        n, _, v = at
                        dve.wait_ge(E["y_ps"], n + 1)
                        dve.tensor_copy(desti[:, v:v + 1], rec[:, v, D:REC]).then_inc(E["di"], 1)
                        dve.tensor_copy(yrow[:, v, :], y_ps[:, 0:D]).then_inc(E["y"], 1)
                steps(dve, step, 3)

            @block.tensor
            def _(pe):
                experts = {}

                def look_up(s, u, t):
                    if not (isinstance(s, int) and not 0 <= s + t < NT):
                        experts[u + t] = pe.value_load(tw[0:1, bass.ds(s + t, 1)], min_val=0, max_val=NE - 1)

                def step(s, i, u):
                    if u == 0:
                        look_up(s, u, -1)
                    if at := tile_at(s, i, u, 0):
                        n, r, _ = at
                        pe.wait_ge(rec_s[u], (r + 1) * 16)
                        wait(pe, E["x_lo"], n)
                        pe.transpose(xT_ps[:, 0:P], rec[:, u, 0:D], ident[:, :]).then_inc(E["xT_ps"], 1)
                    if at := tile_at(s, i, u, 1):
                        n, _, v = at
                        e = experts[u - 1]
                        pe.wait_ge(E["x_lo"], n + 1)
                        wait(pe, E["acts"], n - 1)
                        for k, (xs, ws) in enumerate(((x_hi, w_hi), (x_hi, w_lo), (x_lo, w_hi))):
                            for a in range(2):
                                mmi = pe.matmul(s_ps[:, 2 * (v % 2) + a, 0:F], xs[:, v % 2, :],
                                                ws[:, bass.ds(e, 1), a * F:(a + 1) * F].rearrange("p a f -> p (a f)"),
                                                start=(k == 0), stop=(k == 2))
                        mmi.then_inc(E["gu"], 1)
                    if at := tile_at(s, i, u, 2):
                        n, _, v = at
                        pe.wait_ge(E["acts"], n + 1)
                        wait(pe, E["aT"], n)
                        for c in range(FC):
                            mmi = pe.transpose(aT_ps[:, c * P:(c + 1) * P], acts[:, v % 2, c * P:(c + 1) * P],
                                               ident[:, :])
                        mmi.then_inc(E["aT_ps"], 1)
                    if u < NB - 1:
                        look_up(s, u, 0)
                    if u < 2:
                        look_up(s, u, -3)
                    if at := tile_at(s, i, u, 3):
                        n, _, v = at
                        e = experts[u - 3]
                        pe.wait_ge(E["aT"], n + 1)
                        wait(pe, E["y"], n)
                        for c in range(FC):
                            mmi = pe.matmul(y_ps[:, 0:D], actsT[:, v % 2, c * P:(c + 1) * P],
                                            wd_sb[:, bass.ds(e, 1), c, :].rearrange("p a d -> p (a d)"),
                                            start=(c == 0), stop=(c == FC - 1))
                        mmi.then_inc(E["y_ps"], 1)

                pe.wait_ge(E["tab"], 4)
                pe.wait_ge(S["wd"], FC * 16)
                steps(pe, step, 3)

        C = sems("c_", "ed e1 w1 w2 wg1 wg2 s wy sum out")
        NCH = 4
        CT = TT // NCH
        got = [sem(f"c_got{c}") for c in range(NCH)]
        ed = sb("ed", [P, TT])
        e1 = sb("e1", [P, TT])
        w1 = sb("w1", [P, TT])
        w2 = sb("w2", [P, TT])
        wg = sb("wg", [P, TOPK, TT])
        wy = sb("wy", [P, TT, D])
        y0 = x_sb
        y1 = xnT[:, :].rearrange("p (t d) -> p t d", t=TT)
        with nc.Block() as block:
            @block.sync
            def _(sp):
                for c in range(NCH):
                    for k, dst in enumerate((y0, y1)):
                        r = k * NTOK + c * CT * P
                        sp.dma_start(dst[:, c * CT:(c + 1) * CT, :],
                                     places[r:r + CT * P, :].rearrange("(t p) d -> p t d", p=P)).then_inc(got[c], 16)
                for c in range(NCH):
                    sp.wait_ge(C["sum"], c + 1)
                    sp.dma_start(out[c * CT * P:(c + 1) * CT * P, :].rearrange("(t p) d -> p t d", p=P),
                                 xn[:, c * CT:(c + 1) * CT, :]).then_inc(C["out"], 16)
                sp.wait_ge(C["out"], NCH * 16)

            @block.scalar
            def _(act):
                act.activation(ed[:, :], gap[:, :], ACT.Exp).then_inc(C["ed"], 1)
                act.wait_ge(C["wg2"], 1)
                for c in range(NCH):
                    act.wait_ge(got[c], 32)
                    for t in range(c * CT, (c + 1) * CT):
                        act.activation(wy[:, t, :], y1[:, t, :], ACT.Copy, scale=wg[:, 1, t:t + 1]).then_inc(C["wy"], 1)

            @block.vector
            def _(dve):
                dve.wait_ge(C["ed"], 1)
                dve.tensor_scalar(e1[:, :], ed[:, :], 1.0, None, ALU.add).then_inc(C["e1"], 1)
                dve.wait_ge(C["e1"], 1)
                dve.reciprocal(w1[:, :], e1[:, :]).then_inc(C["w1"], 1)
                dve.wait_ge(C["w1"], 1)
                dve.tensor_tensor(w2[:, :], w1[:, :], ed[:, :], ALU.mult).then_inc(C["w2"], 1)
                dve.tensor_scalar(wg[:, 0, :], w1[:, :], tg[:, 1:2], None, ALU.mult).then_inc(C["wg1"], 1)
                dve.wait_ge(C["w2"], 1)
                dve.tensor_scalar(wg[:, 1, :], w2[:, :], tg[:, 1:2], None, ALU.mult).then_inc(C["wg2"], 1)
                dve.wait_ge(C["wg1"], 1)
                dve.wait_ge(C["wg2"], 1)
                for c in range(NCH):
                    dve.wait_ge(got[c], 32)
                    for t in range(c * CT, (c + 1) * CT):
                        dve.scalar_tensor_tensor(out=xn[:, t, :], in0=y0[:, t, :], scalar=wg[:, 0, t:t + 1],
                                                 in1=xn[:, t, :], op0=ALU.mult, op1=ALU.add).then_inc(C["s"], 1)
                    dve.wait_ge(C["s"], CT * (c + 1))
                    dve.wait_ge(C["wy"], CT * (c + 1))
                    dve.tensor_tensor(xn[:, c * CT:(c + 1) * CT, :], xn[:, c * CT:(c + 1) * CT, :],
                                      wy[:, c * CT:(c + 1) * CT, :], ALU.add).then_inc(C["sum"], 1)


def kernel(x, ctx_1024, mask_Bx1xS2_ik0, g_xattn, g_ffn, L0_xattn_Wq, L0_xattn_bq, L0_xattn_Wk, L0_xattn_bk,
           L0_xattn_Wv, L0_xattn_bv, L0_xattn_Wo, L0_xattn_bo, L0_ffn_router_w, L0_ffn_gate_proj,
           L0_ffn_up_proj, L0_ffn_down_proj):
    import numpy as np
    import concourse.bacc as bacc
    from concourse.bass_utils import run_bass_kernel_spmd

    def thrice(w):
        w = np.asarray(w).reshape(-1, BL, G, DH)
        o = np.zeros((w.shape[0], BL, G, GR), w.dtype)
        for c in range(3):
            o[..., c * DH:(c + 1) * DH] = w
        return o.reshape(w.shape[0], BL, P)

    def columns(b, one):
        o = thrice(b).reshape(BL, G, GR)
        o[..., MASK_ROW] = one
        return np.ascontiguousarray(o.reshape(BL, P).T)

    heads = (BL, G, DH)
    arrays = {
        "x": np.asarray(x).reshape(NTOK, D),
        "ctxT": np.ascontiguousarray(np.asarray(ctx_1024).transpose(0, 2, 1)).reshape(B * D, SK),
        "mask": np.ascontiguousarray(np.asarray(mask_Bx1xS2_ik0).reshape(B, KT, P).transpose(2, 0, 1)).reshape(P, B * KT),
        "wq": thrice(L0_xattn_Wq), "bq": columns(L0_xattn_bq, 1),
        "wk": thrice(L0_xattn_Wk), "bk": columns(L0_xattn_bk, 0),
        "wv": np.asarray(L0_xattn_Wv),
        "bv": np.ascontiguousarray(np.asarray(L0_xattn_bv).reshape(heads).transpose(1, 0, 2)).reshape(P, 1),
        "wo": np.ascontiguousarray(np.asarray(L0_xattn_Wo).reshape(*heads, D).transpose(1, 0, 2, 3)).reshape(P, D),
        "bo": np.asarray(L0_xattn_bo),
        "g": np.concatenate([np.asarray(g_xattn), np.asarray(g_ffn)]),
        "wr": np.asarray(L0_ffn_router_w),
        "wgate": np.asarray(L0_ffn_gate_proj), "wup": np.asarray(L0_ffn_up_proj),
        "wdown": np.asarray(L0_ffn_down_proj),
    }
    nc = bacc.Bacc("TRN2", target_bir_lowering=False, num_devices=1)
    aps = {k: nc.dram_tensor("in_" + k, a.shape, mybir.dt.from_np(a.dtype), kind="ExternalInput").ap()
           for k, a in arrays.items()}
    aps["out"] = nc.dram_tensor("out_x", (NTOK, D), F32, kind="ExternalOutput").ap()
    build(nc, **aps)
    r = run_bass_kernel_spmd(nc, [{"in_" + k: a for k, a in arrays.items()}], core_ids=[0])
    return r.results[0]["out_x"].reshape(B, SQ, D)
```
